# Optimizing a Trainium2 kernel written in Bass

```python
import numpy as np
import jax
import jax.numpy as jnp

def _softmax(x, axis=-1):
    return jax.nn.softmax(x, axis=axis)

def _gelu(x):
    return jax.nn.gelu(x, approximate=True)

def _silu(x):
    return jax.nn.silu(x)

def _sigmoid(x):
    return jax.nn.sigmoid(x)

def _layernorm(x, axis=-1, eps=1e-05):
    m = jnp.mean(x, axis=axis, keepdims=True)
    v = jnp.var(x, axis=axis, keepdims=True)
    return (x - m) / jnp.sqrt(v + eps)

def _scatter_add(tgt, idx, src, axis=0):
    return tgt.at[idx].add(src)

def _segment_sum(src, seg, n):
    return jax.ops.segment_sum(src, seg, n)
kernel_name = 'mk_vit_tower_cls_d1_tok_img768_r4_4e0fca'

def setup_inputs(seed: int=0):
    np.random.seed(seed)
    _w = jnp.asarray

    def _rec_inputs():
        import jax
        import jax.numpy as jnp
        _rk = jax.random.key(seed)
        x = -0.000356955 + 1 * jax.random.normal(jax.random.fold_in(_rk, 1), (64, 224, 224, 3), jnp.float32)
        cls_tok = 0.02 * jax.random.normal(jax.random.fold_in(_rk, 5), (1, 1, 192), jnp.float32)
        return (x, cls_tok)
    x, cls_tok = _rec_inputs()

    def _L0_tok_setup():
        import jax, jax.numpy as jnp
        import numpy as np
        PATCH = 16
        IMG = 224
        NP_SIDE = IMG // PATCH
        EMBED = 192

        def _patchify(batch_image):
            B = batch_image.shape[0]
            x = batch_image.reshape(B, NP_SIDE, PATCH, NP_SIDE, PATCH, 3)
            x = x.transpose(0, 1, 3, 5, 2, 4)
            return x.reshape(B, NP_SIDE * NP_SIDE, 3 * PATCH * PATCH)
        key = jax.random.key(seed)
        k1, k2, k3, k4, k5 = jax.random.split(key, 5)
        return {'batch_image': jax.random.normal(k1, (128, IMG, IMG, 3), dtype=jnp.float32), 'W': jax.random.normal(k2, (EMBED, 3 * PATCH * PATCH), dtype=jnp.float32) * 0.02, 'b': jax.random.normal(k3, (EMBED,), dtype=jnp.float32) * 0.02, 'cls_token': jax.random.normal(k4, (1, 1, EMBED), dtype=jnp.float32), 'pos_embed': jax.random.normal(k5, (1, NP_SIDE * NP_SIDE + 1, EMBED), dtype=jnp.float32)}
    _L0_tok_all = _L0_tok_setup()
    _L0_tok_in = {k: v for k, v in _L0_tok_all.items() if k in ('W', 'b', 'cls_token', 'pos_embed')}
    del _L0_tok_all

    def _L0_attn_setup():
        import jax, jax.numpy as jnp
        import numpy as np
        B, S, D, H = (8, 256, 192, 12)
        HS = D // H
        key = jax.random.key(seed)
        k1, k2, k3 = jax.random.split(key, 3)
        x = jax.random.normal(k1, (B, S, D), dtype=jnp.float32)
        W_attn = jax.random.normal(k2, (D, 3 * H * HS), dtype=jnp.float32) * 0.02
        b_attn = jnp.zeros((3 * H * HS,), dtype=jnp.float32)
        W_proj = jax.random.normal(k3, (H * HS, D), dtype=jnp.float32) * 0.02
        b_proj = jnp.zeros((D,), dtype=jnp.float32)
        return {'x': x, 'W_attn': W_attn, 'b_attn': b_attn, 'W_proj': W_proj, 'b_proj': b_proj}
    _L0_attn_all = _L0_attn_setup()
    _L0_attn_in = {k: v for k, v in _L0_attn_all.items() if k in ('W_attn', 'b_attn', 'W_proj', 'b_proj')}
    del _L0_attn_all

    def _L0_ffn_setup():
        import jax, jax.numpy as jnp
        import numpy as np
        EPS_NORM = 1e-06
        EPS_LN = 1e-05

        def _layernorm(x, g, b):
            mu = jnp.mean(x, axis=-1, keepdims=True)
            var = jnp.mean(jnp.square(x - mu), axis=-1, keepdims=True)
            return (x - mu) * jax.lax.rsqrt(var + EPS_LN) * g + b
        key = jax.random.key(seed)
        ks = jax.random.split(key, 6)
        b, m, d = (8, 256, 192)
        n, p = (64, 16)
        h = 2 * d
        x = jax.random.normal(ks[0], (b, m, d), dtype=jnp.float32)
        phi = jax.random.normal(ks[1], (n, p, d), dtype=jnp.float32)
        ln_g = jnp.ones((n, d), dtype=jnp.float32)
        ln_b = jnp.zeros((n, d), dtype=jnp.float32)
        w1 = jax.random.normal(ks[2], (n, d, h), dtype=jnp.float32) * (1.0 / np.sqrt(d))
        b1 = jax.random.normal(ks[3], (n, h), dtype=jnp.float32) * 0.01
        w2 = jax.random.normal(ks[4], (n, h, d), dtype=jnp.float32) * (1.0 / np.sqrt(h))
        b2 = jax.random.normal(ks[5], (n, d), dtype=jnp.float32) * 0.01
        return {'x': x, 'phi': phi, 'ln_g': ln_g, 'ln_b': ln_b, 'w1': w1, 'b1': b1, 'w2': w2, 'b2': b2}
    _L0_ffn_all = _L0_ffn_setup()
    _L0_ffn_in = {k: v for k, v in _L0_ffn_all.items() if k in ('phi', 'ln_g', 'ln_b', 'w1', 'b1', 'w2', 'b2')}
    del _L0_ffn_all
    return {'x': x, 'cls_tok': cls_tok, 'L0_tok_W': _L0_tok_in['W'], 'L0_tok_b': _L0_tok_in['b'], 'L0_tok_cls_token': _L0_tok_in['cls_token'], 'L0_tok_pos_embed': _L0_tok_in['pos_embed'], 'L0_attn_W_attn': _L0_attn_in['W_attn'], 'L0_attn_b_attn': _L0_attn_in['b_attn'], 'L0_attn_W_proj': _L0_attn_in['W_proj'], 'L0_attn_b_proj': _L0_attn_in['b_proj'], 'L0_ffn_phi': _L0_ffn_in['phi'], 'L0_ffn_ln_g': _L0_ffn_in['ln_g'], 'L0_ffn_ln_b': _L0_ffn_in['ln_b'], 'L0_ffn_w1': _L0_ffn_in['w1'], 'L0_ffn_b1': _L0_ffn_in['b1'], 'L0_ffn_w2': _L0_ffn_in['w2'], 'L0_ffn_b2': _L0_ffn_in['b2']}

def reference(x, cls_tok, L0_tok_W, L0_tok_b, L0_tok_cls_token, L0_tok_pos_embed, L0_attn_W_attn, L0_attn_b_attn, L0_attn_W_proj, L0_attn_b_proj, L0_ffn_phi, L0_ffn_ln_g, L0_ffn_ln_b, L0_ffn_w1, L0_ffn_b1, L0_ffn_w2, L0_ffn_b2):
    import jax
    import jax.numpy as jnp

    def _L0_tok_ref(batch_image, W, b, cls_token, pos_embed):
        import jax, jax.numpy as jnp
        import numpy as np
        PATCH = 16
        IMG = 224
        NP_SIDE = IMG // PATCH
        EMBED = 192

        def _patchify(batch_image):
            B = batch_image.shape[0]
            x = batch_image.reshape(B, NP_SIDE, PATCH, NP_SIDE, PATCH, 3)
            x = x.transpose(0, 1, 3, 5, 2, 4)
            return x.reshape(B, NP_SIDE * NP_SIDE, 3 * PATCH * PATCH)
        B = batch_image.shape[0]
        patches = _patchify(batch_image)
        Zp = jnp.einsum('bpd,ed->bpe', patches, W) + b
        Zcls = jnp.broadcast_to(cls_token, (B, 1, EMBED))
        Zcls_p = jnp.concatenate([Zcls, Zp], axis=1)
        return Zcls_p + pos_embed

    def _L0_attn_ref(x, W_attn, b_attn, W_proj, b_proj):
        import jax, jax.numpy as jnp
        import numpy as np
        B, S, D, H = (8, 256, 192, 12)
        HS = D // H
        b, s, d = x.shape
        qkv = (x @ W_attn + b_attn).reshape(b, s, 3, H, HS)
        q, k, v = (qkv[:, :, 0], qkv[:, :, 1], qkv[:, :, 2])
        scale = jnp.sqrt(jnp.asarray(HS, dtype=x.dtype))
        scores = jnp.einsum('bqhd,bkhd->bhqk', q, k) / scale
        causal = jnp.tril(jnp.ones((s, s), dtype=bool))
        scores = jnp.where(causal, scores, -jnp.inf)
        attn = jax.nn.softmax(scores, axis=-1)
        out = jnp.einsum('bhqk,bkhd->bqhd', attn, v).reshape(b, s, H * HS)
        return out @ W_proj + b_proj

    def _L0_ffn_ref(x, phi, ln_g, ln_b, w1, b1, w2, b2):
        import jax, jax.numpy as jnp
        import numpy as np
        EPS_NORM = 1e-06
        EPS_LN = 1e-05

        def _layernorm(x, g, b):
            mu = jnp.mean(x, axis=-1, keepdims=True)
            var = jnp.mean(jnp.square(x - mu), axis=-1, keepdims=True)
            return (x - mu) * jax.lax.rsqrt(var + EPS_LN) * g + b
        phi_n = phi * jax.lax.rsqrt(jnp.sum(jnp.square(phi), axis=0, keepdims=True) + EPS_NORM)
        bsz, m, d = x.shape
        n, p, _ = phi_n.shape
        logits = jnp.einsum('bmd,npd->bmnp', x, phi_n)
        D = jax.nn.softmax(logits, axis=1)
        C = jax.nn.softmax(logits.reshape(bsz, m, n * p), axis=-1)
        Xs = jnp.einsum('bmd,bmnp->bnpd', x, D)
        hdn = _layernorm(Xs, ln_g[:, None, :], ln_b[:, None, :])
        hdn = jnp.einsum('bnpd,ndh->bnph', hdn, w1) + b1[:, None, :]
        hdn = jax.nn.gelu(hdn, approximate=False)
        Ys = jnp.einsum('bnph,nhd->bnpd', hdn, w2) + b2[:, None, :]
        Ys = Ys.reshape(bsz, n * p, d)
        Y = jnp.einsum('bsd,bms->bmd', Ys, C)
        return Y
    h = _L0_tok_ref(x, L0_tok_W, L0_tok_b, L0_tok_cls_token, L0_tok_pos_embed)
    h = jnp.concatenate([jnp.broadcast_to(cls_tok, (h.shape[0], 1, h.shape[2])), h], axis=1)
    h = h + _L0_attn_ref(_layernorm(h, axis=-1), L0_attn_W_attn, L0_attn_b_attn, L0_attn_W_proj, L0_attn_b_proj)
    h = h + _L0_ffn_ref(_layernorm(h, axis=-1), L0_ffn_phi, L0_ffn_ln_g, L0_ffn_ln_b, L0_ffn_w1, L0_ffn_b1, L0_ffn_w2, L0_ffn_b2)
    return h

_drawn_inputs = setup_inputs


def setup_inputs(seed=0):
    import zlib

    import numpy as np

    out = dict(_drawn_inputs(seed))
    spreads = {'L0_attn_b_attn': (0.0, 0.295),
     'L0_attn_b_proj': (0.0, 0.1),
     'L0_ffn_ln_g': (1.0, 0.6),
     'L0_ffn_ln_b': (0.0, 0.8)}
    factors = {'cls_tok': 8.0,
     'L0_tok_b': 3.018,
     'L0_attn_W_attn': 4.989,
     'L0_ffn_b1': 61.06,
     'L0_ffn_b2': 39.116}
    for name, (base, spread) in spreads.items():
        noise = np.random.default_rng([zlib.crc32(name.encode()), seed]).standard_normal(out[name].shape)
        drawn = base * np.exp(spread * noise) if base else spread * noise
        out[name] = jnp.asarray(drawn.astype(out[name].dtype))
    for name, factor in factors.items():
        out[name] = (out[name] * factor).astype(out[name].dtype)
    return out
```

```python
from contextlib import ExitStack

import concourse.bass as bass
from concourse import mybir

F32 = mybir.dt.float32
ALU = mybir.AluOpType
ACT = mybir.ActivationFunctionType
AX = mybir.AxisListType


def vit_tower(
    nc: bass.Bass,
    x: bass.AP,
    cls_tok: bass.AP,
    W: bass.AP,
    b: bass.AP,
    cls_token: bass.AP,
    pos_embed: bass.AP,
    W_attn: bass.AP,
    b_attn: bass.AP,
    W_proj: bass.AP,
    b_proj: bass.AP,
    phi: bass.AP,
    ln_g: bass.AP,
    ln_b: bass.AP,
    w1: bass.AP,
    b1: bass.AP,
    w2: bass.AP,
    b2: bass.AP,
    out: bass.AP,
):
    B, IMG, _, CH = x.shape
    EMB, PD = W.shape
    PATCH = 16
    SIDE = IMG // PATCH
    NPATCH = SIDE * SIDE
    TOK = NPATCH + 2
    TT = TOK // 2
    HP = NPATCH // 2
    HI = SIDE // 2
    PX = PATCH * CH
    HEADS = 12
    HS = EMB // HEADS
    HG = 4
    GROUPS = HEADS // HG
    FC = 96
    NX, NPX, _ = phi.shape
    SLOTS = NX * NPX
    SJ = SLOTS // 128
    HID = w1.shape[2]
    HC = HID // 128
    ROWS = B * NPX
    RJ = ROWS // 128
    KC = PD // 128
    CAUS = 3 * TT
    SCALE = float(HS) ** -0.5
    NEG = -1.0e30
    EPS = 1e-5
    EPS_NORM = 1e-6
    assert TOK == 2 * TT and EMB == 2 * FC and SJ * 16 == 128 and RJ == 8 and B % 2 == 0 and NX % 2 == 0

    ctx = ExitStack()
    with ctx:
        def sb(name, shape):
            return ctx.enter_context(nc.sbuf_tensor(name, shape, F32))

        def sem(name):
            return ctx.enter_context(nc.semaphore(name))

        def wait_past(eng, signal, value):
            if not (isinstance(value, int) and value <= 0):
                eng.wait_ge(signal, value)

        ctx.enter_context(nc.allow_non_contiguous_dma(reason="small biases, transposed once"))

        xs_d = nc.dram_tensor("xs_scratch", (NX, B, NPX, EMB), F32, kind="Internal").ap()
        ys_d = nc.dram_tensor("ys_scratch", (NX, B, NPX, EMB), F32, kind="Internal").ap()
        ct_d = nc.dram_tensor("combine_scratch", (B, 128, SJ * TOK), F32, kind="Internal").ap()
        h2_d = nc.dram_tensor("residual_scratch", (B, TT, 2 * EMB), F32, kind="Internal").ap()

        ps = ctx.enter_context(nc.psum_tensor("ps", [128, 8, 512], F32))

        ident = sb("ident", [128, 128])
        ones = sb("ones", [TT, 128])
        mask = sb("mask", [TT, CAUS])
        WT = sb("WT", [128, KC, EMB])
        wqk = sb("wqk", [FC, 2, 2, GROUPS, HG, 32])
        watt = sb("watt", [FC, 2, 3 * EMB])
        wproj = sb("wproj", [FC, 2, EMB])
        bqk = sb("bqk", [128, 2, GROUPS])
        bv = sb("bv", [TT, EMB])
        bproj = sb("bproj", [TT, EMB])
        posb = sb("posb", [TT, 2, EMB])
        phiT = sb("phiT", [FC, 2, SJ, 128])
        minus_half = sb("minus_half", [128, RJ])
        eps_ln = sb("eps_ln", [128, RJ])
        spare = sb("spare", [128, 1])
        gT = sb("gT", [FC, 2, NX])
        bT = sb("bT", [FC, 2, NX])
        b1T = sb("b1T", [128, HC, NX])

        xin = sb("xin", [HP, 2, PD])
        xT = sb("xT", [128, KC, TOK])
        h = sb("h", [TT, 2, EMB])
        hb = sb("hb", [TT, 2, EMB])
        st1 = sb("st1", [TT, 2, 6])
        mv1 = sb("mv1", [TT, 2, 2])
        ve1 = sb("ve1", [TT, 2])
        rs1 = sb("rs1", [TT, 2])
        xn1 = sb("xn1", [TT, 2, EMB])
        xn1T = sb("xn1T", [FC, 2, TOK])
        qkT = sb("qkT", [128, 2, GROUPS, TOK])
        vaug = sb("vaug", [TT, 2, HEADS, HS + 1])
        S = sb("S", [TT, HEADS, CAUS])
        mx = sb("mx", [TT, 2, HEADS])
        PT = sb("PT", [TT, HEADS, CAUS])
        rden = sb("rden", [TT, 2, HEADS])
        on = sb("on", [TT, 2, EMB])
        onT = sb("onT", [FC, 2, TOK])
        h2 = sb("h2", [TT, 2, EMB])
        st2 = sb("st2", [TT, 2, 6])
        mv2 = sb("mv2", [TT, 2, 2])
        ve2 = sb("ve2", [TT, 2])
        rs2 = sb("rs2", [TT, 2])
        xn2 = sb("xn2", [TT, 2, EMB + 1])
        xn2T = sb("xn2T", [FC, 2, TOK])
        LT = sb("LT", [128, SJ, TOK])
        slot_max = sb("slot_max", [128, SJ])
        tok_part = sb("tok_part", [128, TOK])
        tok_max = sb("tok_max", [TT, 2])
        tok_diag = sb("tok_diag", [TT, 2, TT])
        Td = sb("Td", [128, SJ, TOK])
        CT = sb("CT", [128, SJ, TOK])
        E = sb("E", [TT, 2, SLOTS])
        rz = sb("rz", [128, SJ])
        xs = sb("xs", [128, SJ, EMB])

        DMA_LOADS = sem("setup_loaded")

        wraw = S[0:FC, :, :].rearrange("p a c -> p (a c)")[:, 0:2 * PD].rearrange("p (h f) -> p h f", h=2)
        wre = PT[0:FC, :, :].rearrange("p a c -> p (a c)")[:, 0:2 * PD].rearrange("p (h f) -> p h f", h=2)
        phin = LT[:, :, :].rearrange("p a c -> p (a c)")[:, 0:SJ * EMB].rearrange("p (j d) -> p j d", j=SJ)
        phisq = Td[:, :, :].rearrange("p a c -> p (a c)")[:, 0:SJ * EMB].rearrange("p (j d) -> p j d", j=SJ)
        phirs = CT[:, :, :].rearrange("p a c -> p (a c)")[:, 0:SJ * EMB].rearrange("p (j d) -> p j d", j=SJ)
        phihalf = xs[:, :, :]
        parity2 = rz[:, 0:2]
        parity = tok_part[:, 0:128]
        posadd = xn1[:, :, :]
        graw = E[0:NX, 0, 0:EMB]
        braw = E[0:NX, 0, EMB:2 * EMB]
        b1raw = E[0:NX, 1, 0:HID]

        s_memset = sem("setup_memset")
        s_ident = sem("setup_ident")
        s_maskset = sem("setup_maskset")
        s_reorder = sem("setup_reorder")
        s_phisq = sem("setup_phisq")
        s_par2 = sem("setup_parity2")
        s_par = sem("setup_parity")
        s_phisum = sem("setup_phisum")
        s_phieps = sem("setup_phieps")
        s_phipow = sem("setup_phipow")
        s_newton = sem("setup_newton")
        s_phin = sem("setup_phin")
        s_sT = sem("setup_transposed")
        s_sE = sem("setup_evacuated")
        s_posb = sem("setup_posb")
        N_LOADS = 0
        with nc.Block() as blk:
            loads = [
                (wraw, W.rearrange("(h p) f -> p h f", p=FC)),
                (watt[:, :, :], W_attn.rearrange("(h p) f -> p h f", p=FC)),
                (wproj[:, :, :], W_proj.rearrange("(h p) f -> p h f", p=FC)),
                (phin, phi.rearrange("n p d -> (n p) d").rearrange("(q j) d -> q j d", j=SJ)),
                (graw, ln_g), (braw, ln_b), (b1raw, b1),
                (bv[:, :], b_attn[2 * EMB:3 * EMB].partition_broadcast(TT)),
                (bproj[:, :], b_proj.partition_broadcast(TT)),
                (posb[1:TT, 0, :], pos_embed[0, 0:TT - 1, :]),
                (posb[:, 1, :], pos_embed[0, TT - 1:TOK - 1, :]),
                (posadd[0:1, 0, :], cls_tok[0]),
                (posadd[1:2, 0, :], cls_token[0]),
                (posadd[2:TT, 0, :], b.partition_broadcast(TT - 2)),
                (posadd[:, 1, :], b.partition_broadcast(TT)),
            ]
            for g in range(HG):
                for qk in range(2):
                    src = b_attn[qk * EMB:(qk + 1) * EMB].rearrange("(j g r) -> g r j", g=HG, r=HS)[g]
                    loads.append((bqk[32 * g:32 * g + HS, qk, :], src))
            N_LOADS = len(loads)

            @blk.sync
            def _(sp):
                sp.wait_ge(s_memset, 2)
                for dst, src in loads:
                    sp.dma_start(dst, src).then_inc(DMA_LOADS, 16)

            @blk.gpsimd
            def _(pool):
                pool.memset(posb[:, :, :], 0.0).then_inc(s_memset, 1)
                pool.memset(bqk[:, :, :], 0.0).then_inc(s_memset, 1)
                pool.memset(ident[:, :], 0.0).then_inc(s_memset, 1)
                pool.wait_ge(s_memset, 3)
                pool.affine_select(out=ident[:, :], in_=ident[:, :], compare_op=ALU.not_equal, fill=1.0,
                                   base=0, pattern=[[-1, 128]], channel_multiplier=1).then_inc(s_ident, 1)
                pool.memset(ones[:, :], 1.0).then_inc(s_memset, 1)
                pool.memset(minus_half[:, :], -0.5).then_inc(s_memset, 1)
                pool.memset(eps_ln[:, :], EPS).then_inc(s_memset, 1)
                pool.memset(mask[:, :], 0.0).then_inc(s_memset, 1)
                pool.wait_ge(s_memset, 7)
                for c in (0, 2):
                    m = mask[:, c * TT:(c + 1) * TT]
                    pool.affine_select(out=m, in_=m, compare_op=ALU.is_ge, fill=NEG, base=0,
                                       pattern=[[-1, TT]], channel_multiplier=1).then_inc(s_maskset, 1)

            @blk.vector
            def _(dve):
                dve.memset(wqk[:, :, :, :, :, :], 0.0).then_inc(s_reorder, 1)
                for k in range(KC):
                    dve.memset(xT[:, k, 0:2], 0.0)
                dve.memset(vaug[:, :, :, :], 1.0)
                dve.memset(xn2[:, :, :], 1.0)
                dve.wait_ge(s_ident, 1)
                dve.tensor_reduce(parity2, ident[:, :].rearrange("p (a c) -> p c a", c=2), AX.X,
                                  ALU.add).then_inc(s_par2, 1)
                dve.wait_ge(s_par2, 1)
                dve.tensor_copy(parity.rearrange("p (a c) -> p a c", c=2),
                                parity2.unsqueeze(1).broadcast_to([128, 64, 2])).then_inc(s_par, 1)
                dve.wait_ge(DMA_LOADS, 16 * N_LOADS)
                for hh in range(2):
                    dve.tensor_copy(wre[:, hh, :].rearrange("p (a b c) -> p a b c", a=PATCH, b=PATCH),
                                    wraw[:, hh, :].rearrange("p (c a b) -> p a b c", a=PATCH, b=PATCH)
                                    ).then_inc(s_reorder, 1)
                dve.wait_ge(s_reorder, 1)
                for hh in range(2):
                    for qk in range(2):
                        dve.tensor_copy(wqk[:, hh, qk, :, :, 0:HS],
                                        watt[:, hh, qk * EMB:(qk + 1) * EMB].rearrange(
                                            "p (j g r) -> p j g r", j=GROUPS, g=HG)).then_inc(s_reorder, 1)
                dve.tensor_tensor(posb[:, :, :], posb[:, :, :], posadd, ALU.add).then_inc(s_posb, 1)
                dve.tensor_tensor(phisq, phin, phin, ALU.mult).then_inc(s_phisq, 1)
                dve.wait_ge(s_phisum, 1)
                dve.tensor_scalar(phirs, ps[:, 0:4, 0:2 * EMB].rearrange("p k (j d) -> p k j d", j=2),
                                  EPS_NORM, None, ALU.add).then_inc(s_phieps, 1)
                dve.wait_ge(s_phipow, 1)
                dve.reciprocal(phihalf, phihalf).then_inc(s_newton, 1)
                dve.wait_ge(s_newton, 1)
                dve.tensor_tensor(phisq, phihalf, phihalf, ALU.mult).then_inc(s_newton, 1)
                dve.wait_ge(s_newton, 2)
                dve.scalar_tensor_tensor(out=phisq, in0=phisq, scalar=-0.5, in1=phirs, op0=ALU.mult,
                                         op1=ALU.mult).then_inc(s_newton, 1)
                dve.wait_ge(s_newton, 3)
                dve.scalar_tensor_tensor(out=phihalf, in0=phisq, scalar=1.5, in1=phihalf, op0=ALU.add,
                                         op1=ALU.mult).then_inc(s_newton, 1)
                dve.wait_ge(s_newton, 4)
                dve.tensor_tensor(phin, phin, phihalf, ALU.mult).then_inc(s_phin, 1)
                dve.wait_ge(s_sT, 1)
                dve.tensor_copy(WT[:, :, :], ps[:, 4:7, 0:2 * EMB].rearrange("p k (c e) -> p k c e", c=2)
                                ).then_inc(s_sE, 1)
                dve.wait_ge(s_sT, 2)
                dve.tensor_copy(gT[:, :, :], ps[0:FC, 7, 0:2 * NX].rearrange("p (c n) -> p c n", c=2))
                dve.tensor_copy(bT[:, :, :], ps[0:FC, 7, 2 * NX:4 * NX].rearrange("p (c n) -> p c n", c=2))
                dve.tensor_copy(b1T[:, :, :], ps[:, 7, 4 * NX:7 * NX].rearrange("p (c n) -> p c n", c=HC)
                                ).then_inc(s_sE, 1)
                dve.wait_ge(s_sT, 3)
                dve.tensor_copy(phiT[:, :, :, :], ps[0:FC, 0:4, :].rearrange("p k n -> p (k n)")
                                ).then_inc(s_sE, 1)

            @blk.scalar
            def _(act):
                act.wait_ge(s_phieps, 1)
                act.activation(phihalf, phirs, ACT.Sqrt).then_inc(s_phipow, 1)

            @blk.tensor
            def _(pe):
                pe.wait_ge(DMA_LOADS, 16 * N_LOADS)
                pe.wait_ge(s_ident, 1)
                pe.wait_ge(s_reorder, 3)
                for k in range(KC):
                    for hh in range(2):
                        mm = pe.transpose(ps[:, 4 + k // 2, (k % 2) * EMB + hh * FC:(k % 2) * EMB + (hh + 1) * FC],
                                          wre[:, hh, k * 128:(k + 1) * 128], ident[0:FC, 0:FC])
                mm.then_inc(s_sT, 1)
                for n, (src, parts, width) in enumerate(
                        [(graw[:, 0:FC], FC, 0), (graw[:, FC:], FC, 0), (braw[:, 0:FC], FC, 0), (braw[:, FC:], FC, 0)]
                        + [(b1raw[:, c * 128:(c + 1) * 128], 128, 0) for c in range(HC)]):
                    mm = pe.transpose(ps[0:parts, 7, n * NX:(n + 1) * NX], src, ident[0:NX, 0:NX])
                mm.then_inc(s_sT, 1)
                pe.wait_ge(s_par, 1)
                pe.wait_ge(s_phisq, 1)
                for k in range(4):
                    mm = pe.matmul(ps[:, k, 0:2 * EMB], parity, phisq[:, 2 * k:2 * k + 2, :],
                                   start=True, stop=True)
                mm.then_inc(s_phisum, 1)
                pe.wait_ge(s_phin, 1)
                pe.wait_ge(s_phieps, 1)
                for hh in range(2):
                    for j in range(SJ):
                        k = hh * SJ + j
                        mm = pe.transpose(ps[0:FC, k // 4, (k % 4) * 128:(k % 4 + 1) * 128],
                                          phin[:, j, hh * FC:(hh + 1) * FC], ident[:, :])
                mm.then_inc(s_sT, 1)

        x_loaded = sem("x_loaded")
        xT_ready = sem("xT_ready")
        xT_copied = sem("xT_copied")
        Z_ready = sem("Z_ready")
        h_ready = sem("h_ready")
        hb_ready = sem("hb_ready")
        st1_ready = sem("st1_ready")
        mv1_ready = sem("mv1_ready")
        ve1_ready = sem("ve1_ready")
        rs1_ready = sem("rs1_ready")
        xn1_ready = sem("xn1_ready")
        xn1T_ready = sem("xn1T_ready")
        xn1T_copied = sem("xn1T_copied")
        qk_ready = sem("qk_ready")
        qk_copied = sem("qk_copied")
        v_ready = sem("v_ready")
        v_copied = sem("v_copied")
        S_ready = sem("S_ready")
        S_masked = sem("S_masked")
        mx_ready = sem("mx_ready")
        S_shifted = sem("S_shifted")
        P_ready = sem("P_ready")
        PT_ready = sem("PT_ready")
        PT_copied = sem("PT_copied")
        O_ready = sem("O_ready")
        rden_ready = sem("rden_ready")
        on_ready = sem("on_ready")
        onT_ready = sem("onT_ready")
        onT_copied = sem("onT_copied")
        proj_ready = sem("proj_ready")
        h2_ready = sem("h2_ready")
        h2_stored = sem("h2_stored")
        st2_ready = sem("st2_ready")
        mv2_ready = sem("mv2_ready")
        ve2_ready = sem("ve2_ready")
        rs2_ready = sem("rs2_ready")
        xn2_ready = sem("xn2_ready")
        xn2T_ready = sem("xn2T_ready")
        xn2T_copied = sem("xn2T_copied")
        LT_ready = sem("LT_ready")
        LT_copied = sem("LT_copied")
        smax_ready = sem("smax_ready")
        tpart_ready = sem("tpart_ready")
        tpartT_ready = sem("tpartT_ready")
        tmax_ready = sem("tmax_ready")
        tdiag_ready = sem("tdiag_ready")
        tbc_ready = sem("tbc_ready")
        U_ready = sem("U_ready")
        CT_ready = sem("CT_ready")
        CT_stored = sem("CT_stored")
        Td_ready = sem("Td_ready")
        TdT_ready = sem("TdT_ready")
        E_ready = sem("E_ready")
        Xs_ready = sem("Xs_ready")
        rz_ready = sem("rz_ready")
        xs_ready = sem("xs_ready")
        xs_stored = sem("xs_stored")

        def seg(bank, width=TOK):
            return ps[:, bank, 0:2 * width].rearrange("p (c t) -> p c t", c=2)

        class pe_att:
            @staticmethod
            def patches(pe, i):
                pe.wait_ge(x_loaded, (i + 1) * (16 * SIDE))
                wait_past(pe, xn2T_copied, i)
                for k in range(KC):
                    for t in range(2):
                        mm = pe.transpose(ps[:, k // 2, (k % 2) * NPATCH + t * HP:(k % 2) * NPATCH + (t + 1) * HP],
                                          xin[:, t, k * 128:(k + 1) * 128], ident[0:HP, 0:HP])
                mm.then_inc(xT_ready, 1)

            @staticmethod
            def embed(pe, i):
                pe.wait_ge(xT_copied, i + 1)
                for t in range(2):
                    for k in range(KC):
                        mm = pe.matmul(ps[0:TT, 3, t * EMB:(t + 1) * EMB], xT[:, k, t * TT:(t + 1) * TT],
                                       WT[:, k, :], start=(k == 0), stop=(k == KC - 1))
                mm.then_inc(Z_ready, 1)

            @staticmethod
            def turn(pe, i, src, bank, ready, done):
                pe.wait_ge(ready, i + 1)
                for t in range(2):
                    for c in range(2):
                        mm = pe.transpose(ps[0:FC, bank, c * TOK + t * TT:c * TOK + (t + 1) * TT],
                                          src[:, t, c * FC:(c + 1) * FC], ident[0:TT, 0:TT])
                mm.then_inc(done, 1)

            @staticmethod
            def qkv(pe, i):
                pe.wait_ge(xn1T_copied, i + 1)
                for n in range(2 * GROUPS):
                    for c in range(2):
                        mm = pe.matmul(ps[:, 1 + n // 2, (n % 2) * TOK:(n % 2 + 1) * TOK],
                                       wqk[:, c, n // GROUPS, n % GROUPS, :, :], xn1T[:, c, :],
                                       start=(c == 0), stop=(c == 1))
                mm.then_inc(qk_ready, 1)
                for t in range(2):
                    for c in range(2):
                        mm = pe.matmul(ps[0:TT, 0, t * EMB:(t + 1) * EMB], xn1T[:, c, t * TT:(t + 1) * TT],
                                       watt[:, c, 2 * EMB:3 * EMB], start=(c == 0), stop=(c == 1))
                mm.then_inc(v_ready, 1)

            @staticmethod
            def scores(pe, i, j):
                if j == 0:
                    pe.wait_ge(qk_copied, i + 1)
                    pe.wait_ge(v_copied, i + 1)
                else:
                    pe.wait_ge(S_masked, i * GROUPS + j)
                for t in range(2):
                    for g in range(HG):
                        q = qkT[32 * g:32 * g + HS, 0, j, t * TT:(t + 1) * TT]
                        kk = qkT[32 * g:32 * g + HS, 1, j, 0:(t + 1) * TT]
                        mm = pe.matmul(ps[0:TT, g, t * TT:t * TT + (t + 1) * TT], q, kk, start=True, stop=True)
                mm.then_inc(S_ready, 1)

            @staticmethod
            def probs_turn(pe, i, j):
                pe.wait_ge(P_ready, i * GROUPS + j + 1)
                if j == 0:
                    pe.wait_ge(S_masked, (i + 1) * GROUPS)
                else:
                    pe.wait_ge(PT_copied, i * GROUPS + j)
                for g in range(HG):
                    for c in range(3):
                        mm = pe.transpose(ps[0:TT, g, c * TT:(c + 1) * TT],
                                          S[:, HG * j + g, c * TT:(c + 1) * TT], ident[0:TT, 0:TT])
                mm.then_inc(PT_ready, 1)

            @staticmethod
            def weigh(pe, i):
                pe.wait_ge(PT_copied, (i + 1) * GROUPS)
                W1 = HS + 1
                for n in range(HEADS):
                    o0 = ps[0:TT, 0, n * W1:(n + 1) * W1]
                    o1 = ps[0:TT, 0, (HEADS + n) * W1:(HEADS + n + 1) * W1]
                    pe.matmul(o0, PT[:, n, 0:TT], vaug[:, 0, n, :], start=True, stop=True)
                    pe.matmul(o1, PT[:, n, TT:2 * TT], vaug[:, 0, n, :], start=True, stop=False)
                    mm = pe.matmul(o1, PT[:, n, 2 * TT:3 * TT], vaug[:, 1, n, :], start=False, stop=True)
                mm.then_inc(O_ready, 1)

            @staticmethod
            def proj(pe, i):
                pe.wait_ge(onT_copied, i + 1)
                for t in range(2):
                    for c in range(2):
                        mm = pe.matmul(ps[0:TT, 2, t * EMB:(t + 1) * EMB], onT[:, c, t * TT:(t + 1) * TT],
                                       wproj[:, c, :], start=(c == 0), stop=(c == 1))
                mm.then_inc(proj_ready, 1)

        class act_att:
            @staticmethod
            def patches(act, i):
                act.wait_ge(xT_ready, i + 1)
                wait_past(act, Z_ready, i)
                for k in range(3):
                    cp = act.activation(xT[:, 2 * k:2 * k + 2, 2:TOK], seg(k, NPATCH), ACT.Copy)
                cp.then_inc(xT_copied, 1)

            @staticmethod
            def turn(act, i, dst, bank, ready, done, free=None):
                act.wait_ge(ready, i + 1)
                if free is not None:
                    wait_past(act, free, i)
                act.activation(dst[:, :, :], ps[0:FC, bank, 0:2 * TOK].rearrange("p (c t) -> p c t", c=2),
                               ACT.Copy).then_inc(done, 1)

            @staticmethod
            def qk(act, i):
                act.wait_ge(qk_ready, i + 1)
                wait_past(act, S_ready, i * GROUPS)
                for n in range(2 * GROUPS):
                    cp = act.activation(qkT[:, n // GROUPS, n % GROUPS, :],
                                        ps[:, 1 + n // 2, (n % 2) * TOK:(n % 2 + 1) * TOK], ACT.Identity,
                                        bias=bqk[:, n // GROUPS, n % GROUPS:n % GROUPS + 1])
                cp.then_inc(qk_copied, 1)

            @staticmethod
            def probs(act, i, j):
                act.wait_ge(S_shifted, i * GROUPS + j + 1)
                s = S[:, HG * j:HG * (j + 1), :]
                act.activation(s, s, ACT.Exp).then_inc(P_ready, 1)

            @staticmethod
            def probs_turn(act, i, j):
                act.wait_ge(PT_ready, i * GROUPS + j + 1)
                if j == 0:
                    wait_past(act, O_ready, i)
                act.activation(PT[:, HG * j:HG * (j + 1), :], ps[0:TT, 0:HG, 0:CAUS],
                               ACT.Copy).then_inc(PT_copied, 1)

        def layernorm_stats(dve, i, src, st, mv, src_ready, st_ready, mv_ready):
            dve.wait_ge(src_ready, i + 1)
            for t in range(2):
                s_ = dve.bn_stats(st[:, t, :], src[:, t, :])
            s_.then_inc(st_ready, 1)
            dve.wait_ge(st_ready, i + 1)
            dve.memset(spare[:, :], 0.0)
            for t in range(2):
                s_ = dve.bn_aggr(mv[:, t, :], st[:, t, :])
            s_.then_inc(mv_ready, 1)

        class dve_att:
            @staticmethod
            def embed(dve, i):
                dve.wait_ge(Z_ready, i + 1)
                wait_past(dve, hb_ready, i)
                dve.tensor_tensor(h[:, :, :], ps[0:TT, 3, 0:2 * EMB].rearrange("p (t e) -> p t e", t=2),
                                  posb[:, :, :], ALU.add).then_inc(h_ready, 1)
                layernorm_stats(dve, i, h, st1, mv1, h_ready, st1_ready, mv1_ready)

            @staticmethod
            def norm1(dve, i):
                dve.wait_ge(rs1_ready, i + 1)
                wait_past(dve, xn1T_ready, i)
                for t in range(2):
                    s_ = dve.tensor_scalar(xn1[:, t, :], h[:, t, :], mv1[:, t, 0:1], rs1[:, t:t + 1],
                                           ALU.subtract, ALU.mult)
                s_.then_inc(xn1_ready, 1)

            @staticmethod
            def v(dve, i):
                dve.wait_ge(v_ready, i + 1)
                wait_past(dve, O_ready, i)
                for t in range(2):
                    s_ = dve.tensor_tensor(vaug[:, t, :, 0:HS],
                                           ps[0:TT, 0, t * EMB:(t + 1) * EMB].rearrange("p (n r) -> p n r", r=HS),
                                           bv[:, :].rearrange("p (n r) -> p n r", r=HS), ALU.add)
                s_.then_inc(v_copied, 1)

            @staticmethod
            def softmax(dve, i, j):
                n = i * GROUPS + j + 1
                s = S[:, HG * j:HG * (j + 1), :]
                dve.wait_ge(S_ready, n)
                wait_past(dve, PT_ready, i * GROUPS)
                dve.scalar_tensor_tensor(out=s, in0=ps[0:TT, 0:HG, 0:CAUS], scalar=SCALE,
                                         in1=mask[:, :].unsqueeze(1).broadcast_to([TT, HG, CAUS]),
                                         op0=ALU.mult, op1=ALU.add).then_inc(S_masked, 1)
                dve.wait_ge(S_masked, n)
                for t in range(2):
                    m = dve.tensor_reduce(mx[:, t, HG * j:HG * (j + 1)], s[:, :, t * TT:(2 * t + 1) * TT], AX.X,
                                          ALU.max)
                m.then_inc(mx_ready, 1)
                dve.wait_ge(mx_ready, n)
                for t in range(2):
                    w = (t + 1) * TT
                    sh = dve.tensor_tensor(s[:, :, t * TT:t * TT + w], s[:, :, t * TT:t * TT + w],
                                           mx[:, t, HG * j:HG * (j + 1)].unsqueeze(2).broadcast_to([TT, HG, w]),
                                           ALU.subtract)
                sh.then_inc(S_shifted, 1)

            @staticmethod
            def weigh(dve, i):
                dve.wait_ge(O_ready, i + 1)
                o = ps[0:TT, 0, 0:2 * HEADS * (HS + 1)].rearrange("p (t n r) -> p t n r", t=2, n=HEADS)
                dve.reciprocal(rden[:, :, :], o[:, :, :, HS]).then_inc(rden_ready, 1)
                dve.wait_ge(rden_ready, i + 1)
                wait_past(dve, onT_ready, i)
                for t in range(2):
                    m = dve.tensor_tensor(on[:, t, :].rearrange("p (n r) -> p n r", r=HS), o[:, t, :, 0:HS],
                                          rden[:, t, :].unsqueeze(2).broadcast_to([TT, HEADS, HS]), ALU.mult)
                m.then_inc(on_ready, 1)

            @staticmethod
            def resid(dve, i):
                dve.wait_ge(proj_ready, i + 1)
                dve.wait_ge(hb_ready, i + 1)
                wait_past(dve, h2_stored, i * 16)
                dve.tensor_tensor(h2[:, :, :], ps[0:TT, 2, 0:2 * EMB].rearrange("p (t e) -> p t e", t=2),
                                  hb[:, :, :], ALU.add).then_inc(h2_ready, 1)
                layernorm_stats(dve, i, h2, st2, mv2, h2_ready, st2_ready, mv2_ready)

            @staticmethod
            def norm2(dve, i):
                dve.wait_ge(rs2_ready, i + 1)
                wait_past(dve, Xs_ready, i * 4)
                for t in range(2):
                    s_ = dve.tensor_scalar(xn2[:, t, 0:EMB], h2[:, t, :], mv2[:, t, 0:1], rs2[:, t:t + 1],
                                           ALU.subtract, ALU.mult)
                s_.then_inc(xn2_ready, 1)

        def pool_rstd(pool, i, mv, ve, rs, mv_ready, ve_ready, rs_ready, reader):
            pool.wait_ge(mv_ready, i + 1)
            pool.tensor_tensor(ve[:, :], mv[:, :, 1], eps_ln[0:TT, 0:2], ALU.add).then_inc(ve_ready, 1)
            pool.wait_ge(ve_ready, i + 1)
            wait_past(pool, reader, i)
            pool.tensor_tensor(rs[:, :], ve[:, :], minus_half[0:TT, 0:2], ALU.pow).then_inc(rs_ready, 1)

        class pe_moe:
            @staticmethod
            def logits(pe, i, k):
                if k == 0:
                    pe.wait_ge(xn2T_copied, i + 1)
                    wait_past(pe, xs_ready, i * 4)
                for j in (2 * k, 2 * k + 1):
                    for c in range(2):
                        mm = pe.matmul(ps[:, 4 + k, (j % 2) * TOK:(j % 2 + 1) * TOK], phiT[:, c, j, :],
                                       xn2T[:, c, :], start=(c == 0), stop=(c == 1))
                mm.then_inc(LT_ready, 1)

            @staticmethod
            def tokmax_turn(pe, i):
                pe.wait_ge(tpart_ready, i + 1)
                pe.wait_ge(LT_copied, (i + 1) * 4)
                for t in range(2):
                    mm = pe.transpose(ps[0:TT, 4, t * 128:(t + 1) * 128], tok_part[:, t * TT:(t + 1) * TT],
                                      ident[:, :])
                mm.then_inc(tpartT_ready, 1)

            @staticmethod
            def tokmax_spread(pe, i):
                pe.wait_ge(tdiag_ready, i + 1)
                for t in range(2):
                    mm = pe.matmul(ps[:, 5, t * TT:(t + 1) * TT], ones[:, :], tok_diag[:, t, :],
                                   start=True, stop=True)
                mm.then_inc(tbc_ready, 1)

            @staticmethod
            def shifted_turn(pe, i):
                pe.wait_ge(Td_ready, i + 1)
                pe.wait_ge(U_ready, i + 1)
                for t in range(2):
                    for j in range(SJ):
                        mm = pe.transpose(ps[0:TT, 4 + 2 * t + j // 4, (j % 4) * 128:(j % 4 + 1) * 128],
                                          Td[:, j, t * TT:(t + 1) * TT], ident[:, :])
                mm.then_inc(TdT_ready, 1)

            @staticmethod
            def dispatch(pe, i, k):
                pe.wait_ge(E_ready, i + 1)
                for j in (2 * k, 2 * k + 1):
                    for t in range(2):
                        mm = pe.matmul(ps[:, 4 + k, (j % 2) * (EMB + 1):(j % 2 + 1) * (EMB + 1)],
                                       E[:, t, j * 128:(j + 1) * 128], xn2[:, t, :],
                                       start=(t == 0), stop=(t == 1))
                mm.then_inc(Xs_ready, 1)

        class act_moe:
            @staticmethod
            def logits(act, i, k):
                act.wait_ge(LT_ready, i * 4 + k + 1)
                if k == 0:
                    wait_past(act, U_ready, i)
                act.activation(LT[:, 2 * k:2 * k + 2, :], seg(4 + k), ACT.Copy).then_inc(LT_copied, 1)

            @staticmethod
            def combine(act, i):
                act.wait_ge(U_ready, i + 1)
                act.activation(CT[:, :, :], CT[:, :, :], ACT.Exp).then_inc(CT_ready, 1)

            @staticmethod
            def dispatch(act, i):
                act.wait_ge(TdT_ready, i + 1)
                wait_past(act, Xs_ready, i * 4)
                act.activation(E[:, :, :], ps[0:TT, 4:8, :].rearrange("p (t k) n -> p t (k n)", t=2),
                               ACT.Exp).then_inc(E_ready, 1)

        class dve_moe:
            @staticmethod
            def maxima(dve, i):
                dve.wait_ge(LT_copied, (i + 1) * 4)
                wait_past(dve, tpartT_ready, i)
                dve.tensor_reduce(tok_part[:, :], LT[:, :, :].rearrange("p j t -> p t j"), AX.X,
                                  ALU.max).then_inc(tpart_ready, 1)
                dve.tensor_reduce(slot_max[:, :], LT[:, :, :], AX.X, ALU.max).then_inc(smax_ready, 1)

            @staticmethod
            def shift(dve, i):
                dve.wait_ge(smax_ready, i + 1)
                wait_past(dve, TdT_ready, i)
                dve.tensor_tensor(Td[:, :, :], LT[:, :, :],
                                  slot_max[:, :].unsqueeze(2).broadcast_to([128, SJ, TOK]),
                                  ALU.subtract).then_inc(Td_ready, 1)

            @staticmethod
            def tokmax(dve, i):
                dve.wait_ge(tpartT_ready, i + 1)
                dve.tensor_reduce(tok_max[:, :], ps[0:TT, 4, 0:256].rearrange("p (t n) -> p t n", t=2), AX.X,
                                  ALU.max).then_inc(tmax_ready, 1)
                dve.wait_ge(tmax_ready, i + 1)
                for t in range(2):
                    d = dve.tensor_scalar(tok_diag[:, t, :], ident[0:TT, 0:TT], tok_max[:, t:t + 1], None,
                                          ALU.mult)
                d.then_inc(tdiag_ready, 1)

            @staticmethod
            def combine(dve, i):
                dve.wait_ge(tbc_ready, i + 1)
                wait_past(dve, CT_stored, i * 16)
                dve.tensor_tensor(CT[:, :, :], LT[:, :, :],
                                  ps[:, 5, 0:TOK].unsqueeze(1).broadcast_to([128, SJ, TOK]),
                                  ALU.subtract).then_inc(U_ready, 1)

            @staticmethod
            def dispatch(dve, i, k):
                n = i * 4 + k + 1
                o = seg(4 + k, EMB + 1)
                dve.wait_ge(Xs_ready, n)
                dve.reciprocal(rz[:, 2 * k:2 * k + 2], o[:, :, EMB]).then_inc(rz_ready, 1)
                dve.wait_ge(rz_ready, n)
                if k == 0:
                    wait_past(dve, xs_stored, i * 16)
                dve.tensor_tensor(xs[:, 2 * k:2 * k + 2, :], o[:, :, 0:EMB],
                                  rz[:, 2 * k:2 * k + 2].unsqueeze(2).broadcast_to([128, 2, EMB]),
                                  ALU.mult).then_inc(xs_ready, 1)

        def load_x(sp, i):
            for r in range(SIDE):
                src = x[i, r * PATCH:(r + 1) * PATCH, :, :].rearrange(
                    "a (j b) c -> j a (b c)", j=SIDE)
                p0 = (r % HI) * SIDE
                dst = xin[p0:p0 + SIDE, r // HI, :].rearrange("p (a f) -> p a f", a=PATCH)
                sp.dma_start(dst, src).then_inc(x_loaded, 16)

        def order(att, moe):
            both = ["a.patches", "m.l0", "m.l1", "a.embed", "m.l2", "m.l3", "m.maxima", "a.turn1",
                    "m.tokmax", "m.spread", "a.qkv", "m.dturn",
                    "a.s0", "m.x0", "a.s1", "m.x1", "a.s2", "m.x2", "a.p0", "m.x3", "a.p1", "a.p2",
                    "a.weigh", "a.turno", "a.proj", "a.turn2"]
            return [s for s in both if (att and s[0] == "a") or (moe and s[0] == "m")]

        def run_pe(pe, i, att, moe):
            for s in order(att, moe):
                if s == "a.patches":
                    pe_att.patches(pe, i)
                elif s == "a.embed":
                    pe_att.embed(pe, i)
                elif s == "a.turn1":
                    pe_att.turn(pe, i, xn1, 0, xn1_ready, xn1T_ready)
                elif s == "a.qkv":
                    pe_att.qkv(pe, i)
                elif s in ("a.s0", "a.s1", "a.s2"):
                    pe_att.scores(pe, i, int(s[3]))
                elif s in ("a.p0", "a.p1", "a.p2"):
                    pe_att.probs_turn(pe, i, int(s[3]))
                elif s == "a.weigh":
                    pe_att.weigh(pe, i)
                elif s == "a.turno":
                    pe_att.turn(pe, i, on, 1, on_ready, onT_ready)
                elif s == "a.proj":
                    pe_att.proj(pe, i)
                elif s == "a.turn2":
                    pe_att.turn(pe, i, xn2, 3, xn2_ready, xn2T_ready)
                elif s[:3] == "m.l":
                    pe_moe.logits(pe, i - 1, int(s[3]))
                elif s == "m.tokmax":
                    pe_moe.tokmax_turn(pe, i - 1)
                elif s == "m.spread":
                    pe_moe.tokmax_spread(pe, i - 1)
                elif s == "m.dturn":
                    pe_moe.shifted_turn(pe, i - 1)
                elif s[:3] == "m.x":
                    pe_moe.dispatch(pe, i - 1, int(s[3]))

        def run_act(act, i, att, moe):
            for s in order(att, moe):
                if s == "a.patches":
                    act_att.patches(act, i)
                elif s == "a.turn1":
                    act_att.turn(act, i, xn1T, 0, xn1T_ready, xn1T_copied)
                elif s == "a.qkv":
                    act_att.qk(act, i)
                elif s in ("a.s0", "a.s1", "a.s2"):
                    act_att.probs(act, i, int(s[3]))
                elif s in ("a.p0", "a.p1", "a.p2"):
                    act_att.probs_turn(act, i, int(s[3]))
                elif s == "a.turno":
                    act_att.turn(act, i, onT, 1, onT_ready, onT_copied)
                elif s == "a.turn2":
                    wait_past(act, LT_ready, i * 4)
                    act_att.turn(act, i, xn2T, 3, xn2T_ready, xn2T_copied)
                elif s[:3] == "m.l":
                    act_moe.logits(act, i - 1, int(s[3]))
                elif s == "m.spread":
                    act_moe.combine(act, i - 1)
                elif s == "m.dturn":
                    act_moe.dispatch(act, i - 1)

        def run_dve(dve, i, att, moe):
            for s in order(att, moe):
                if s == "a.embed":
                    dve_att.embed(dve, i)
                elif s == "a.turn1":
                    dve_att.norm1(dve, i)
                elif s == "a.qkv":
                    dve_att.v(dve, i)
                elif s in ("a.s0", "a.s1", "a.s2"):
                    dve_att.softmax(dve, i, int(s[3]))
                elif s == "a.weigh":
                    dve_att.weigh(dve, i)
                elif s == "a.proj":
                    dve_att.resid(dve, i)
                elif s == "a.turn2":
                    dve_att.norm2(dve, i)
                elif s == "m.maxima":
                    dve_moe.maxima(dve, i - 1)
                elif s == "m.tokmax":
                    dve_moe.tokmax(dve, i - 1)
                    dve_moe.shift(dve, i - 1)
                elif s == "m.spread":
                    dve_moe.combine(dve, i - 1)
                elif s[:3] == "m.x":
                    dve_moe.dispatch(dve, i - 1, int(s[3]))

        def run_pool(pool, i, att, moe):
            if att:
                pool_rstd(pool, i, mv1, ve1, rs1, mv1_ready, ve1_ready, rs1_ready, xn1_ready)
                wait_past(pool, h2_ready, i)
                pool.tensor_tensor(hb[:, :, :], h[:, :, :],
                                   bproj[:, :].unsqueeze(1).broadcast_to([TT, 2, EMB]),
                                   ALU.add).then_inc(hb_ready, 1)
                pool_rstd(pool, i, mv2, ve2, rs2, mv2_ready, ve2_ready, rs2_ready, xn2_ready)

        def run_sp(sp, i, att, moe, load):
            if load:
                sp.wait_ge(xT_ready, i + 1)
                load_x(sp, i + 1)
            if moe:
                wait_past(sp, CT_ready, i)
                sp.dma_start(ct_d[i - 1], CT[:, :, :].rearrange("p j t -> p (j t)")).then_inc(CT_stored, 16)
                wait_past(sp, xs_ready, i * 4)
                sp.dma_start(xs_d[:, i - 1, :, :].rearrange("n (a j) d -> n a (j d)", a=2),
                             xs[:, :, :].rearrange("q j d -> q (j d)")).then_inc(xs_stored, 16)
            if att:
                sp.wait_ge(h2_ready, i + 1)
                sp.dma_start(h2_d[i], h2[:, :, :].rearrange("p t e -> p (t e)")).then_inc(h2_stored, 16)

        with nc.Block() as blk:
            @blk.sync
            def _(sp):
                load_x(sp, 0)
                run_sp(sp, 0, True, False, True)
                run_sp(sp, 1, True, True, True)
                with sp.Fori(2, B - 1) as i:
                    run_sp(sp, i, True, True, True)
                run_sp(sp, B - 1, True, True, False)
                run_sp(sp, B, False, True, False)
                sp.wait_ge(xs_stored, B * 16)
                sp.wait_ge(CT_stored, B * 16)
                sp.wait_ge(h2_stored, B * 16)

            @blk.tensor
            def _(pe):
                run_pe(pe, 0, True, False)
                run_pe(pe, 1, True, True)
                with pe.Fori(2, B) as i:
                    run_pe(pe, i, True, True)
                run_pe(pe, B, False, True)

            @blk.scalar
            def _(act):
                run_act(act, 0, True, False)
                run_act(act, 1, True, True)
                with act.Fori(2, B) as i:
                    run_act(act, i, True, True)
                run_act(act, B, False, True)

            @blk.vector
            def _(dve):
                run_dve(dve, 0, True, False)
                run_dve(dve, 1, True, True)
                with dve.Fori(2, B) as i:
                    run_dve(dve, i, True, True)
                run_dve(dve, B, False, True)

            @blk.gpsimd
            def _(pool):
                run_pool(pool, 0, True, False)
                run_pool(pool, 1, True, True)
                with pool.Fori(2, B) as i:
                    run_pool(pool, i, True, True)

        ein = [sb(f"ein{u}", [128, RJ, EMB]) for u in range(2)]
        ew1 = [sb(f"ew1_{u}", [FC, 2, HID]) for u in range(2)]
        ew2 = [sb(f"ew2_{u}", [128, HC, EMB]) for u in range(2)]
        eb2 = [sb(f"eb2_{u}", [128, EMB]) for u in range(2)]
        col = sb("ecol", [128, 2 * 2 + HC])
        est = sb("est", [128, RJ, 6])
        emv = sb("emv", [128, RJ, 2])
        eve = sb("eve", [128, RJ])
        ers = sb("ers", [128, RJ])

        def region(t, shape):
            flat = t.rearrange("p a c -> p (a c)")
            n = 1
            for s in shape:
                n *= s
            return flat[:, 0:n].rearrange("p (a c) -> p a c", c=shape[-1])

        ehn = region(LT[:, :, :], [RJ, EMB])
        ehT = E[0:FC, :, :]
        ys = region(Td[:, :, :], [RJ, EMB])
        hid = sb("hid", [128, HC, ROWS])

        e_loaded = [sem(f"e_loaded{u}") for u in range(2)]
        est_ready = sem("est_ready")
        emv_ready = sem("emv_ready")
        eve_ready = sem("eve_ready")
        ers_ready = sem("ers_ready")
        ehn_ready = sem("ehn_ready")
        ehT_ready = sem("ehT_ready")
        col_ready = sem("col_ready")
        ehT_copied = sem("ehT_copied")
        H_ready = sem("H_ready")
        H_copied = sem("H_copied")
        Y_ready = sem("Y_ready")
        Y_copied = sem("Y_copied")
        ys_stored = sem("ys_stored")
        NH = 2 * HC

        def load_expert(sp, n, u, k):
            wait_past(sp, Y_ready, (n - 1) * 4)
            sp.dma_start(ein[u][:, :, :].rearrange("r j d -> r (j d)"),
                         xs_d[n].rearrange("b p d -> (b p) d").rearrange("(r j) d -> r (j d)", j=RJ)
                         ).then_inc(e_loaded[u], 16)
            sp.dma_start(ew1[u][:, :, :], w1[n].rearrange("(c p) f -> p c f", p=FC)).then_inc(e_loaded[u], 16)
            sp.dma_start(ew2[u][:, :, :], w2[n].rearrange("(c p) f -> p c f", p=128)).then_inc(e_loaded[u], 16)
            sp.dma_start(eb2[u][:, :], b2[n].partition_broadcast(128)).then_inc(e_loaded[u], 16)

        def store_expert(sp, n):
            sp.wait_ge(Y_copied, (n + 1) * 4)
            sp.dma_start(ys_d[n].rearrange("b p d -> (b p) d").rearrange("(r j) d -> r (j d)", j=RJ),
                         ys.rearrange("r j d -> r (j d)")).then_inc(ys_stored, 16)

        def expert_pre_dve(dve, n, u, k):
            dve.wait_ge(e_loaded[u], k * 64)
            for t in range(RJ):
                s_ = dve.bn_stats(est[:, t, :], ein[u][:, t, :])
            s_.then_inc(est_ready, 1)
            dve.wait_ge(est_ready, n + 1)
            dve.memset(spare[:, :], 0.0)
            for t in range(RJ):
                s_ = dve.bn_aggr(emv[:, t, :], est[:, t, :])
            s_.then_inc(emv_ready, 1)
            wait_past(dve, H_copied, n * NH)
            dve.tensor_copy(col[0:FC, 0:2], gT[:, :, n])
            dve.tensor_copy(col[0:FC, 2:4], bT[:, :, n])
            dve.tensor_copy(col[:, 4:4 + HC], b1T[:, :, n]).then_inc(col_ready, 1)
            dve.wait_ge(ers_ready, n + 1)
            for t in range(RJ):
                s_ = dve.tensor_scalar(ehn[:, t, :], ein[u][:, t, :], emv[:, t, 0:1], ers[:, t:t + 1],
                                       ALU.subtract, ALU.mult)
            s_.then_inc(ehn_ready, 1)

        def expert_pre_pe(pe, n):
            pe.wait_ge(ehn_ready, n + 1)
            wait_past(pe, ehT_copied, n * 4)
            for c in range(2):
                for hh in range(2):
                    for t in range(4):
                        mm = pe.transpose(ps[0:FC, 2 * c + hh, t * 128:(t + 1) * 128],
                                          ehn[:, 4 * hh + t, c * FC:(c + 1) * FC], ident[:, :])
                    mm.then_inc(ehT_ready, 1)

        def expert_pre_act(act, n):
            act.wait_ge(col_ready, n + 1)
            wait_past(act, H_ready, n * NH)
            for c in range(2):
                for hh in range(2):
                    act.wait_ge(ehT_ready, n * 4 + 2 * c + hh + 1)
                    act.activation(ehT[:, c, hh * 512:(hh + 1) * 512], ps[0:FC, 2 * c + hh, :], ACT.Identity,
                                   bias=col[0:FC, 2 + c:3 + c], scale=col[0:FC, c:c + 1]
                                   ).then_inc(ehT_copied, 1)

        def expert_pe(pe, n, u, k):
            pe.wait_ge(e_loaded[u], k * 64)
            pe.wait_ge(ehT_copied, (n + 1) * 4)
            for m in range(NH):
                if m >= 2:
                    pe.wait_ge(H_copied, n * NH + m - 1)
                else:
                    wait_past(pe, H_copied, n * NH)
                for c in range(2):
                    mm = pe.matmul(ps[:, 4 + m % 2, :], ew1[u][:, c, (m // 2) * 128:(m // 2 + 1) * 128],
                                   ehT[:, c, (m % 2) * 512:(m % 2 + 1) * 512], start=(c == 0), stop=(c == 1))
                mm.then_inc(H_ready, 1)

        def expert_act(act, n):
            wait_past(act, Y_ready, n * 4)
            for m in range(NH):
                act.wait_ge(H_ready, n * NH + m + 1)
                act.activation(hid[:, m // 2, (m % 2) * 512:(m % 2 + 1) * 512], ps[:, 4 + m % 2, :], ACT.Gelu,
                               bias=col[:, 4 + m // 2:5 + m // 2]).then_inc(H_copied, 1)

        def expert_pe2(pe, n, u):
            pe.wait_ge(H_copied, (n + 1) * NH)
            for m in range(4):
                if m >= 2:
                    pe.wait_ge(Y_copied, n * 4 + m - 1)
                else:
                    wait_past(pe, Y_copied, n * 4)
                for t in (2 * m, 2 * m + 1):
                    for c in range(HC):
                        mm = pe.matmul(ps[:, 6 + m % 2, (t % 2) * EMB:(t % 2 + 1) * EMB],
                                       hid[:, c, t * 128:(t + 1) * 128], ew2[u][:, c, :],
                                       start=(c == 0), stop=(c == HC - 1))
                mm.then_inc(Y_ready, 1)

        def expert_dve(dve, n, u):
            wait_past(dve, ys_stored, n * 16)
            for m in range(4):
                dve.wait_ge(Y_ready, n * 4 + m + 1)
                dve.tensor_tensor(ys[:, 2 * m:2 * m + 2, :],
                                  ps[:, 6 + m % 2, 0:2 * EMB].rearrange("p (t e) -> p t e", t=2),
                                  eb2[u][:, :].unsqueeze(1).broadcast_to([128, 2, EMB]),
                                  ALU.add).then_inc(Y_copied, 1)

        with nc.Block() as blk:
            @blk.sync
            def _(sp):
                load_expert(sp, 0, 0, 0)
                load_expert(sp, 1, 1, 0)
                store_expert(sp, 0)
                load_expert(sp, 2, 0, 1)
                store_expert(sp, 1)
                with sp.Fori(1, NX // 2 - 1) as i:
                    load_expert(sp, 2 * i + 1, 1, i)
                    store_expert(sp, 2 * i)
                    load_expert(sp, 2 * i + 2, 0, i + 1)
                    store_expert(sp, 2 * i + 1)
                load_expert(sp, NX - 1, 1, NX // 2 - 1)
                store_expert(sp, NX - 2)
                store_expert(sp, NX - 1)
                sp.wait_ge(ys_stored, NX * 16)

            @blk.tensor
            def _(pe):
                expert_pre_pe(pe, 0)
                for u in range(2):
                    expert_pe(pe, u, u, 1)
                    expert_pre_pe(pe, u + 1)
                    expert_pe2(pe, u, u)
                with pe.Fori(1, NX // 2 - 1) as i:
                    for u in range(2):
                        expert_pe(pe, 2 * i + u, u, i + 1)
                        expert_pre_pe(pe, 2 * i + u + 1)
                        expert_pe2(pe, 2 * i + u, u)
                expert_pe(pe, NX - 2, 0, NX // 2)
                expert_pre_pe(pe, NX - 1)
                expert_pe2(pe, NX - 2, 0)
                expert_pe(pe, NX - 1, 1, NX // 2)
                expert_pe2(pe, NX - 1, 1)

            @blk.scalar
            def _(act):
                expert_pre_act(act, 0)
                expert_act(act, 0)
                expert_pre_act(act, 1)
                with act.Fori(1, NX - 1) as n:
                    expert_act(act, n)
                    expert_pre_act(act, n + 1)
                expert_act(act, NX - 1)

            @blk.vector
            def _(dve):
                expert_pre_dve(dve, 0, 0, 1)
                expert_pre_dve(dve, 1, 1, 1)
                expert_dve(dve, 0, 0)
                expert_pre_dve(dve, 2, 0, 2)
                expert_dve(dve, 1, 1)
                with dve.Fori(1, NX // 2 - 1) as i:
                    expert_pre_dve(dve, 2 * i + 1, 1, i + 1)
                    expert_dve(dve, 2 * i, 0)
                    expert_pre_dve(dve, 2 * i + 2, 0, i + 2)
                    expert_dve(dve, 2 * i + 1, 1)
                expert_pre_dve(dve, NX - 1, 1, NX // 2)
                expert_dve(dve, NX - 2, 0)
                expert_dve(dve, NX - 1, 1)

            @blk.gpsimd
            def _(pool):
                with pool.Fori(0, NX) as n:
                    pool.wait_ge(emv_ready, n + 1)
                    pool.tensor_tensor(eve[:, :], emv[:, :, 1], eps_ln[:, :], ALU.add).then_inc(eve_ready, 1)
                    pool.wait_ge(eve_ready, n + 1)
                    pool.tensor_tensor(ers[:, :], eve[:, :], minus_half[:, :], ALU.pow).then_inc(ers_ready, 1)

        YW = EMB + 1
        cct = [region(PT2, [SJ, TOK]) for PT2 in (LT[:, :, :], CT[:, :, :])]
        cys = [sb(f"cys{u}", [128, SJ, YW]) for u in range(2)]
        ch2 = [h, h2]
        cout = [xn1, on]
        crd = [rs1, rs2]

        c_loaded = [sem(f"c_loaded{u}") for u in range(2)]
        ones_set = sem("ones_set")
        comb_ready = sem("comb_ready")
        crd_ready = sem("crd_ready")
        cout_ready = sem("cout_ready")
        out_stored = [sem(f"out_stored{u}") for u in range(2)]

        def load_comb(sp, i, u):
            sp.dma_start(cct[u].rearrange("p j t -> p (j t)"), ct_d[i]).then_inc(c_loaded[u], 16)
            sp.dma_start(cys[u][:, :, 0:EMB], ys_d[:, i, :, :].rearrange("n (a j) d -> n a (j d)", a=2)
                         ).then_inc(c_loaded[u], 16)
            sp.dma_start(ch2[u][:, :, :].rearrange("p t e -> p (t e)"), h2_d[i]).then_inc(c_loaded[u], 16)

        def store_out(sp, i, u):
            sp.wait_ge(cout_ready, i + 1)
            for t in range(2):
                sp.dma_start(out[i, t * TT:(t + 1) * TT, :], cout[u][:, t, :]).then_inc(out_stored[u], 16)

        def comb_pe(pe, i, u, k):
            pe.wait_ge(c_loaded[u], k * 48)
            wait_past(pe, cout_ready, i - 1)
            for t in range(2):
                for j in range(SJ):
                    mm = pe.matmul(ps[0:TT, u, t * YW:(t + 1) * YW], cct[u][:, j, t * TT:(t + 1) * TT],
                                   cys[u][:, j, :], start=(j == 0), stop=(j == SJ - 1))
            mm.then_inc(comb_ready, 1)

        def comb_dve(dve, i, u, k):
            dve.wait_ge(c_loaded[u], k * 48)
            dve.wait_ge(comb_ready, i + 1)
            dve.reciprocal(crd[u][:, :], ps[0:TT, u, 0:2 * YW].rearrange("p (t e) -> p t e", t=2)[:, :, EMB]
                           ).then_inc(crd_ready, 1)
            dve.wait_ge(crd_ready, i + 1)
            wait_past(dve, out_stored[u], (k - 1) * 32)
            for t in range(2):
                o = dve.scalar_tensor_tensor(out=cout[u][:, t, :], in0=ps[0:TT, u, t * YW:t * YW + EMB],
                                             scalar=crd[u][:, t:t + 1], in1=ch2[u][:, t, :],
                                             op0=ALU.mult, op1=ALU.add)
            o.then_inc(cout_ready, 1)

        with nc.Block() as blk:
            @blk.sync
            def _(sp):
                sp.wait_ge(ones_set, 2)
                load_comb(sp, 0, 0)
                load_comb(sp, 1, 1)
                with sp.Fori(0, B // 2 - 1) as i:
                    for u in range(2):
                        store_out(sp, 2 * i + u, u)
                        load_comb(sp, 2 * i + 2 + u, u)
                for u in range(2):
                    store_out(sp, B - 2 + u, u)
                for u in range(2):
                    sp.wait_ge(out_stored[u], B // 2 * 32)

            @blk.tensor
            def _(pe):
                pe.wait_ge(ones_set, 2)
                comb_pe(pe, 0, 0, 1)
                comb_pe(pe, 1, 1, 1)
                with pe.Fori(1, B // 2) as i:
                    for u in range(2):
                        comb_pe(pe, 2 * i + u, u, i + 1)

            @blk.vector
            def _(dve):
                for u in range(2):
                    dve.memset(cys[u][:, :, :], 1.0).then_inc(ones_set, 1)
                for u in range(2):
                    comb_dve(dve, u, u, 1)
                with dve.Fori(1, B // 2) as i:
                    for u in range(2):
                        comb_dve(dve, 2 * i + u, u, i + 1)


_INS = ['x', 'cls_tok', 'L0_tok_W', 'L0_tok_b', 'L0_tok_cls_token', 'L0_tok_pos_embed', 'L0_attn_W_attn',
        'L0_attn_b_attn', 'L0_attn_W_proj', 'L0_attn_b_proj', 'L0_ffn_phi', 'L0_ffn_ln_g', 'L0_ffn_ln_b',
        'L0_ffn_w1', 'L0_ffn_b1', 'L0_ffn_w2', 'L0_ffn_b2']
_OUTS = [((64, 198, 192), 'float32')]


def kernel(**inputs):
    import numpy as _np
    import concourse.bacc as _bacc
    from concourse import mybir as _mybir
    from concourse.bass_utils import run_bass_kernel_spmd as _run

    nc = _bacc.Bacc("TRN2", target_bir_lowering=False, num_devices=1)
    arrays, args = {}, []
    for name in _INS:
        a = _np.ascontiguousarray(inputs[name])
        arrays[f"in_{name}_dram"] = a
        args.append(nc.dram_tensor(f"in_{name}_dram", a.shape, _mybir.dt.from_np(a.dtype), kind="ExternalInput").ap())
    for i, (shape, dtype) in enumerate(_OUTS):
        dt = _mybir.dt.from_np(_np.dtype(dtype))
        args.append(nc.dram_tensor(f"out_{i}_dram", shape, dt, kind="ExternalOutput").ap())
    vit_tower(nc, *args)
    r = _run(nc, [arrays], core_ids=[0])
    got = tuple(r.results[0][f"out_{i}_dram"] for i in range(len(_OUTS)))
    return got[0]
```

```python
from contextlib import ExitStack

import concourse.bass as bass
from concourse import mybir

F32 = mybir.dt.float32
ALU = mybir.AluOpType
ACT = mybir.ActivationFunctionType
AX = mybir.AxisListType


def vit_tower(
    nc: bass.Bass,
    x: bass.AP,
    cls_tok: bass.AP,
    W: bass.AP,
    b: bass.AP,
    cls_token: bass.AP,
    pos_embed: bass.AP,
    W_attn: bass.AP,
    b_attn: bass.AP,
    W_proj: bass.AP,
    b_proj: bass.AP,
    phi: bass.AP,
    ln_g: bass.AP,
    ln_b: bass.AP,
    w1: bass.AP,
    b1: bass.AP,
    w2: bass.AP,
    b2: bass.AP,
    out: bass.AP,
):
    B, IMG, _, CH = x.shape
    EMB, PD = W.shape
    PATCH = 16
    SIDE = IMG // PATCH
    NPATCH = SIDE * SIDE
    TOK = NPATCH + 2
    TT = TOK // 2
    HP = NPATCH // 2
    HI = SIDE // 2
    PX = PATCH * CH
    HEADS = 12
    WIN = 6
    HS = EMB // HEADS
    HG = 4
    GROUPS = HEADS // HG
    FC = 96
    NX, NPX, _ = phi.shape
    SLOTS = NX * NPX
    SJ = SLOTS // 128
    HID = w1.shape[2]
    HC = HID // 128
    ROWS = B * NPX
    RJ = ROWS // 128
    KC = PD // 128
    CAUS = 3 * TT
    SCALE = float(HS) ** -0.5
    NEG = -1.0e30
    EPS = 1e-5
    EPS_NORM = 1e-6
    assert TOK == 2 * TT and EMB == 2 * FC and SJ * 16 == 128 and RJ == 8 and B % 2 == 0 and NX % 2 == 0

    ctx = ExitStack()
    with ctx:
        def sb(name, shape, dtype=F32):
            return ctx.enter_context(nc.sbuf_tensor(name, shape, dtype))

        def sbp(phase, name, shape, dtype=F32):
            return phase.enter_context(nc.sbuf_tensor(name, shape, dtype))

        def sem(name):
            return ctx.enter_context(nc.semaphore(name))

        def wait_past(eng, signal, value):
            if not (isinstance(value, int) and value <= 0):
                eng.wait_ge(signal, value)

        ctx.enter_context(nc.allow_non_contiguous_dma(reason="small biases, transposed once"))

        xs_d = nc.dram_tensor("xs_scratch", (NX, B, NPX, EMB), F32, kind="Internal").ap()
        ys_d = nc.dram_tensor("ys_scratch", (NX, B, NPX, EMB), F32, kind="Internal").ap()
        ct_d = nc.dram_tensor("combine_scratch", (B, 128, SJ * TOK), F32, kind="Internal").ap()
        h2_d = nc.dram_tensor("residual_scratch", (B, TT, 2 * EMB), F32, kind="Internal").ap()

        ps = ctx.enter_context(nc.psum_tensor("ps", [128, 8, 512], F32))

        ident = sb("ident", [128, 128])
        ones = sb("ones", [TT, 128])
        mask = sb("mask", [TT, CAUS])
        WT = sb("WT", [128, KC, EMB])
        wqk = sb("wqk", [FC, 2, 2, GROUPS, HG, 32])
        watt = sb("watt", [FC, 2, 3 * EMB])
        wproj = sb("wproj", [FC, 2, EMB])
        bqk = sb("bqk", [128, 2, GROUPS])
        bv = sb("bv", [TT, EMB])
        bproj = sb("bproj", [TT, EMB])
        posb = sb("posb", [TT, 2, EMB])
        phiT = sb("phiT", [FC, 2, SJ, 128])
        minus_half = sb("minus_half", [128, RJ])
        eps_ln = sb("eps_ln", [128, RJ])
        spare = sb("spare", [128, 1])
        gT = sb("gT", [FC, 2, NX])
        bT = sb("bT", [FC, 2, NX])
        b1T = sb("b1T", [128, HC, NX])

        phase_a = ExitStack()
        ctx.enter_context(phase_a)
        xin = sbp(phase_a, "xin", [HP, 2, PD])
        xT = sbp(phase_a, "xT", [128, KC, TOK])
        h = sbp(phase_a, "h", [TT, 2, EMB])
        hb = sbp(phase_a, "hb", [TT, 2, EMB])
        st1 = sbp(phase_a, "st1", [TT, 2, 6])
        mv1 = sbp(phase_a, "mv1", [TT, 2, 2])
        ve1 = sbp(phase_a, "ve1", [TT, 2])
        rs1 = sbp(phase_a, "rs1", [TT, 2])
        xn1 = sbp(phase_a, "xn1", [TT, 2, EMB])
        xn1T = sbp(phase_a, "xn1T", [FC, 2, TOK])
        qkT = sbp(phase_a, "qkT", [128, 2, GROUPS, TOK])
        vaug = sbp(phase_a, "vaug", [TT, 2, HEADS + WIN - 1, HS + 1])
        S = sbp(phase_a, "S", [TT, HEADS, CAUS])
        mx = sbp(phase_a, "mx", [TT, 2, HEADS])
        PT = sbp(phase_a, "PT", [TT, HEADS, CAUS])
        rden = sbp(phase_a, "rden", [TT, 2, HEADS])
        on = sbp(phase_a, "on", [TT, 2, EMB])
        onT = sbp(phase_a, "onT", [FC, 2, TOK])
        h2 = sbp(phase_a, "h2", [TT, 2, EMB])
        st2 = sbp(phase_a, "st2", [TT, 2, 6])
        mv2 = sbp(phase_a, "mv2", [TT, 2, 2])
        ve2 = sbp(phase_a, "ve2", [TT, 2])
        rs2 = sbp(phase_a, "rs2", [TT, 2])
        xn2 = sbp(phase_a, "xn2", [TT, 2, EMB + 1])
        xn2T = sbp(phase_a, "xn2T", [FC, 2, TOK])
        LT = sbp(phase_a, "LT", [128, SJ, TOK])
        slot_max = sbp(phase_a, "slot_max", [128, SJ])
        tok_part = sbp(phase_a, "tok_part", [128, TOK])
        tok_max = sbp(phase_a, "tok_max", [TT, 2])
        tok_bc = sbp(phase_a, "tok_bc", [128, TOK])
        tok_diag = sbp(phase_a, "tok_diag", [TT, 2, TT])
        Td = sbp(phase_a, "Td", [128, SJ, TOK])
        CT = sbp(phase_a, "CT", [128, SJ, TOK])
        E = sbp(phase_a, "E", [TT, 2, SLOTS])
        rz = sbp(phase_a, "rz", [128, SJ])
        xs = sbp(phase_a, "xs", [128, SJ, EMB])

        DMA_LOADS = sem("setup_loaded")

        wraw = S[0:FC, :, :].rearrange("p a c -> p (a c)")[:, 0:2 * PD].rearrange("p (h f) -> p h f", h=2)
        wre = PT[0:FC, :, :].rearrange("p a c -> p (a c)")[:, 0:2 * PD].rearrange("p (h f) -> p h f", h=2)
        phin = LT[:, :, :].rearrange("p a c -> p (a c)")[:, 0:SJ * EMB].rearrange("p (j d) -> p j d", j=SJ)
        phisq = Td[:, :, :].rearrange("p a c -> p (a c)")[:, 0:SJ * EMB].rearrange("p (j d) -> p j d", j=SJ)
        phirs = CT[:, :, :].rearrange("p a c -> p (a c)")[:, 0:SJ * EMB].rearrange("p (j d) -> p j d", j=SJ)
        phihalf = xs[:, :, :]
        parity2 = rz[:, 0:2]
        parity = tok_part[:, 0:128]
        posadd = xn1[:, :, :]
        graw = E[0:NX, 0, 0:EMB]
        braw = E[0:NX, 0, EMB:2 * EMB]
        b1raw = E[0:NX, 1, 0:HID]

        s_memset = sem("setup_memset")
        s_ident = sem("setup_ident")
        s_maskset = sem("setup_maskset")
        s_reorder = sem("setup_reorder")
        s_phisq = sem("setup_phisq")
        s_par2 = sem("setup_parity2")
        s_par = sem("setup_parity")
        s_phisum = sem("setup_phisum")
        s_phieps = sem("setup_phieps")
        s_phipow = sem("setup_phipow")
        s_newton = sem("setup_newton")
        s_phin = sem("setup_phin")
        s_sT = sem("setup_transposed")
        s_sE = sem("setup_evacuated")
        s_posb = sem("setup_posb")
        N_LOADS = 0
        with nc.Block() as blk:
            loads = [
                (wraw, W.rearrange("(h p) f -> p h f", p=FC)),
                (watt[:, :, :], W_attn.rearrange("(h p) f -> p h f", p=FC)),
                (wproj[:, :, :], W_proj.rearrange("(h p) f -> p h f", p=FC)),
                (phin, phi.rearrange("n p d -> (n p) d").rearrange("(q j) d -> q j d", j=SJ)),
                (graw, ln_g), (braw, ln_b), (b1raw, b1),
                (bv[:, :], b_attn[2 * EMB:3 * EMB].partition_broadcast(TT)),
                (bproj[:, :], b_proj.partition_broadcast(TT)),
                (posb[1:TT, 0, :], pos_embed[0, 0:TT - 1, :]),
                (posb[:, 1, :], pos_embed[0, TT - 1:TOK - 1, :]),
                (posadd[0:1, 0, :], cls_tok[0]),
                (posadd[1:2, 0, :], cls_token[0]),
                (posadd[2:TT, 0, :], b.partition_broadcast(TT - 2)),
                (posadd[:, 1, :], b.partition_broadcast(TT)),
            ]
            for g in range(HG):
                for qk in range(2):
                    src = b_attn[qk * EMB:(qk + 1) * EMB].rearrange("(j g r) -> g r j", g=HG, r=HS)[g]
                    loads.append((bqk[32 * g:32 * g + HS, qk, :], src))
            N_LOADS = len(loads)

            @blk.sync
            def _(sp):
                sp.wait_ge(s_memset, 2)
                for dst, src in loads:
                    sp.dma_start(dst, src).then_inc(DMA_LOADS, 16)

            @blk.gpsimd
            def _(pool):
                pool.memset(posb[:, :, :], 0.0).then_inc(s_memset, 1)
                pool.memset(bqk[:, :, :], 0.0).then_inc(s_memset, 1)
                pool.memset(ident[:, :], 0.0).then_inc(s_memset, 1)
                pool.wait_ge(s_memset, 3)
                pool.affine_select(out=ident[:, :], in_=ident[:, :], compare_op=ALU.not_equal, fill=1.0,
                                   base=0, pattern=[[-1, 128]], channel_multiplier=1).then_inc(s_ident, 1)
                pool.memset(ones[:, :], 1.0).then_inc(s_memset, 1)
                pool.memset(minus_half[:, :], -0.5).then_inc(s_memset, 1)
                pool.memset(eps_ln[:, :], EPS).then_inc(s_memset, 1)
                pool.memset(mask[:, :], 0.0).then_inc(s_memset, 1)
                pool.wait_ge(s_memset, 7)
                for c in (0, 2):
                    m = mask[:, c * TT:(c + 1) * TT]
                    pool.affine_select(out=m, in_=m, compare_op=ALU.is_ge, fill=NEG, base=0,
                                       pattern=[[-1, TT]], channel_multiplier=1).then_inc(s_maskset, 1)

            @blk.vector
            def _(dve):
                dve.memset(wqk[:, :, :, :, :, :], 0.0).then_inc(s_reorder, 1)
                for k in range(KC):
                    dve.memset(xT[:, k, 0:2], 0.0)
                dve.memset(vaug[:, :, 0:HEADS, :], 1.0)
                dve.memset(vaug[:, :, HEADS:, :], 0.0)
                dve.memset(xn2[:, :, :], 1.0)
                dve.wait_ge(s_ident, 1)
                dve.tensor_reduce(parity2, ident[:, :].rearrange("p (a c) -> p c a", c=2), AX.X,
                                  ALU.add).then_inc(s_par2, 1)
                dve.wait_ge(s_par2, 1)
                dve.tensor_copy(parity.rearrange("p (a c) -> p a c", c=2),
                                parity2.unsqueeze(1).broadcast_to([128, 64, 2])).then_inc(s_par, 1)
                dve.wait_ge(DMA_LOADS, 16 * N_LOADS)
                for hh in range(2):
                    dve.tensor_copy(wre[:, hh, :].rearrange("p (a b c) -> p a b c", a=PATCH, b=PATCH),
                                    wraw[:, hh, :].rearrange("p (c a b) -> p a b c", a=PATCH, b=PATCH)
                                    ).then_inc(s_reorder, 1)
                dve.wait_ge(s_reorder, 1)
                for hh in range(2):
                    for qk in range(2):
                        dve.tensor_copy(wqk[:, hh, qk, :, :, 0:HS],
                                        watt[:, hh, qk * EMB:(qk + 1) * EMB].rearrange(
                                            "p (j g r) -> p j g r", j=GROUPS, g=HG)).then_inc(s_reorder, 1)
                dve.tensor_tensor(posb[:, :, :], posb[:, :, :], posadd, ALU.add).then_inc(s_posb, 1)
                dve.tensor_tensor(phisq, phin, phin, ALU.mult).then_inc(s_phisq, 1)
                dve.wait_ge(s_phisum, 1)
                dve.tensor_scalar(phirs, ps[:, 0:4, 0:2 * EMB].rearrange("p k (j d) -> p k j d", j=2),
                                  EPS_NORM, None, ALU.add).then_inc(s_phieps, 1)
                dve.wait_ge(s_phipow, 1)
                dve.reciprocal(phihalf, phihalf).then_inc(s_newton, 1)
                dve.wait_ge(s_newton, 1)
                dve.tensor_tensor(phisq, phihalf, phihalf, ALU.mult).then_inc(s_newton, 1)
                dve.wait_ge(s_newton, 2)
                dve.scalar_tensor_tensor(out=phisq, in0=phisq, scalar=-0.5, in1=phirs, op0=ALU.mult,
                                         op1=ALU.mult).then_inc(s_newton, 1)
                dve.wait_ge(s_newton, 3)
                dve.scalar_tensor_tensor(out=phihalf, in0=phisq, scalar=1.5, in1=phihalf, op0=ALU.add,
                                         op1=ALU.mult).then_inc(s_newton, 1)
                dve.wait_ge(s_newton, 4)
                dve.tensor_tensor(phin, phin, phihalf, ALU.mult).then_inc(s_phin, 1)
                dve.wait_ge(s_sT, 1)
                dve.tensor_copy(WT[:, :, :], ps[:, 4:7, 0:2 * EMB].rearrange("p k (c e) -> p k c e", c=2)
                                ).then_inc(s_sE, 1)
                dve.wait_ge(s_sT, 2)
                dve.tensor_copy(gT[:, :, :], ps[0:FC, 7, 0:2 * NX].rearrange("p (c n) -> p c n", c=2))
                dve.tensor_copy(bT[:, :, :], ps[0:FC, 7, 2 * NX:4 * NX].rearrange("p (c n) -> p c n", c=2))
                dve.tensor_copy(b1T[:, :, :], ps[:, 7, 4 * NX:7 * NX].rearrange("p (c n) -> p c n", c=HC)
                                ).then_inc(s_sE, 1)
                dve.wait_ge(s_sT, 3)
                dve.tensor_copy(phiT[:, :, :, :], ps[0:FC, 0:4, :].rearrange("p k n -> p (k n)")
                                ).then_inc(s_sE, 1)

            @blk.scalar
            def _(act):
                act.wait_ge(s_phieps, 1)
                act.activation(phihalf, phirs, ACT.Sqrt).then_inc(s_phipow, 1)

            @blk.tensor
            def _(pe):
                pe.wait_ge(DMA_LOADS, 16 * N_LOADS)
                pe.wait_ge(s_ident, 1)
                pe.wait_ge(s_reorder, 3)
                for k in range(KC):
                    for hh in range(2):
                        mm = pe.transpose(ps[:, 4 + k // 2, (k % 2) * EMB + hh * FC:(k % 2) * EMB + (hh + 1) * FC],
                                          wre[:, hh, k * 128:(k + 1) * 128], ident[0:FC, 0:FC])
                mm.then_inc(s_sT, 1)
                for n, (src, parts, width) in enumerate(
                        [(graw[:, 0:FC], FC, 0), (graw[:, FC:], FC, 0), (braw[:, 0:FC], FC, 0), (braw[:, FC:], FC, 0)]
                        + [(b1raw[:, c * 128:(c + 1) * 128], 128, 0) for c in range(HC)]):
                    mm = pe.transpose(ps[0:parts, 7, n * NX:(n + 1) * NX], src, ident[0:NX, 0:NX])
                mm.then_inc(s_sT, 1)
                pe.wait_ge(s_par, 1)
                pe.wait_ge(s_phisq, 1)
                for k in range(4):
                    mm = pe.matmul(ps[:, k, 0:2 * EMB], parity, phisq[:, 2 * k:2 * k + 2, :],
                                   start=True, stop=True)
                mm.then_inc(s_phisum, 1)
                pe.wait_ge(s_phin, 1)
                pe.wait_ge(s_phieps, 1)
                for hh in range(2):
                    for j in range(SJ):
                        k = hh * SJ + j
                        mm = pe.transpose(ps[0:FC, k // 4, (k % 4) * 128:(k % 4 + 1) * 128],
                                          phin[:, j, hh * FC:(hh + 1) * FC], ident[:, :])
                mm.then_inc(s_sT, 1)

        x_loaded = sem("x_loaded")
        xT_ready = sem("xT_ready")
        xT_copied = sem("xT_copied")
        Z_ready = sem("Z_ready")
        h_ready = sem("h_ready")
        hb_ready = sem("hb_ready")
        st1_ready = sem("st1_ready")
        mv1_ready = sem("mv1_ready")
        ve1_ready = sem("ve1_ready")
        rs1_ready = sem("rs1_ready")
        xn1_ready = sem("xn1_ready")
        xn1T_ready = sem("xn1T_ready")
        xn1T_copied = sem("xn1T_copied")
        qk_ready = sem("qk_ready")
        qk_copied = sem("qk_copied")
        v_ready = sem("v_ready")
        v_copied = sem("v_copied")
        S_ready = sem("S_ready")
        S_masked = sem("S_masked")
        mx_ready = sem("mx_ready")
        S_shifted = sem("S_shifted")
        P_ready = sem("P_ready")
        PT_ready = sem("PT_ready")
        PT_copied = sem("PT_copied")
        O_ready = sem("O_ready")
        rden_ready = sem("rden_ready")
        on_ready = sem("on_ready")
        onT_ready = sem("onT_ready")
        onT_copied = sem("onT_copied")
        proj_ready = sem("proj_ready")
        h2_ready = sem("h2_ready")
        h2_stored = sem("h2_stored")
        st2_ready = sem("st2_ready")
        mv2_ready = sem("mv2_ready")
        ve2_ready = sem("ve2_ready")
        rs2_ready = sem("rs2_ready")
        xn2_ready = sem("xn2_ready")
        xn2T_ready = sem("xn2T_ready")
        xn2T_copied = sem("xn2T_copied")
        LT_ready = sem("LT_ready")
        LT_copied = sem("LT_copied")
        smax_ready = sem("smax_ready")
        tpart_ready = sem("tpart_ready")
        tpartT_ready = sem("tpartT_ready")
        tmax_ready = sem("tmax_ready")
        tdiag_ready = sem("tdiag_ready")
        tbc_ready = sem("tbc_ready")
        tbc_copied = sem("tbc_copied")
        U_ready = sem("U_ready")
        CT_ready = sem("CT_ready")
        CT_stored = sem("CT_stored")
        Td_ready = sem("Td_ready")
        TdT_ready = sem("TdT_ready")
        E_ready = sem("E_ready")
        Xs_ready = sem("Xs_ready")
        rz_ready = sem("rz_ready")
        xs_ready = sem("xs_ready")
        xs_stored = sem("xs_stored")

        def seg(bank, width=TOK):
            return ps[:, bank, 0:2 * width].rearrange("p (c t) -> p c t", c=2)

        class pe_att:
            @staticmethod
            def patches(pe, i):
                pe.wait_ge(x_loaded, (i + 1) * (16 * SIDE))
                wait_past(pe, E_ready, i - 1)
                for k in range(KC):
                    for t in range(2):
                        mm = pe.transpose(ps[:, 4 + k // 2, (k % 2) * NPATCH + t * HP:(k % 2) * NPATCH + (t + 1) * HP],
                                          xin[:, t, k * 128:(k + 1) * 128], ident[0:HP, 0:HP])
                mm.then_inc(xT_ready, 1)

            @staticmethod
            def embed(pe, i):
                pe.wait_ge(xT_copied, i + 1)
                for t in range(2):
                    for k in range(KC):
                        mm = pe.matmul(ps[0:TT, 7, t * EMB:(t + 1) * EMB], xT[:, k, t * TT:(t + 1) * TT],
                                       WT[:, k, :], start=(k == 0), stop=(k == KC - 1))
                mm.then_inc(Z_ready, 1)

            @staticmethod
            def turn(pe, i, src, bank, ready, done):
                pe.wait_ge(ready, i + 1)
                for t in range(2):
                    for c in range(2):
                        mm = pe.transpose(ps[0:FC, bank, c * TOK + t * TT:c * TOK + (t + 1) * TT],
                                          src[:, t, c * FC:(c + 1) * FC], ident[0:TT, 0:TT])
                mm.then_inc(done, 1)

            @staticmethod
            def qkv(pe, i):
                pe.wait_ge(xn1T_copied, i + 1)
                for n in range(2 * GROUPS):
                    for c in range(2):
                        mm = pe.matmul(ps[:, 1 + n // 2, (n % 2) * TOK:(n % 2 + 1) * TOK],
                                       wqk[:, c, n // GROUPS, n % GROUPS, :, :], xn1T[:, c, :],
                                       start=(c == 0), stop=(c == 1))
                mm.then_inc(qk_ready, 1)
                for t in range(2):
                    for c in range(2):
                        mm = pe.matmul(ps[0:TT, 0, t * EMB:(t + 1) * EMB], xn1T[:, c, t * TT:(t + 1) * TT],
                                       watt[:, c, 2 * EMB:3 * EMB], start=(c == 0), stop=(c == 1))
                mm.then_inc(v_ready, 1)

            @staticmethod
            def scores(pe, i, j):
                if j == 0:
                    pe.wait_ge(qk_copied, i + 1)
                    pe.wait_ge(v_copied, i + 1)
                else:
                    pe.wait_ge(S_masked, i * GROUPS + j)
                for t in range(2):
                    for g in range(HG):
                        q = qkT[32 * g:32 * g + HS, 0, j, t * TT:(t + 1) * TT]
                        kk = qkT[32 * g:32 * g + HS, 1, j, 0:(t + 1) * TT]
                        mm = pe.matmul(ps[0:TT, g, t * TT:t * TT + (t + 1) * TT], q, kk, start=True, stop=True)
                mm.then_inc(S_ready, 1)

            @staticmethod
            def probs_turn(pe, i, j):
                pe.wait_ge(P_ready, i * GROUPS + j + 1)
                if j == 0:
                    pe.wait_ge(S_masked, (i + 1) * GROUPS)
                else:
                    pe.wait_ge(PT_copied, i * GROUPS + j)
                for g in range(HG):
                    for c in range(3):
                        mm = pe.transpose(ps[0:TT, g, c * TT:(c + 1) * TT],
                                          S[:, HG * j + g, c * TT:(c + 1) * TT], ident[0:TT, 0:TT])
                mm.then_inc(PT_ready, 1)

            @staticmethod
            def weigh(pe, i):
                pe.wait_ge(PT_copied, (i + 1) * GROUPS)
                W1 = HS + 1
                for n in range(HEADS):
                    for t in range(2):
                        o = ps[0:TT, t, n * W1:(n + WIN) * W1]
                        for kt in range(t + 1):
                            mm = pe.matmul(o, PT[:, n, (t + kt) * TT:(t + kt + 1) * TT], vaug[:, kt, n:n + WIN, :],
                                           start=(kt == 0), stop=(kt == t))
                mm.then_inc(O_ready, 1)

            @staticmethod
            def proj(pe, i):
                pe.wait_ge(onT_copied, i + 1)
                for t in range(2):
                    for c in range(2):
                        mm = pe.matmul(ps[0:TT, 3, t * EMB:(t + 1) * EMB], onT[:, c, t * TT:(t + 1) * TT],
                                       wproj[:, c, :], start=(c == 0), stop=(c == 1))
                mm.then_inc(proj_ready, 1)

        class act_att:
            @staticmethod
            def patches(act, i):
                act.wait_ge(xT_ready, i + 1)
                wait_past(act, Z_ready, i)
                for k in range(3):
                    cp = act.activation(xT[:, 2 * k:2 * k + 2, 2:TOK], seg(4 + k, NPATCH), ACT.Copy)
                cp.then_inc(xT_copied, 1)

            @staticmethod
            def turn(act, i, dst, bank, ready, done, free=None):
                act.wait_ge(ready, i + 1)
                if free is not None:
                    wait_past(act, free, i)
                act.activation(dst[:, :, :], ps[0:FC, bank, 0:2 * TOK].rearrange("p (c t) -> p c t", c=2),
                               ACT.Copy).then_inc(done, 1)

            @staticmethod
            def qk(act, i):
                act.wait_ge(qk_ready, i + 1)
                wait_past(act, S_ready, i * GROUPS)
                for n in range(2 * GROUPS):
                    cp = act.activation(qkT[:, n // GROUPS, n % GROUPS, :],
                                        ps[:, 1 + n // 2, (n % 2) * TOK:(n % 2 + 1) * TOK], ACT.Identity,
                                        bias=bqk[:, n // GROUPS, n % GROUPS:n % GROUPS + 1])
                cp.then_inc(qk_copied, 1)

            @staticmethod
            def probs(act, i, j):
                act.wait_ge(S_shifted, i * GROUPS + j + 1)
                s = S[:, HG * j:HG * (j + 1), :]
                act.activation(s, s, ACT.Exp).then_inc(P_ready, 1)

            @staticmethod
            def probs_turn(act, i, j):
                act.wait_ge(PT_ready, i * GROUPS + j + 1)
                if j == 0:
                    wait_past(act, O_ready, i)
                act.activation(PT[:, HG * j:HG * (j + 1), :], ps[0:TT, 0:HG, 0:CAUS],
                               ACT.Copy).then_inc(PT_copied, 1)

        def layernorm_stats(dve, i, src, st, mv, src_ready, st_ready, mv_ready):
            dve.wait_ge(src_ready, i + 1)
            for t in range(2):
                s_ = dve.bn_stats(st[:, t, :], src[:, t, :])
            s_.then_inc(st_ready, 1)
            dve.wait_ge(st_ready, i + 1)
            dve.memset(spare[:, :], 0.0)
            for t in range(2):
                s_ = dve.bn_aggr(mv[:, t, :], st[:, t, :])
            s_.then_inc(mv_ready, 1)

        class dve_att:
            @staticmethod
            def embed(dve, i):
                dve.wait_ge(Z_ready, i + 1)
                wait_past(dve, hb_ready, i)
                dve.tensor_tensor(h[:, :, :], ps[0:TT, 7, 0:2 * EMB].rearrange("p (t e) -> p t e", t=2),
                                  posb[:, :, :], ALU.add).then_inc(h_ready, 1)
                layernorm_stats(dve, i, h, st1, mv1, h_ready, st1_ready, mv1_ready)

            @staticmethod
            def norm1(dve, i):
                dve.wait_ge(rs1_ready, i + 1)
                wait_past(dve, xn1T_ready, i)
                for t in range(2):
                    s_ = dve.tensor_scalar(xn1[:, t, :], h[:, t, :], mv1[:, t, 0:1], rs1[:, t:t + 1],
                                           ALU.subtract, ALU.mult)
                s_.then_inc(xn1_ready, 1)

            @staticmethod
            def v(dve, i):
                dve.wait_ge(v_ready, i + 1)
                wait_past(dve, O_ready, i)
                for t in range(2):
                    s_ = dve.tensor_tensor(vaug[:, t, 0:HEADS, 0:HS],
                                           ps[0:TT, 0, t * EMB:(t + 1) * EMB].rearrange("p (n r) -> p n r", r=HS),
                                           bv[:, :].rearrange("p (n r) -> p n r", r=HS), ALU.add)
                s_.then_inc(v_copied, 1)

            @staticmethod
            def softmax(dve, i, j):
                n = i * GROUPS + j + 1
                s = S[:, HG * j:HG * (j + 1), :]
                dve.wait_ge(S_ready, n)
                wait_past(dve, PT_ready, i * GROUPS)
                dve.scalar_tensor_tensor(out=s, in0=ps[0:TT, 0:HG, 0:CAUS], scalar=SCALE,
                                         in1=mask[:, :].unsqueeze(1).broadcast_to([TT, HG, CAUS]),
                                         op0=ALU.mult, op1=ALU.add).then_inc(S_masked, 1)
                dve.wait_ge(S_masked, n)
                for t in range(2):
                    m = dve.tensor_reduce(mx[:, t, HG * j:HG * (j + 1)], s[:, :, t * TT:(2 * t + 1) * TT], AX.X,
                                          ALU.max)
                m.then_inc(mx_ready, 1)
                dve.wait_ge(mx_ready, n)
                for t in range(2):
                    w = (t + 1) * TT
                    sh = dve.tensor_tensor(s[:, :, t * TT:t * TT + w], s[:, :, t * TT:t * TT + w],
                                           mx[:, t, HG * j:HG * (j + 1)].unsqueeze(2).broadcast_to([TT, HG, w]),
                                           ALU.subtract)
                sh.then_inc(S_shifted, 1)

            @staticmethod
            def weigh(dve, i):
                dve.wait_ge(O_ready, i + 1)
                o = ps[0:TT, 0:2, 0:HEADS * (HS + 1)].rearrange("p t (n r) -> p t n r", n=HEADS)
                dve.reciprocal(rden[:, :, :], o[:, :, :, HS]).then_inc(rden_ready, 1)
                dve.wait_ge(rden_ready, i + 1)
                wait_past(dve, onT_ready, i)
                for t in range(2):
                    m = dve.tensor_tensor(on[:, t, :].rearrange("p (n r) -> p n r", r=HS), o[:, t, :, 0:HS],
                                          rden[:, t, :].unsqueeze(2).broadcast_to([TT, HEADS, HS]), ALU.mult)
                m.then_inc(on_ready, 1)

            @staticmethod
            def resid(dve, i):
                dve.wait_ge(proj_ready, i + 1)
                dve.wait_ge(hb_ready, i + 1)
                wait_past(dve, h2_stored, i * 16)
                dve.tensor_tensor(h2[:, :, :], ps[0:TT, 3, 0:2 * EMB].rearrange("p (t e) -> p t e", t=2),
                                  hb[:, :, :], ALU.add).then_inc(h2_ready, 1)
                layernorm_stats(dve, i, h2, st2, mv2, h2_ready, st2_ready, mv2_ready)

            @staticmethod
            def norm2(dve, i):
                dve.wait_ge(rs2_ready, i + 1)
                wait_past(dve, Xs_ready, i * 4)
                for t in range(2):
                    s_ = dve.tensor_scalar(xn2[:, t, 0:EMB], h2[:, t, :], mv2[:, t, 0:1], rs2[:, t:t + 1],
                                           ALU.subtract, ALU.mult)
                s_.then_inc(xn2_ready, 1)

        def pool_rstd(pool, i, mv, ve, rs, mv_ready, ve_ready, rs_ready, reader):
            pool.wait_ge(mv_ready, i + 1)
            pool.tensor_tensor(ve[:, :], mv[:, :, 1], eps_ln[0:TT, 0:2], ALU.add).then_inc(ve_ready, 1)
            pool.wait_ge(ve_ready, i + 1)
            wait_past(pool, reader, i)
            pool.tensor_tensor(rs[:, :], ve[:, :], minus_half[0:TT, 0:2], ALU.pow).then_inc(rs_ready, 1)

        class pe_moe:
            @staticmethod
            def logits(pe, i, k, patched):
                if k == 0:
                    pe.wait_ge(xn2T_copied, i + 1)
                    wait_past(pe, xs_ready, i * 4)
                    wait_past(pe, tbc_copied, i)
                    pe.wait_ge(h_ready, patched)
                for j in (2 * k, 2 * k + 1):
                    for c in range(2):
                        mm = pe.matmul(ps[:, 4 + k, (j % 2) * TOK:(j % 2 + 1) * TOK], phiT[:, c, j, :],
                                       xn2T[:, c, :], start=(c == 0), stop=(c == 1))
                mm.then_inc(LT_ready, 1)

            @staticmethod
            def tokmax_turn(pe, i, patched):
                pe.wait_ge(tpart_ready, i + 1)
                pe.wait_ge(xT_copied, patched)
                for t in range(2):
                    mm = pe.transpose(ps[0:TT, 6, t * 128:(t + 1) * 128], tok_part[:, t * TT:(t + 1) * TT],
                                      ident[:, :])
                mm.then_inc(tpartT_ready, 1)

            @staticmethod
            def tokmax_spread(pe, i):
                pe.wait_ge(tdiag_ready, i + 1)
                for t in range(2):
                    mm = pe.matmul(ps[:, 6, 256 + t * TT:256 + (t + 1) * TT], ones[:, :], tok_diag[:, t, :],
                                   start=True, stop=True)
                mm.then_inc(tbc_ready, 1)

            @staticmethod
            def shifted_turn(pe, i):
                pe.wait_ge(Td_ready, i + 1)
                pe.wait_ge(LT_copied, (i + 1) * 4)
                for t in range(2):
                    for j in range(SJ):
                        mm = pe.transpose(ps[0:TT, 4 + 2 * t + j // 4, (j % 4) * 128:(j % 4 + 1) * 128],
                                          Td[:, j, t * TT:(t + 1) * TT], ident[:, :])
                mm.then_inc(TdT_ready, 1)

            @staticmethod
            def dispatch(pe, i, k, patched):
                pe.wait_ge(E_ready, i + 1)
                if k < 2:
                    pe.wait_ge(xT_copied, patched)
                else:
                    pe.wait_ge(xs_ready, i * 4 + k - 1)
                for j in (2 * k, 2 * k + 1):
                    for t in range(2):
                        mm = pe.matmul(ps[:, 4 + k % 2, (j % 2) * (EMB + 1):(j % 2 + 1) * (EMB + 1)],
                                       E[:, t, j * 128:(j + 1) * 128], xn2[:, t, :],
                                       start=(t == 0), stop=(t == 1))
                mm.then_inc(Xs_ready, 1)

        class act_moe:
            @staticmethod
            def logits(act, i, k):
                act.wait_ge(LT_ready, i * 4 + k + 1)
                if k == 0:
                    wait_past(act, U_ready, i)
                    wait_past(act, tpart_ready, i)
                act.activation(LT[:, 2 * k:2 * k + 2, :], seg(4 + k), ACT.Copy).then_inc(LT_copied, 1)

            @staticmethod
            def spread(act, i):
                act.wait_ge(tbc_ready, i + 1)
                wait_past(act, U_ready, i)
                act.activation(tok_bc[:, :], ps[:, 6, 256:256 + TOK], ACT.Copy).then_inc(tbc_copied, 1)

            @staticmethod
            def combine(act, i):
                act.wait_ge(U_ready, i + 1)
                act.activation(CT[:, :, :], CT[:, :, :], ACT.Exp).then_inc(CT_ready, 1)

            @staticmethod
            def dispatch(act, i):
                act.wait_ge(TdT_ready, i + 1)
                wait_past(act, Xs_ready, i * 4)
                act.activation(E[:, :, :], ps[0:TT, 4:8, :].rearrange("p (t k) n -> p t (k n)", t=2),
                               ACT.Exp).then_inc(E_ready, 1)

        class dve_moe:
            @staticmethod
            def slotmax(dve, i):
                dve.wait_ge(LT_copied, (i + 1) * 4)
                dve.tensor_reduce(slot_max[:, :], LT[:, :, :], AX.X, ALU.max).then_inc(smax_ready, 1)

            @staticmethod
            def tokpart(dve, i):
                wait_past(dve, tpartT_ready, i)
                dve.tensor_reduce(tok_part[:, :], LT[:, :, :].rearrange("p j t -> p t j"), AX.X,
                                  ALU.max).then_inc(tpart_ready, 1)

            @staticmethod
            def shift(dve, i):
                dve.wait_ge(smax_ready, i + 1)
                wait_past(dve, TdT_ready, i)
                dve.tensor_tensor(Td[:, :, :], LT[:, :, :],
                                  slot_max[:, :].unsqueeze(2).broadcast_to([128, SJ, TOK]),
                                  ALU.subtract).then_inc(Td_ready, 1)

            @staticmethod
            def tokmax(dve, i):
                dve.wait_ge(tpartT_ready, i + 1)
                dve.tensor_reduce(tok_max[:, :], ps[0:TT, 6, 0:256].rearrange("p (t n) -> p t n", t=2), AX.X,
                                  ALU.max).then_inc(tmax_ready, 1)
                dve.wait_ge(tmax_ready, i + 1)
                for t in range(2):
                    d = dve.tensor_scalar(tok_diag[:, t, :], ident[0:TT, 0:TT], tok_max[:, t:t + 1], None,
                                          ALU.mult)
                d.then_inc(tdiag_ready, 1)

            @staticmethod
            def dispatch(dve, i, k):
                n = i * 4 + k + 1
                o = seg(4 + k % 2, EMB + 1)
                dve.wait_ge(Xs_ready, n)
                dve.reciprocal(rz[:, 2 * k:2 * k + 2], o[:, :, EMB]).then_inc(rz_ready, 1)
                dve.wait_ge(rz_ready, n)
                if k == 0:
                    wait_past(dve, xs_stored, i * 16)
                dve.tensor_tensor(xs[:, 2 * k:2 * k + 2, :], o[:, :, 0:EMB],
                                  rz[:, 2 * k:2 * k + 2].unsqueeze(2).broadcast_to([128, 2, EMB]),
                                  ALU.mult).then_inc(xs_ready, 1)

        def load_x(sp, i):
            for r in range(SIDE):
                src = x[i, r * PATCH:(r + 1) * PATCH, :, :].rearrange(
                    "a (j b) c -> j a (b c)", j=SIDE)
                p0 = (r % HI) * SIDE
                dst = xin[p0:p0 + SIDE, r // HI, :].rearrange("p (a f) -> p a f", a=PATCH)
                sp.dma_start(dst, src).then_inc(x_loaded, 16)

        PE_ORDER = ["a.qkv", "m.dturn", "a.s0", "e.patches", "a.s1", "m.x0", "m.tokmax", "m.x1", "a.s2", "m.spread",
                    "a.p0", "a.p1", "m.x2", "a.p2", "m.x3", "a.weigh", "a.turno", "a.proj", "e.embed", "a.turn2",
                    "l.0", "l.1", "e.turn1", "l.2", "l.3"]
        ACT_ORDER = ["a.qkv", "m.dturn", "e.patches", "a.s0", "a.s1", "m.spread", "a.p0", "a.p1", "a.s2", "a.p2",
                     "m.combine", "a.turno", "a.turn2", "l.0", "l.1", "e.turn1", "l.2", "l.3"]
        DVE_ORDER = ["m.slotmax", "m.shift", "m.tokpart", "a.qkv", "a.s0", "a.s1", "m.tokmax", "a.s2", "m.x0", "m.x1",
                     "m.x2", "m.x3", "a.weigh", "a.proj", "a.turn2", "e.embed", "e.norm1"]

        def run_pe(pe, i, parts):
            for s in PE_ORDER:
                if s[0] not in parts:
                    continue
                if s == "e.patches":
                    pe_att.patches(pe, i + 1)
                elif s == "e.embed":
                    pe_att.embed(pe, i + 1)
                elif s == "e.turn1":
                    pe_att.turn(pe, i + 1, xn1, 1, xn1_ready, xn1T_ready)
                elif s == "a.qkv":
                    pe_att.qkv(pe, i)
                elif s in ("a.s0", "a.s1", "a.s2"):
                    pe_att.scores(pe, i, int(s[3]))
                elif s in ("a.p0", "a.p1", "a.p2"):
                    pe_att.probs_turn(pe, i, int(s[3]))
                elif s == "a.weigh":
                    pe_att.weigh(pe, i)
                elif s == "a.turno":
                    pe_att.turn(pe, i, on, 2, on_ready, onT_ready)
                elif s == "a.proj":
                    pe_att.proj(pe, i)
                elif s == "a.turn2":
                    pe_att.turn(pe, i, xn2, 0, xn2_ready, xn2T_ready)
                elif s[0] == "l":
                    pe_moe.logits(pe, i, int(s[2]), i + 2 if "e" in parts else B)
                elif s == "m.tokmax":
                    pe_moe.tokmax_turn(pe, i - 1, i + 2 if "e" in parts else B)
                elif s == "m.spread":
                    pe_moe.tokmax_spread(pe, i - 1)
                elif s == "m.dturn":
                    pe_moe.shifted_turn(pe, i - 1)
                elif s[:3] == "m.x":
                    pe_moe.dispatch(pe, i - 1, int(s[3]), i + 2 if "e" in parts else B)

        def run_act(act, i, parts):
            for s in ACT_ORDER:
                if s[0] not in parts:
                    continue
                if s == "e.patches":
                    act_att.patches(act, i + 1)
                elif s == "e.turn1":
                    wait_past(act, v_ready, i + 1)
                    act_att.turn(act, i + 1, xn1T, 1, xn1T_ready, xn1T_copied)
                elif s == "a.qkv":
                    act_att.qk(act, i)
                elif s in ("a.s0", "a.s1", "a.s2"):
                    act_att.probs(act, i, int(s[3]))
                elif s in ("a.p0", "a.p1", "a.p2"):
                    act_att.probs_turn(act, i, int(s[3]))
                elif s == "a.turno":
                    wait_past(act, proj_ready, i)
                    act_att.turn(act, i, onT, 2, onT_ready, onT_copied)
                elif s == "a.turn2":
                    wait_past(act, LT_ready, i * 4)
                    act_att.turn(act, i, xn2T, 0, xn2T_ready, xn2T_copied)
                elif s[0] == "l":
                    act_moe.logits(act, i, int(s[2]))
                elif s == "m.spread":
                    act_moe.spread(act, i - 1)
                elif s == "m.combine":
                    act_moe.combine(act, i - 1)
                elif s == "m.dturn":
                    act_moe.dispatch(act, i - 1)

        def run_dve(dve, i, parts):
            for s in DVE_ORDER:
                if s[0] not in parts:
                    continue
                if s == "e.embed":
                    dve_att.embed(dve, i + 1)
                elif s == "e.norm1":
                    dve_att.norm1(dve, i + 1)
                elif s == "a.qkv":
                    dve_att.v(dve, i)
                elif s in ("a.s0", "a.s1", "a.s2"):
                    dve_att.softmax(dve, i, int(s[3]))
                elif s == "a.weigh":
                    dve_att.weigh(dve, i)
                elif s == "a.proj":
                    dve_att.resid(dve, i)
                elif s == "a.turn2":
                    dve_att.norm2(dve, i)
                elif s == "m.slotmax":
                    dve_moe.slotmax(dve, i - 1)
                elif s == "m.tokpart":
                    dve_moe.tokpart(dve, i - 1)
                elif s == "m.tokmax":
                    dve_moe.tokmax(dve, i - 1)
                elif s == "m.shift":
                    dve_moe.shift(dve, i - 1)
                elif s[:3] == "m.x":
                    dve_moe.dispatch(dve, i - 1, int(s[3]))

        def pool_combine(pool, i):
            pool.wait_ge(tbc_copied, i + 1)
            pool.wait_ge(LT_copied, (i + 1) * 4)
            wait_past(pool, CT_stored, i * 16)
            pool.tensor_tensor(CT[:, :, :], LT[:, :, :],
                               tok_bc[:, :].unsqueeze(1).broadcast_to([128, SJ, TOK]),
                               ALU.subtract).then_inc(U_ready, 1)

        def run_pool(pool, i, parts):
            if "m" in parts:
                pool_combine(pool, i - 1)
            if "a" in parts:
                pool_rstd(pool, i, mv2, ve2, rs2, mv2_ready, ve2_ready, rs2_ready, xn2_ready)
            if "e" in parts:
                pool_rstd(pool, i + 1, mv1, ve1, rs1, mv1_ready, ve1_ready, rs1_ready, xn1_ready)
                wait_past(pool, h2_ready, i + 1)
                pool.tensor_tensor(hb[:, :, :], h[:, :, :],
                                   bproj[:, :].unsqueeze(1).broadcast_to([TT, 2, EMB]),
                                   ALU.add).then_inc(hb_ready, 1)

        def run_sp(sp, i, parts, load=True):
            if load:
                sp.wait_ge(xT_ready, i + 2)
                load_x(sp, i + 2)
            if "m" in parts:
                wait_past(sp, CT_ready, i)
                sp.dma_start(ct_d[i - 1], CT[:, :, :].rearrange("p j t -> p (j t)")).then_inc(CT_stored, 16)
                wait_past(sp, xs_ready, i * 4)
                sp.dma_start(xs_d[:, i - 1, :, :].rearrange("n (a j) d -> n a (j d)", a=2),
                             xs[:, :, :].rearrange("q j d -> q (j d)")).then_inc(xs_stored, 16)
            if "a" in parts:
                sp.wait_ge(h2_ready, i + 1)
                sp.dma_start(h2_d[i], h2[:, :, :].rearrange("p t e -> p (t e)")).then_inc(h2_stored, 16)

        def all_turns(eng, run):
            run(eng, -1, "e")
            run(eng, 0, "ael")
            run(eng, 1, "amel")
            with eng.Fori(2, B - 1) as i:
                run(eng, i, "amel")
            run(eng, B - 1, "aml")
            run(eng, B, "m")

        with nc.Block() as blk:
            @blk.sync
            def _(sp):
                load_x(sp, 0)
                run_sp(sp, -1, "e")
                run_sp(sp, 0, "ael")
                run_sp(sp, 1, "amel")
                with sp.Fori(2, B - 2) as i:
                    run_sp(sp, i, "amel")
                run_sp(sp, B - 2, "amel", load=False)
                run_sp(sp, B - 1, "aml", load=False)
                run_sp(sp, B, "m", load=False)
                sp.wait_ge(xs_stored, B * 16)
                sp.wait_ge(CT_stored, B * 16)
                sp.wait_ge(h2_stored, B * 16)

            @blk.tensor
            def _(pe):
                all_turns(pe, run_pe)

            @blk.scalar
            def _(act):
                all_turns(act, run_act)

            @blk.vector
            def _(dve):
                all_turns(dve, run_dve)

            @blk.gpsimd
            def _(pool):
                all_turns(pool, run_pool)

        phase_a.close()
        phase_b = ExitStack()
        ctx.enter_context(phase_b)
        ein = [sbp(phase_b, f"ein{u}", [128, RJ, EMB]) for u in range(2)]
        ew1 = [sbp(phase_b, f"ew1_{u}", [FC, 2, HID]) for u in range(2)]
        ew2 = [sbp(phase_b, f"ew2_{u}", [128, HC, EMB]) for u in range(2)]
        eb2 = [sbp(phase_b, f"eb2_{u}", [128, EMB]) for u in range(2)]
        col = [sbp(phase_b, f"ecol{u}", [128, 2 * 2 + HC]) for u in range(2)]
        est = sbp(phase_b, "est", [128, RJ, 6])
        emv = sbp(phase_b, "emv", [128, RJ, 2])
        eve = sbp(phase_b, "eve", [128, RJ])
        ers = sbp(phase_b, "ers", [128, RJ])
        ehn = sbp(phase_b, "ehn", [128, RJ, EMB])
        ehT = sbp(phase_b, "ehT", [FC, 2, ROWS])
        ys = sbp(phase_b, "ys", [128, RJ, EMB])
        hid = sbp(phase_b, "hid", [128, HC, ROWS])

        e_loaded = [sem(f"e_loaded{u}") for u in range(2)]
        w_loaded = [sem(f"w_loaded{u}") for u in range(2)]
        est_ready = sem("est_ready")
        emv_ready = sem("emv_ready")
        eve_ready = sem("eve_ready")
        ers_ready = sem("ers_ready")
        ehn_ready = sem("ehn_ready")
        ehT_ready = sem("ehT_ready")
        col_ready = sem("col_ready")
        ehT_copied = sem("ehT_copied")
        H_ready = sem("H_ready")
        H_copied = sem("H_copied")
        Y_ready = sem("Y_ready")
        Y_copied = sem("Y_copied")
        ys_stored = sem("ys_stored")
        NH = 2 * HC

        def load_rows(sp, n, u):
            wait_past(sp, ehn_ready, n - 1)
            sp.dma_start(ein[u][:, :, :].rearrange("r j d -> r (j d)"),
                         xs_d[n].rearrange("b p d -> (b p) d").rearrange("(r j) d -> r (j d)", j=RJ)
                         ).then_inc(e_loaded[u], 16)

        def load_weights(sp, n, u):
            wait_past(sp, Y_copied, (n - 1) * 4)
            sp.dma_start(ew1[u][:, :, :], w1[n].rearrange("(c p) f -> p c f", p=FC)).then_inc(w_loaded[u], 16)
            sp.dma_start(ew2[u][:, :, :], w2[n].rearrange("(c p) f -> p c f", p=128)).then_inc(w_loaded[u], 16)
            sp.dma_start(eb2[u][:, :], b2[n].partition_broadcast(128)).then_inc(w_loaded[u], 16)

        def store_expert(sp, n):
            sp.wait_ge(Y_copied, (n + 1) * 4)
            sp.dma_start(ys_d[n].rearrange("b p d -> (b p) d").rearrange("(r j) d -> r (j d)", j=RJ),
                         ys[:, :, :].rearrange("r j d -> r (j d)")).then_inc(ys_stored, 16)

        def run_sp_experts(sp, n, u, rows=True, weights=True):
            if rows:
                load_rows(sp, n + 2, u)
            if weights:
                load_weights(sp, n + 1, 1 - u)
            store_expert(sp, n)

        def expert_pre_dve(dve, n, u, k):
            dve.wait_ge(e_loaded[u], k * 16)
            for t in range(RJ):
                s_ = dve.bn_stats(est[:, t, :], ein[u][:, t, :])
            s_.then_inc(est_ready, 1)
            dve.wait_ge(est_ready, n + 1)
            dve.memset(spare[:, :], 0.0)
            for t in range(RJ):
                s_ = dve.bn_aggr(emv[:, t, :], est[:, t, :])
            s_.then_inc(emv_ready, 1)
            wait_past(dve, H_copied, (n - 1) * NH)
            dve.tensor_copy(col[u][0:FC, 0:2], gT[:, :, n])
            dve.tensor_copy(col[u][0:FC, 2:4], bT[:, :, n])
            dve.tensor_copy(col[u][:, 4:4 + HC], b1T[:, :, n]).then_inc(col_ready, 1)
            wait_past(dve, ehT_ready, n * 4)
            dve.wait_ge(ers_ready, n + 1)
            for t in range(RJ):
                s_ = dve.tensor_scalar(ehn[:, t, :], ein[u][:, t, :], emv[:, t, 0:1], ers[:, t:t + 1],
                                       ALU.subtract, ALU.mult)
            s_.then_inc(ehn_ready, 1)

        def expert_pre_pe(pe, n):
            pe.wait_ge(ehn_ready, n + 1)
            wait_past(pe, ehT_copied, n * 4)
            for c in range(2):
                for hh in range(2):
                    for t in range(4):
                        mm = pe.transpose(ps[0:FC, 2 * c + hh, t * 128:(t + 1) * 128],
                                          ehn[:, 4 * hh + t, c * FC:(c + 1) * FC], ident[:, :])
                    mm.then_inc(ehT_ready, 1)

        def expert_pre_act(act, n, u):
            act.wait_ge(col_ready, n + 1)
            wait_past(act, H_ready, n * NH)
            for c in range(2):
                for hh in range(2):
                    act.wait_ge(ehT_ready, n * 4 + 2 * c + hh + 1)
                    act.activation(ehT[:, c, hh * 512:(hh + 1) * 512], ps[0:FC, 2 * c + hh, :], ACT.Identity,
                                   bias=col[u][0:FC, 2 + c:3 + c], scale=col[u][0:FC, c:c + 1]
                                   ).then_inc(ehT_copied, 1)

        def expert_pe(pe, n, u, k):
            pe.wait_ge(w_loaded[u], k * 48)
            pe.wait_ge(ehT_copied, (n + 1) * 4)
            for m in range(NH):
                if m >= 2:
                    pe.wait_ge(H_copied, n * NH + m - 1)
                else:
                    wait_past(pe, H_copied, n * NH)
                for c in range(2):
                    mm = pe.matmul(ps[:, 4 + m % 2, :], ew1[u][:, c, (m // 2) * 128:(m // 2 + 1) * 128],
                                   ehT[:, c, (m % 2) * 512:(m % 2 + 1) * 512], start=(c == 0), stop=(c == 1))
                mm.then_inc(H_ready, 1)

        def expert_act(act, n, u):
            wait_past(act, Y_ready, n * 4)
            for m in range(NH):
                act.wait_ge(H_ready, n * NH + m + 1)
                act.activation(hid[:, m // 2, (m % 2) * 512:(m % 2 + 1) * 512], ps[:, 4 + m % 2, :], ACT.Gelu,
                               bias=col[u][:, 4 + m // 2:5 + m // 2]).then_inc(H_copied, 1)

        def expert_pe2(pe, n, u):
            pe.wait_ge(H_copied, (n + 1) * NH)
            for m in range(4):
                if m >= 2:
                    pe.wait_ge(Y_copied, n * 4 + m - 1)
                else:
                    wait_past(pe, Y_copied, n * 4)
                for t in (2 * m, 2 * m + 1):
                    for c in range(HC):
                        mm = pe.matmul(ps[:, 6 + m % 2, (t % 2) * EMB:(t % 2 + 1) * EMB],
                                       hid[:, c, t * 128:(t + 1) * 128], ew2[u][:, c, :],
                                       start=(c == 0), stop=(c == HC - 1))
                mm.then_inc(Y_ready, 1)

        def expert_dve(dve, n, u):
            wait_past(dve, ys_stored, n * 16)
            for m in range(4):
                dve.wait_ge(Y_ready, n * 4 + m + 1)
                dve.tensor_tensor(ys[:, 2 * m:2 * m + 2, :],
                                  ps[:, 6 + m % 2, 0:2 * EMB].rearrange("p (t e) -> p t e", t=2),
                                  eb2[u][:, :].unsqueeze(1).broadcast_to([128, 2, EMB]),
                                  ALU.add).then_inc(Y_copied, 1)

        with nc.Block() as blk:
            @blk.sync
            def _(sp):
                load_rows(sp, 0, 0)
                load_weights(sp, 0, 0)
                load_rows(sp, 1, 1)
                for u in range(2):
                    run_sp_experts(sp, u, u)
                with sp.Fori(1, NX // 2 - 1) as i:
                    for u in range(2):
                        run_sp_experts(sp, 2 * i + u, u)
                run_sp_experts(sp, NX - 2, 0, rows=False)
                run_sp_experts(sp, NX - 1, 1, rows=False, weights=False)
                sp.wait_ge(ys_stored, NX * 16)

            @blk.tensor
            def _(pe):
                expert_pre_pe(pe, 0)
                for u in range(2):
                    expert_pe(pe, u, u, 1)
                    expert_pre_pe(pe, u + 1)
                    expert_pe2(pe, u, u)
                with pe.Fori(1, NX // 2 - 1) as i:
                    for u in range(2):
                        expert_pe(pe, 2 * i + u, u, i + 1)
                        expert_pre_pe(pe, 2 * i + u + 1)
                        expert_pe2(pe, 2 * i + u, u)
                expert_pe(pe, NX - 2, 0, NX // 2)
                expert_pre_pe(pe, NX - 1)
                expert_pe2(pe, NX - 2, 0)
                expert_pe(pe, NX - 1, 1, NX // 2)
                expert_pe2(pe, NX - 1, 1)

            @blk.scalar
            def _(act):
                expert_pre_act(act, 0, 0)
                for u in range(2):
                    expert_act(act, u, u)
                    expert_pre_act(act, u + 1, 1 - u)
                with act.Fori(1, NX // 2 - 1) as i:
                    for u in range(2):
                        expert_act(act, 2 * i + u, u)
                        expert_pre_act(act, 2 * i + u + 1, 1 - u)
                expert_act(act, NX - 2, 0)
                expert_pre_act(act, NX - 1, 1)
                expert_act(act, NX - 1, 1)

            @blk.vector
            def _(dve):
                expert_pre_dve(dve, 0, 0, 1)
                expert_pre_dve(dve, 1, 1, 1)
                expert_dve(dve, 0, 0)
                expert_pre_dve(dve, 2, 0, 2)
                expert_dve(dve, 1, 1)
                with dve.Fori(1, NX // 2 - 1) as i:
                    expert_pre_dve(dve, 2 * i + 1, 1, i + 1)
                    expert_dve(dve, 2 * i, 0)
                    expert_pre_dve(dve, 2 * i + 2, 0, i + 2)
                    expert_dve(dve, 2 * i + 1, 1)
                expert_pre_dve(dve, NX - 1, 1, NX // 2)
                expert_dve(dve, NX - 2, 0)
                expert_dve(dve, NX - 1, 1)

            @blk.gpsimd
            def _(pool):
                with pool.Fori(0, NX) as n:
                    pool.wait_ge(emv_ready, n + 1)
                    pool.tensor_tensor(eve[:, :], emv[:, :, 1], eps_ln[:, :], ALU.add).then_inc(eve_ready, 1)
                    pool.wait_ge(eve_ready, n + 1)
                    pool.tensor_tensor(ers[:, :], eve[:, :], minus_half[:, :], ALU.pow).then_inc(ers_ready, 1)

        phase_b.close()
        YW = EMB + 1
        NB = 4
        cct = [sb(f"cct{u}", [128, SJ, TOK]) for u in range(NB)]
        cys = [sb(f"cys{u}", [128, SJ, YW]) for u in range(NB)]
        ch2 = [sb(f"ch2_{u}", [TT, 2, EMB]) for u in range(NB)]
        cout = [sb(f"cout{u}", [TT, 2, EMB]) for u in range(NB)]
        crd = [sb(f"crd{u}", [TT, 2]) for u in range(NB)]

        c_loaded = [sem(f"c_loaded{u}") for u in range(NB)]
        ones_set = sem("ones_set")
        comb_ready = sem("comb_ready")
        crd_ready = sem("crd_ready")
        cout_ready = sem("cout_ready")
        out_stored = [sem(f"out_stored{u}") for u in range(NB)]

        def load_comb(sp, i, u):
            sp.dma_start(cct[u].rearrange("p j t -> p (j t)"), ct_d[i]).then_inc(c_loaded[u], 16)
            sp.dma_start(cys[u][:, :, 0:EMB], ys_d[:, i, :, :].rearrange("n (a j) d -> n a (j d)", a=2)
                         ).then_inc(c_loaded[u], 16)
            sp.dma_start(ch2[u][:, :, :].rearrange("p t e -> p (t e)"), h2_d[i]).then_inc(c_loaded[u], 16)

        def store_out(act, i, u):
            act.wait_ge(cout_ready, i + 1)
            for t in range(2):
                act.dma_start(out[i, t * TT:(t + 1) * TT, :], cout[u][:, t, :]).then_inc(out_stored[u], 16)

        def comb_pe(pe, i, u, k):
            pe.wait_ge(c_loaded[u], k * 48)
            wait_past(pe, cout_ready, i - NB + 1)
            for t in range(2):
                for j in range(SJ):
                    mm = pe.matmul(ps[0:TT, u, t * YW:(t + 1) * YW], cct[u][:, j, t * TT:(t + 1) * TT],
                                   cys[u][:, j, :], start=(j == 0), stop=(j == SJ - 1))
            mm.then_inc(comb_ready, 1)

        def comb_dve(dve, i, u, k):
            dve.wait_ge(c_loaded[u], k * 48)
            dve.wait_ge(comb_ready, i + 1)
            dve.reciprocal(crd[u][:, :], ps[0:TT, u, 0:2 * YW].rearrange("p (t e) -> p t e", t=2)[:, :, EMB]
                           ).then_inc(crd_ready, 1)
            dve.wait_ge(crd_ready, i + 1)
            wait_past(dve, out_stored[u], (k - 1) * 32)
            for t in range(2):
                o = dve.scalar_tensor_tensor(out=cout[u][:, t, :], in0=ps[0:TT, u, t * YW:t * YW + EMB],
                                             scalar=crd[u][:, t:t + 1], in1=ch2[u][:, t, :],
                                             op0=ALU.mult, op1=ALU.add)
            o.then_inc(cout_ready, 1)

        with nc.Block() as blk:
            @blk.sync
            def _(sp):
                sp.wait_ge(ones_set, NB)
                for u in range(NB):
                    load_comb(sp, u, u)
                with sp.Fori(0, B // NB - 1) as i:
                    for u in range(NB):
                        sp.wait_ge(cout_ready, NB * i + u + 1)
                        load_comb(sp, NB * i + NB + u, u)

            @blk.scalar
            def _(act):
                with act.Fori(0, B // NB) as i:
                    for u in range(NB):
                        store_out(act, NB * i + u, u)
                for u in range(NB):
                    act.wait_ge(out_stored[u], B // NB * 32)

            @blk.tensor
            def _(pe):
                pe.wait_ge(ones_set, NB)
                for u in range(NB):
                    comb_pe(pe, u, u, 1)
                with pe.Fori(1, B // NB) as i:
                    for u in range(NB):
                        comb_pe(pe, NB * i + u, u, i + 1)

            @blk.vector
            def _(dve):
                for u in range(NB):
                    dve.memset(cys[u][:, :, :], 1.0).then_inc(ones_set, 1)
                for u in range(NB):
                    comb_dve(dve, u, u, 1)
                with dve.Fori(1, B // NB) as i:
                    for u in range(NB):
                        comb_dve(dve, NB * i + u, u, i + 1)


_INS = ['x', 'cls_tok', 'L0_tok_W', 'L0_tok_b', 'L0_tok_cls_token', 'L0_tok_pos_embed', 'L0_attn_W_attn',
        'L0_attn_b_attn', 'L0_attn_W_proj', 'L0_attn_b_proj', 'L0_ffn_phi', 'L0_ffn_ln_g', 'L0_ffn_ln_b',
        'L0_ffn_w1', 'L0_ffn_b1', 'L0_ffn_w2', 'L0_ffn_b2']
_OUTS = [((64, 198, 192), 'float32')]


def kernel(**inputs):
    import numpy as _np
    import concourse.bacc as _bacc
    from concourse import mybir as _mybir
    from concourse.bass_utils import run_bass_kernel_spmd as _run

    nc = _bacc.Bacc("TRN2", target_bir_lowering=False, num_devices=1)
    arrays, args = {}, []
    for name in _INS:
        a = _np.ascontiguousarray(inputs[name])
        arrays[f"in_{name}_dram"] = a
        args.append(nc.dram_tensor(f"in_{name}_dram", a.shape, _mybir.dt.from_np(a.dtype), kind="ExternalInput").ap())
    for i, (shape, dtype) in enumerate(_OUTS):
        dt = _mybir.dt.from_np(_np.dtype(dtype))
        args.append(nc.dram_tensor(f"out_{i}_dram", shape, dt, kind="ExternalOutput").ap())
    vit_tower(nc, *args)
    r = _run(nc, [arrays], core_ids=[0])
    got = tuple(r.results[0][f"out_{i}_dram"] for i in range(len(_OUTS)))
    return got[0]
```

```python
from contextlib import ExitStack

import concourse.bass as bass
from concourse import mybir

F32 = mybir.dt.float32
F32R = mybir.dt.float32r
ALU = mybir.AluOpType
ACT = mybir.ActivationFunctionType
AX = mybir.AxisListType


def vit_tower(
    nc: bass.Bass,
    x: bass.AP,
    cls_tok: bass.AP,
    W: bass.AP,
    b: bass.AP,
    cls_token: bass.AP,
    pos_embed: bass.AP,
    W_attn: bass.AP,
    b_attn: bass.AP,
    W_proj: bass.AP,
    b_proj: bass.AP,
    phi: bass.AP,
    ln_g: bass.AP,
    ln_b: bass.AP,
    w1: bass.AP,
    b1: bass.AP,
    w2: bass.AP,
    b2: bass.AP,
    out: bass.AP,
):
    B, IMG, _, CH = x.shape
    EMB, PD = W.shape
    PATCH = 16
    SIDE = IMG // PATCH
    NPATCH = SIDE * SIDE
    TOK = NPATCH + 2
    TT = TOK // 2
    TE = TT + TT % 2
    HP = NPATCH // 2
    HI = SIDE // 2
    PX = PATCH * CH
    HEADS = 12
    WIN = 6
    HS = EMB // HEADS
    HG = 4
    GROUPS = HEADS // HG
    FC = 96
    NX, NPX, _ = phi.shape
    SLOTS = NX * NPX
    SJ = SLOTS // 128
    HID = w1.shape[2]
    HC = HID // 128
    ROWS = B * NPX
    RJ = ROWS // 128
    KC = PD // 128
    CAUS = 3 * TT
    SCALE = float(HS) ** -0.5
    FAR = 1.0e30
    EPS = 1e-5
    EPS_NORM = 1e-6
    assert TOK == 2 * TT and EMB == 2 * FC and SJ * 16 == 128 and RJ == 8 and B % 2 == 0 and NX % 2 == 0

    ctx = ExitStack()
    with ctx:
        def sb(name, shape, dtype=F32):
            return ctx.enter_context(nc.sbuf_tensor(name, shape, dtype))

        def sbp(phase, name, shape, dtype=F32):
            return phase.enter_context(nc.sbuf_tensor(name, shape, dtype))

        def sem(name):
            return ctx.enter_context(nc.semaphore(name))

        def wait_past(eng, signal, value):
            if not (isinstance(value, int) and value <= 0):
                eng.wait_ge(signal, value)

        ctx.enter_context(nc.allow_non_contiguous_dma(reason="small biases, transposed once"))

        xs_d = nc.dram_tensor("xs_scratch", (NX, B, NPX, EMB), F32, kind="Internal").ap()
        ys_d = nc.dram_tensor("ys_scratch", (NX, B, NPX, EMB), F32, kind="Internal").ap()
        ct_d = nc.dram_tensor("combine_scratch", (B, 128, SJ * TOK), F32, kind="Internal").ap()
        h2_d = nc.dram_tensor("residual_scratch", (B, TT, 2 * EMB), F32, kind="Internal").ap()

        ps = ctx.enter_context(nc.psum_tensor("ps", [128, 8, 512], F32))

        ident = sb("ident", [128, 128])
        ones = sb("ones", [TT, 128])
        mask = sb("mask", [TT, CAUS])
        WT = sb("WT", [128, KC, EMB])
        wqk = sb("wqk", [FC + 1, 2, 2, HEADS, 2 * HS])
        watt = sb("watt", [FC + 1, 2, 3 * EMB])
        wproj = sb("wproj", [FC, 2, EMB])
        bproj = sb("bproj", [TT, EMB])
        posb = sb("posb", [TT, 2, EMB])
        phiT = sb("phiT", [FC, 2, SJ, 128])
        minus_half = sb("minus_half", [128, RJ])
        eps_ln = sb("eps_ln", [128, RJ])
        spare = sb("spare", [128, 1])
        minus_rest = sb("minus_rest", [128, 1])
        gT = sb("gT", [FC, 2, NX])
        bT = sb("bT", [FC, 2, NX])
        b1T = sb("b1T", [128, HC, NX])

        phase_a = ExitStack()
        ctx.enter_context(phase_a)
        xin = sbp(phase_a, "xin", [HP, 2, PD])
        xT = sbp(phase_a, "xT", [128, KC, TOK])
        h = sbp(phase_a, "h", [TT, 2, EMB])
        hb = sbp(phase_a, "hb", [TT, 2, EMB])
        st1 = sbp(phase_a, "st1", [TT, 2, 6])
        mv1 = sbp(phase_a, "mv1", [TT, 2, 2])
        ve1 = sbp(phase_a, "ve1", [TT, 2])
        rs1 = sbp(phase_a, "rs1", [TT, 2])
        xn1 = sbp(phase_a, "xn1", [TT, 2, EMB])
        xn1T = sbp(phase_a, "xn1T", [FC + 1, 2, TOK])
        q_high = sbp(phase_a, "q_high", [128, GROUPS, TOK], F32R)
        qT = sbp(phase_a, "qT", [128, GROUPS, TOK], F32R)
        k_high = sbp(phase_a, "k_high", [128, GROUPS, HG, TOK], F32R)
        k_rest = sbp(phase_a, "k_rest", [128, GROUPS, HG, TOK], F32R)
        vaug = sbp(phase_a, "vaug", [TT, 2, HEADS + WIN - 1, HS + 1])
        S = sbp(phase_a, "S", [TT, HEADS, CAUS])
        mn = sbp(phase_a, "mn", [TT, 2, HEADS])
        PT = sbp(phase_a, "PT", [TT, 3, HEADS, TT])
        rden = sbp(phase_a, "rden", [TT, 2, HEADS])
        on = sbp(phase_a, "on", [TT, 2, EMB])
        onT = sbp(phase_a, "onT", [FC, 2, TOK])
        h2 = sbp(phase_a, "h2", [TT, 2, EMB])
        st2 = sbp(phase_a, "st2", [TT, 2, 6])
        mv2 = sbp(phase_a, "mv2", [TT, 2, 2])
        ve2 = sbp(phase_a, "ve2", [TT, 2])
        rs2 = sbp(phase_a, "rs2", [TT, 2])
        xn2 = sbp(phase_a, "xn2", [TT, 2, EMB + 1])
        xn2T = sbp(phase_a, "xn2T", [FC, 2, TOK])
        LT = sbp(phase_a, "LT", [128, SJ, TOK])
        slot_max = sbp(phase_a, "slot_max", [128, SJ])
        tok_part = sbp(phase_a, "tok_part", [128, TOK])
        tok_max = sbp(phase_a, "tok_max", [TT, 2])
        tok_bc = sbp(phase_a, "tok_bc", [128, TOK])
        tok_diag = sbp(phase_a, "tok_diag", [TT, 2, TT])
        Td = sbp(phase_a, "Td", [128, SJ, TOK])
        CT = sbp(phase_a, "CT", [128, SJ, TOK])
        E = sbp(phase_a, "E", [TT, 2, SLOTS])
        rz = sbp(phase_a, "rz", [128, SJ])
        xs = sbp(phase_a, "xs", [128, SJ, EMB])

        DMA_LOADS = sem("setup_loaded")

        wraw = S[0:FC, :, :].rearrange("p a c -> p (a c)")[:, 0:2 * PD].rearrange("p (h f) -> p h f", h=2)
        wre = PT[0:FC, :, :, :].rearrange("p a b c -> p (a b c)")[:, 0:2 * PD].rearrange("p (h f) -> p h f", h=2)
        phin = LT[:, :, :].rearrange("p a c -> p (a c)")[:, 0:SJ * EMB].rearrange("p (j d) -> p j d", j=SJ)
        phisq = Td[:, :, :].rearrange("p a c -> p (a c)")[:, 0:SJ * EMB].rearrange("p (j d) -> p j d", j=SJ)
        phirs = CT[:, :, :].rearrange("p a c -> p (a c)")[:, 0:SJ * EMB].rearrange("p (j d) -> p j d", j=SJ)
        phihalf = xs[:, :, :]
        parity2 = rz[:, 0:2]
        row_rest = rz[:, 2:3]
        parity = tok_part[:, 0:128]
        posadd = xn1[:, :, :]
        graw = E[0:NX, 0, 0:EMB]
        braw = E[0:NX, 0, EMB:2 * EMB]
        b1raw = E[0:NX, 1, 0:HID]

        s_memset = sem("setup_memset")
        s_ident = sem("setup_ident")
        s_maskset = sem("setup_maskset")
        s_reorder = sem("setup_reorder")
        s_phisq = sem("setup_phisq")
        s_par2 = sem("setup_parity2")
        s_par = sem("setup_parity")
        s_phisum = sem("setup_phisum")
        s_phieps = sem("setup_phieps")
        s_phipow = sem("setup_phipow")
        s_newton = sem("setup_newton")
        s_phin = sem("setup_phin")
        s_sT = sem("setup_transposed")
        s_sE = sem("setup_evacuated")
        s_posb = sem("setup_posb")
        N_LOADS = 0
        with nc.Block() as blk:
            loads = [
                (wraw, W.rearrange("(h p) f -> p h f", p=FC)),
                (watt[0:FC, :, :], W_attn.rearrange("(h p) f -> p h f", p=FC)),
                (watt[FC:FC + 1, 0, :], b_attn.unsqueeze(0)),
                (wproj[:, :, :], W_proj.rearrange("(h p) f -> p h f", p=FC)),
                (phin, phi.rearrange("n p d -> (n p) d").rearrange("(q j) d -> q j d", j=SJ)),
                (graw, ln_g), (braw, ln_b), (b1raw, b1),
                (bproj[:, :], b_proj.partition_broadcast(TT)),
                (posb[1:TT, 0, :], pos_embed[0, 0:TT - 1, :]),
                (posb[:, 1, :], pos_embed[0, TT - 1:TOK - 1, :]),
                (posadd[0:1, 0, :], cls_tok[0]),
                (posadd[1:2, 0, :], cls_token[0]),
                (posadd[2:TT, 0, :], b.partition_broadcast(TT - 2)),
                (posadd[:, 1, :], b.partition_broadcast(TT)),
            ]
            N_LOADS = len(loads)

            @blk.sync
            def _(sp):
                sp.wait_ge(s_memset, 1)
                for dst, src in loads:
                    sp.dma_start(dst, src).then_inc(DMA_LOADS, 16)

            @blk.gpsimd
            def _(pool):
                pool.memset(posb[:, :, :], 0.0).then_inc(s_memset, 1)
                pool.memset(k_high[:, :, :, :].bitcast(F32), 0.0).then_inc(s_memset, 1)
                pool.memset(k_rest[:, :, :, :].bitcast(F32), 0.0).then_inc(s_memset, 1)
                pool.memset(ident[:, :], 0.0).then_inc(s_memset, 1)
                pool.wait_ge(s_memset, 4)
                pool.affine_select(out=ident[:, :], in_=ident[:, :], compare_op=ALU.not_equal, fill=1.0,
                                   base=0, pattern=[[-1, 128]], channel_multiplier=1).then_inc(s_ident, 1)
                pool.memset(ones[:, :], 1.0).then_inc(s_memset, 1)
                pool.memset(minus_half[:, :], -0.5).then_inc(s_memset, 1)
                pool.memset(eps_ln[:, :], EPS).then_inc(s_memset, 1)
                pool.memset(mask[:, :], 0.0).then_inc(s_memset, 1)
                pool.wait_ge(s_memset, 8)
                for c in (0, 2):
                    m = mask[:, c * TT:(c + 1) * TT]
                    pool.affine_select(out=m, in_=m, compare_op=ALU.is_ge, fill=FAR, base=0,
                                       pattern=[[-1, TT]], channel_multiplier=1).then_inc(s_maskset, 1)

            @blk.vector
            def _(dve):
                for k in range(KC):
                    dve.memset(xT[:, k, 0:2], 0.0)
                dve.memset(vaug[:, :, 0:HEADS, :], 1.0)
                dve.memset(vaug[:, :, HEADS:, :], 0.0)
                dve.memset(xn2[:, :, :], 1.0)
                dve.memset(xn1T[FC:FC + 1, 0, :], 1.0)
                dve.wait_ge(s_ident, 1)
                dve.tensor_reduce(parity2, ident[:, :].rearrange("p (a c) -> p c a", c=2), AX.X,
                                  ALU.add).then_inc(s_par2, 1)
                dve.tensor_reduce(row_rest, ident[:, :].rearrange("p (s u r) -> p s u r", s=4, u=2)[:, :, 1, :],
                                  AX.XY, ALU.add).then_inc(s_par2, 1)
                dve.wait_ge(s_par2, 2)
                dve.tensor_scalar(minus_rest[:, :], row_rest, -1.0, None, ALU.mult)
                dve.tensor_copy(parity.rearrange("p (a c) -> p a c", c=2),
                                parity2.unsqueeze(1).broadcast_to([128, 64, 2])).then_inc(s_par, 1)
                dve.wait_ge(DMA_LOADS, 16 * N_LOADS)
                for hh in range(2):
                    dve.tensor_copy(wre[:, hh, :].rearrange("p (a b c) -> p a b c", a=PATCH, b=PATCH),
                                    wraw[:, hh, :].rearrange("p (c a b) -> p a b c", a=PATCH, b=PATCH)
                                    ).then_inc(s_reorder, 1)
                for hh in range(2):
                    for qk in range(2):
                        for u in range(2):
                            parts = FC + 1 - hh
                            dve.tensor_scalar(wqk[0:parts, hh, qk, :, u * HS:(u + 1) * HS],
                                              watt[0:parts, hh, qk * EMB:(qk + 1) * EMB].rearrange(
                                                  "p (n r) -> p n r", r=HS),
                                              -1.0 if (qk, u) == (0, 1) else 1.0, None, ALU.mult)
                dve.tensor_tensor(posb[:, :, :], posb[:, :, :], posadd, ALU.add).then_inc(s_posb, 1)
                dve.tensor_tensor(phisq, phin, phin, ALU.mult).then_inc(s_phisq, 1)
                dve.wait_ge(s_phisum, 1)
                dve.tensor_scalar(phirs, ps[:, 0:4, 0:2 * EMB].rearrange("p k (j d) -> p k j d", j=2),
                                  EPS_NORM, None, ALU.add).then_inc(s_phieps, 1)
                dve.wait_ge(s_phipow, 1)
                dve.reciprocal(phihalf, phihalf).then_inc(s_newton, 1)
                dve.wait_ge(s_newton, 1)
                dve.tensor_tensor(phisq, phihalf, phihalf, ALU.mult).then_inc(s_newton, 1)
                dve.wait_ge(s_newton, 2)
                dve.scalar_tensor_tensor(out=phisq, in0=phisq, scalar=-0.5, in1=phirs, op0=ALU.mult,
                                         op1=ALU.mult).then_inc(s_newton, 1)
                dve.wait_ge(s_newton, 3)
                dve.scalar_tensor_tensor(out=phihalf, in0=phisq, scalar=1.5, in1=phihalf, op0=ALU.add,
                                         op1=ALU.mult).then_inc(s_newton, 1)
                dve.wait_ge(s_newton, 4)
                dve.tensor_tensor(phin, phin, phihalf, ALU.mult).then_inc(s_phin, 1)
                dve.wait_ge(s_sT, 1)
                dve.tensor_copy(WT[:, :, :], ps[:, 4:7, 0:2 * EMB].rearrange("p k (c e) -> p k c e", c=2)
                                ).then_inc(s_sE, 1)
                dve.wait_ge(s_sT, 2)
                dve.tensor_copy(gT[:, :, :], ps[0:FC, 7, 0:2 * NX].rearrange("p (c n) -> p c n", c=2))
                dve.tensor_copy(bT[:, :, :], ps[0:FC, 7, 2 * NX:4 * NX].rearrange("p (c n) -> p c n", c=2))
                dve.tensor_copy(b1T[:, :, :], ps[:, 7, 4 * NX:7 * NX].rearrange("p (c n) -> p c n", c=HC)
                                ).then_inc(s_sE, 1)
                dve.wait_ge(s_sT, 3)
                dve.tensor_copy(phiT[:, :, :, :], ps[0:FC, 0:4, :].rearrange("p k n -> p (k n)")
                                ).then_inc(s_sE, 1)

            @blk.scalar
            def _(act):
                act.wait_ge(s_phieps, 1)
                act.activation(phihalf, phirs, ACT.Sqrt).then_inc(s_phipow, 1)

            @blk.tensor
            def _(pe):
                pe.wait_ge(DMA_LOADS, 16 * N_LOADS)
                pe.wait_ge(s_ident, 1)
                pe.wait_ge(s_reorder, 2)
                for k in range(KC):
                    for hh in range(2):
                        mm = pe.transpose(ps[:, 4 + k // 2, (k % 2) * EMB + hh * FC:(k % 2) * EMB + (hh + 1) * FC],
                                          wre[:, hh, k * 128:(k + 1) * 128], ident[0:FC, 0:FC])
                mm.then_inc(s_sT, 1)
                for n, (src, parts) in enumerate(
                        [(graw[:, 0:FC], FC), (graw[:, FC:], FC), (braw[:, 0:FC], FC), (braw[:, FC:], FC)]
                        + [(b1raw[:, c * 128:(c + 1) * 128], 128) for c in range(HC)]):
                    mm = pe.transpose(ps[0:parts, 7, n * NX:(n + 1) * NX], src, ident[0:NX, 0:NX])
                mm.then_inc(s_sT, 1)
                pe.wait_ge(s_par, 1)
                pe.wait_ge(s_phisq, 1)
                for k in range(4):
                    mm = pe.matmul(ps[:, k, 0:2 * EMB], parity, phisq[:, 2 * k:2 * k + 2, :],
                                   start=True, stop=True)
                mm.then_inc(s_phisum, 1)
                pe.wait_ge(s_phin, 1)
                pe.wait_ge(s_phieps, 1)
                for hh in range(2):
                    for j in range(SJ):
                        k = hh * SJ + j
                        mm = pe.transpose(ps[0:FC, k // 4, (k % 4) * 128:(k % 4 + 1) * 128],
                                          phin[:, j, hh * FC:(hh + 1) * FC], ident[:, :])
                mm.then_inc(s_sT, 1)

        x_loaded = sem("x_loaded")
        xT_ready = sem("xT_ready")
        xT_copied = sem("xT_copied")
        Z_ready = sem("Z_ready")
        h_ready = sem("h_ready")
        hb_ready = sem("hb_ready")
        st1_ready = sem("st1_ready")
        mv1_ready = sem("mv1_ready")
        ve1_ready = sem("ve1_ready")
        rs1_ready = sem("rs1_ready")
        xn1_ready = sem("xn1_ready")
        xn1T_ready = sem("xn1T_ready")
        xn1T_copied = sem("xn1T_copied")
        qk_ready = sem("qk_ready")
        q_high_ready = sem("q_high_ready")
        q_split = sem("q_split")
        k_high_ready = sem("k_high_ready")
        k_split = sem("k_split")
        v_ready = sem("v_ready")
        v_copied = sem("v_copied")
        S_ready = sem("S_ready")
        S_masked = sem("S_masked")
        mn_ready = sem("mn_ready")
        P_ready = sem("P_ready")
        PT_ready = sem("PT_ready")
        PT_copied = sem("PT_copied")
        O_ready = sem("O_ready")
        rden_ready = sem("rden_ready")
        on_ready = sem("on_ready")
        onT_ready = sem("onT_ready")
        onT_copied = sem("onT_copied")
        proj_ready = sem("proj_ready")
        h2_ready = sem("h2_ready")
        h2_stored = sem("h2_stored")
        st2_ready = sem("st2_ready")
        mv2_ready = sem("mv2_ready")
        ve2_ready = sem("ve2_ready")
        rs2_ready = sem("rs2_ready")
        xn2_ready = sem("xn2_ready")
        xn2T_ready = sem("xn2T_ready")
        xn2T_copied = sem("xn2T_copied")
        LT_ready = sem("LT_ready")
        LT_copied = sem("LT_copied")
        smax_ready = sem("smax_ready")
        tpart_ready = sem("tpart_ready")
        tpartT_ready = sem("tpartT_ready")
        tmax_ready = sem("tmax_ready")
        tdiag_ready = sem("tdiag_ready")
        tbc_ready = sem("tbc_ready")
        tbc_copied = sem("tbc_copied")
        U_ready = sem("U_ready")
        CT_ready = sem("CT_ready")
        CT_stored = sem("CT_stored")
        Td_first_ready = sem("Td_first_ready")
        Td_ready = sem("Td_ready")
        TdT_ready = sem("TdT_ready")
        E_ready = sem("E_ready")
        Xs_ready = sem("Xs_ready")
        rz_ready = sem("rz_ready")
        xs_ready = sem("xs_ready")
        xs_stored = sem("xs_stored")

        def seg(bank, width=TOK):
            return ps[:, bank, 0:2 * width].rearrange("p (c t) -> p c t", c=2)

        def head_keys(dst, g):
            return dst[32 * g:32 * (g + 1), :, g, :]

        class pe_att:
            @staticmethod
            def patches(pe, i):
                pe.wait_ge(x_loaded, (i + 1) * (16 * SIDE))
                wait_past(pe, v_copied, i)
                wait_past(pe, E_ready, 2 * i - 3)
                for k in range(KC):
                    for t in range(2):
                        mm = pe.transpose(ps[:, 3 + k // 2, (k % 2) * NPATCH + t * HP:(k % 2) * NPATCH + (t + 1) * HP],
                                          xin[:, t, k * 128:(k + 1) * 128], ident[0:HP, 0:HP])
                mm.then_inc(xT_ready, 1)

            @staticmethod
            def embed(pe, i):
                pe.wait_ge(xT_copied, i + 1)
                wait_past(pe, S_masked, i * GROUPS * 2)
                for t in range(2):
                    for k in range(KC):
                        mm = pe.matmul(ps[0:TT, 0, t * EMB:(t + 1) * EMB], xT[:, k, t * TT:(t + 1) * TT],
                                       WT[:, k, :], start=(k == 0), stop=(k == KC - 1))
                mm.then_inc(Z_ready, 1)

            @staticmethod
            def turn(pe, i, src, bank, ready, done):
                pe.wait_ge(ready, i + 1)
                for t in range(2):
                    for c in range(2):
                        mm = pe.transpose(ps[0:FC, bank, c * TOK + t * TT:c * TOK + (t + 1) * TT],
                                          src[:, t, c * FC:(c + 1) * FC], ident[0:TT, 0:TT])
                mm.then_inc(done, 1)

            @staticmethod
            def qk(pe, i, j):
                if j == 0:
                    pe.wait_ge(xn1T_copied, i + 1)
                for qk in range(2):
                    for c in range(2):
                        n = FC + 1 - c
                        mm = pe.matmul(ps[:, j, qk * TOK:(qk + 1) * TOK], wqk[0:n, c, qk, HG * j:HG * (j + 1), :],
                                       xn1T[0:n, c, :], start=(c == 0), stop=(c == 1))
                if j == GROUPS - 1:
                    mm.then_inc(qk_ready, 1)

            @staticmethod
            def v(pe, i):
                wait_past(pe, h2_ready, i)
                for t in range(2):
                    for c in range(2):
                        n = FC + 1 - c
                        mm = pe.matmul(ps[0:TT, 4, t * EMB:(t + 1) * EMB], xn1T[0:n, c, t * TT:(t + 1) * TT],
                                       watt[0:n, c, 2 * EMB:3 * EMB], start=(c == 0), stop=(c == 1))
                mm.then_inc(v_ready, 1)

            @staticmethod
            def scores(pe, i, j):
                if j == 0:
                    pe.wait_ge(q_split, i + 1)
                    pe.wait_ge(k_split, i + 1)
                else:
                    pe.wait_ge(S_masked, (i * GROUPS + j) * 2)
                for k, keys in enumerate((k_high, k_rest)):
                    pe.matmul(ps[0:TT, 0, 0:HG * TE], qT[:, j, 0:TT], keys[:, j, :, 0:TE],
                              start=(k == 0), stop=(k == 1))
                for k, keys in enumerate((k_high, k_rest)):
                    for g in range(0, HG, 2):
                        mm = pe.matmul(ps[0:TT, 1 + g // 2, :].rearrange("p (g t) -> p g t", g=2)[:, :, 0:TOK],
                                       qT[:, j, TT:TOK], keys[:, j, g:g + 2, :], start=(k == 0), stop=(k == 1))
                mm.then_inc(S_ready, 1)

            @staticmethod
            def probs_turn(pe, i, j, embedded):
                pe.wait_ge(P_ready, i * GROUPS + j + 1)
                if j == 0:
                    pe.wait_ge(xT_copied, embedded)
                elif j == 1:
                    pe.wait_ge(PT_copied, i * GROUPS + 1)
                else:
                    pe.wait_ge(h_ready, embedded)
                    pe.wait_ge(S_masked, (i + 1) * GROUPS * 2)
                for c in range(3):
                    for g in range(HG):
                        mm = pe.transpose(ps[0:TT, (3, 3, 0)[j] + c, g * TT:(g + 1) * TT],
                                          S[:, HG * j + g, c * TT:(c + 1) * TT], ident[0:TT, 0:TT])
                mm.then_inc(PT_ready, 1)

            @staticmethod
            def weigh(pe, i, part):
                pe.wait_ge(PT_copied, i * GROUPS + 2 + part)
                pe.wait_ge(v_copied, i + 1)
                W1 = HS + 1
                for n in (range(2 * HG), range(2 * HG, HEADS))[part]:
                    for t in range(2):
                        o = ps[0:TT, 3 + t, n * W1:(n + WIN) * W1]
                        for kt in range(t + 1):
                            mm = pe.matmul(o, PT[:, t + kt, n, :], vaug[:, kt, n:n + WIN, :],
                                           start=(kt == 0), stop=(kt == t))
                if part == 1:
                    mm.then_inc(O_ready, 1)

            @staticmethod
            def proj(pe, i):
                pe.wait_ge(onT_copied, i + 1)
                for t in range(2):
                    for c in range(2):
                        mm = pe.matmul(ps[0:TT, 4, t * EMB:(t + 1) * EMB], onT[:, c, t * TT:(t + 1) * TT],
                                       wproj[:, c, :], start=(c == 0), stop=(c == 1))
                mm.then_inc(proj_ready, 1)

        class act_att:
            @staticmethod
            def turn(act, i, dst, bank, ready, done, free=None):
                act.wait_ge(ready, i + 1)
                if free is not None:
                    wait_past(act, free, i)
                act.activation(dst[0:FC, :, :], ps[0:FC, bank, 0:2 * TOK].rearrange("p (c t) -> p c t", c=2),
                               ACT.Copy).then_inc(done, 1)

            @staticmethod
            def qk(act, i):
                act.wait_ge(qk_ready, i + 1)
                wait_past(act, S_ready, i * GROUPS)
                act.activation(q_high[:, :, :], ps[:, 0:GROUPS, 0:TOK], ACT.Copy).then_inc(q_high_ready, 1)
                for g in range(HG):
                    act.activation(head_keys(k_high, g), ps[32 * g:32 * (g + 1), 0:GROUPS, TOK:2 * TOK],
                                   ACT.Copy).then_inc(k_high_ready, 1)

            @staticmethod
            def v(act, i):
                act.wait_ge(v_ready, i + 1)
                wait_past(act, O_ready, i)
                act.activation(vaug[:, :, 0:HEADS, 0:HS],
                               ps[0:TT, 4, 0:2 * EMB].rearrange("p (t n r) -> p t n r", t=2, r=HS),
                               ACT.Copy).then_inc(v_copied, 1)

            @staticmethod
            def probs(act, i, j):
                act.wait_ge(mn_ready, i * GROUPS + j + 1)
                for n in range(HG * j, HG * (j + 1)):
                    for t in range(2):
                        s = S[:, n, t * TT:(2 * t + 1) * TT]
                        p = act.activation(s, s, ACT.Exp, bias=mn[:, t, n:n + 1], scale=-1.0)
                p.then_inc(P_ready, 1)

            @staticmethod
            def probs_turn(act, i, j):
                act.wait_ge(PT_ready, i * GROUPS + j + 1)
                if j == 0:
                    wait_past(act, O_ready, i)
                act.activation(PT[:, :, HG * j:HG * (j + 1), :].rearrange("p c g t -> p c (g t)"),
                               ps[0:TT, (3, 3, 0)[j]:(6, 6, 3)[j], 0:HG * TT],
                               ACT.Copy).then_inc(PT_copied, 1)

        def layernorm_stats(dve, i, src, st, mv, src_ready, st_ready, mv_ready):
            dve.wait_ge(src_ready, i + 1)
            for t in range(2):
                s_ = dve.bn_stats(st[:, t, :], src[:, t, :])
            s_.then_inc(st_ready, 1)
            dve.wait_ge(st_ready, i + 1)
            dve.memset(spare[:, :], 0.0)
            for t in range(2):
                s_ = dve.bn_aggr(mv[:, t, :], st[:, t, :])
            s_.then_inc(mv_ready, 1)

        class dve_att:
            @staticmethod
            def patches(dve, i):
                dve.wait_ge(xT_ready, i + 1)
                wait_past(dve, Z_ready, i)
                for k in range(3):
                    cp = dve.tensor_copy(xT[:, 2 * k:2 * k + 2, 2:TOK], seg(3 + k, NPATCH))
                cp.then_inc(xT_copied, 1)

            @staticmethod
            def embed(dve, i):
                dve.wait_ge(Z_ready, i + 1)
                wait_past(dve, hb_ready, i)
                dve.tensor_tensor(h[:, :, :], ps[0:TT, 0, 0:2 * EMB].rearrange("p (t e) -> p t e", t=2),
                                  posb[:, :, :], ALU.add).then_inc(h_ready, 1)
                layernorm_stats(dve, i, h, st1, mv1, h_ready, st1_ready, mv1_ready)

            @staticmethod
            def norm1(dve, i):
                dve.wait_ge(rs1_ready, i + 1)
                wait_past(dve, xn1T_ready, i)
                for t in range(2):
                    s_ = dve.tensor_scalar(xn1[:, t, :], h[:, t, :], mv1[:, t, 0:1], rs1[:, t:t + 1],
                                           ALU.subtract, ALU.mult)
                s_.then_inc(xn1_ready, 1)

            @staticmethod
            def k(dve, i):
                wait_past(dve, S_ready, i * GROUPS)
                for g in range(HG):
                    dve.wait_ge(k_high_ready, i * HG + g + 1)
                    sp_ = dve.tensor_tensor(head_keys(k_rest, g),
                                            ps[32 * g:32 * (g + 1), 0:GROUPS, TOK:2 * TOK],
                                            head_keys(k_high, g), ALU.subtract)
                sp_.then_inc(k_split, 1)
                dve.wait_ge(q_high_ready, i + 1)
                dve.scalar_tensor_tensor(out=qT[:, :, :], in0=ps[:, 0:GROUPS, 0:TOK],
                                         scalar=minus_rest[:, 0:1], in1=q_high[:, :, :],
                                         op0=ALU.mult, op1=ALU.add).then_inc(q_split, 1)

            @staticmethod
            def softmax(dve, i, j):
                n = i * GROUPS + j + 1
                s = S[:, HG * j:HG * (j + 1), :]
                dve.wait_ge(S_ready, n)
                wait_past(dve, PT_ready, i * GROUPS)
                dve.scalar_tensor_tensor(out=s[:, :, 0:TT],
                                         in0=ps[0:TT, 0, 0:HG * TE].rearrange("p (g t) -> p g t", g=HG)[:, :, 0:TT],
                                         scalar=-SCALE, in1=mask[:, 0:TT].unsqueeze(1).broadcast_to([TT, HG, TT]),
                                         op0=ALU.mult, op1=ALU.add).then_inc(S_masked, 1)
                dve.scalar_tensor_tensor(out=s[:, :, TT:],
                                         in0=ps[0:TT, 1:3, :].rearrange("p b (g t) -> p (b g) t", g=2)[:, :, 0:TOK],
                                         scalar=-SCALE, in1=mask[:, TT:].unsqueeze(1).broadcast_to([TT, HG, TOK]),
                                         op0=ALU.mult, op1=ALU.add).then_inc(S_masked, 1)
                dve.wait_ge(S_masked, 2 * n)
                for t in range(2):
                    m = dve.tensor_reduce(mn[:, t, HG * j:HG * (j + 1)], s[:, :, t * TT:(2 * t + 1) * TT], AX.X,
                                          ALU.min)
                m.then_inc(mn_ready, 1)

            @staticmethod
            def weigh(dve, i):
                dve.wait_ge(O_ready, i + 1)
                o = ps[0:TT, 3:5, 0:HEADS * (HS + 1)].rearrange("p t (n r) -> p t n r", n=HEADS)
                dve.reciprocal(rden[:, :, :], o[:, :, :, HS]).then_inc(rden_ready, 1)
                dve.wait_ge(rden_ready, i + 1)
                wait_past(dve, onT_ready, i)
                for t in range(2):
                    m = dve.tensor_tensor(on[:, t, :].rearrange("p (n r) -> p n r", r=HS), o[:, t, :, 0:HS],
                                          rden[:, t, :].unsqueeze(2).broadcast_to([TT, HEADS, HS]), ALU.mult)
                m.then_inc(on_ready, 1)

            @staticmethod
            def resid(dve, i):
                dve.wait_ge(proj_ready, i + 1)
                dve.wait_ge(hb_ready, i + 1)
                wait_past(dve, h2_stored, i * 16)
                dve.tensor_tensor(h2[:, :, :], ps[0:TT, 4, 0:2 * EMB].rearrange("p (t e) -> p t e", t=2),
                                  hb[:, :, :], ALU.add).then_inc(h2_ready, 1)
                layernorm_stats(dve, i, h2, st2, mv2, h2_ready, st2_ready, mv2_ready)

            @staticmethod
            def norm2(dve, i):
                dve.wait_ge(rs2_ready, i + 1)
                wait_past(dve, Xs_ready, i * 4)
                for t in range(2):
                    s_ = dve.tensor_scalar(xn2[:, t, 0:EMB], h2[:, t, :], mv2[:, t, 0:1], rs2[:, t:t + 1],
                                           ALU.subtract, ALU.mult)
                s_.then_inc(xn2_ready, 1)

        def pool_rstd(pool, i, mv, ve, rs, mv_ready, ve_ready, rs_ready, reader):
            pool.wait_ge(mv_ready, i + 1)
            pool.tensor_tensor(ve[:, :], mv[:, :, 1], eps_ln[0:TT, 0:2], ALU.add).then_inc(ve_ready, 1)
            pool.wait_ge(ve_ready, i + 1)
            wait_past(pool, reader, i)
            pool.tensor_tensor(rs[:, :], ve[:, :], minus_half[0:TT, 0:2], ALU.pow).then_inc(rs_ready, 1)

        class pe_moe:
            @staticmethod
            def logits(pe, i, k, v_images):
                if k == 0:
                    pe.wait_ge(xn2T_copied, i + 1)
                    wait_past(pe, tbc_copied, i)
                if k == 1:
                    wait_past(pe, xs_ready, i * 4)
                if k == 3:
                    pe.wait_ge(v_copied, v_images)
                for j in (2 * k, 2 * k + 1):
                    for c in range(2):
                        mm = pe.matmul(ps[:, (5, 6, 7, 4)[k], (j % 2) * TOK:(j % 2 + 1) * TOK], phiT[:, c, j, :],
                                       xn2T[:, c, :], start=(c == 0), stop=(c == 1))
                mm.then_inc(LT_ready, 1)

            @staticmethod
            def tokmax_turn(pe, i):
                pe.wait_ge(tpart_ready, i + 1)
                for t in range(2):
                    mm = pe.transpose(ps[0:TT, 5, t * 128:(t + 1) * 128], tok_part[:, t * TT:(t + 1) * TT],
                                      ident[:, :])
                mm.then_inc(tpartT_ready, 1)

            @staticmethod
            def tokmax_spread(pe, i):
                pe.wait_ge(tdiag_ready, i + 1)
                for t in range(2):
                    mm = pe.matmul(ps[:, 5, 256 + t * TT:256 + (t + 1) * TT], ones[:, :], tok_diag[:, t, :],
                                   start=True, stop=True)
                mm.then_inc(tbc_ready, 1)

            @staticmethod
            def shifted_turn(pe, i):
                pe.wait_ge(Td_first_ready, i + 1)
                pe.wait_ge(Td_ready, 2 * (i + 1))
                pe.wait_ge(LT_copied, (i + 1) * 4)
                for t in range(2):
                    for j in range(SJ):
                        mm = pe.transpose(ps[0:TT, 4 + 2 * t + j // 4, (j % 4) * 128:(j % 4 + 1) * 128],
                                          Td[:, j, t * TT:(t + 1) * TT], ident[:, :])
                    mm.then_inc(TdT_ready, 1)

            @staticmethod
            def dispatch(pe, i, k):
                if k == 0:
                    pe.wait_ge(E_ready, 2 * (i + 1))
                if k >= 2:
                    pe.wait_ge(xs_ready, i * 4 + k - 1)
                for j in (2 * k, 2 * k + 1):
                    for t in range(2):
                        mm = pe.matmul(ps[:, 6 + k % 2, (j % 2) * (EMB + 1):(j % 2 + 1) * (EMB + 1)],
                                       E[:, t, j * 128:(j + 1) * 128], xn2[:, t, :],
                                       start=(t == 0), stop=(t == 1))
                mm.then_inc(Xs_ready, 1)

        class act_moe:
            @staticmethod
            def logits(act, i, k):
                act.wait_ge(LT_ready, i * 4 + k + 1)
                if k == 0:
                    wait_past(act, U_ready, i)
                    wait_past(act, tpart_ready, i)
                act.activation(LT[:, 2 * k:2 * k + 2, :], seg((5, 6, 7, 4)[k]), ACT.Copy).then_inc(LT_copied, 1)

            @staticmethod
            def spread(act, i):
                act.wait_ge(tbc_ready, i + 1)
                wait_past(act, U_ready, i)
                act.activation(tok_bc[:, :], ps[:, 5, 256:256 + TOK], ACT.Copy).then_inc(tbc_copied, 1)

            @staticmethod
            def combine(act, i):
                act.wait_ge(U_ready, i + 1)
                act.activation(CT[:, :, :], CT[:, :, :], ACT.Exp).then_inc(CT_ready, 1)

            @staticmethod
            def dispatch(act, i):
                wait_past(act, Xs_ready, i * 4)
                for t in range(2):
                    act.wait_ge(TdT_ready, 2 * i + t + 1)
                    act.activation(E[:, t, :], ps[0:TT, 4 + 2 * t:6 + 2 * t, :].rearrange("p k n -> p (k n)"),
                                   ACT.Exp).then_inc(E_ready, 1)

        SLOT_PARTS = (slice(0, SJ // 2), slice(SJ // 2, 3 * SJ // 4), slice(3 * SJ // 4, SJ))

        class dve_moe:
            @staticmethod
            def slotmax(dve, i, part):
                js = SLOT_PARTS[part]
                dve.wait_ge(LT_copied, i * 4 + 2 + part)
                dve.tensor_reduce(slot_max[:, js], LT[:, js, :], AX.X, ALU.max).then_inc(smax_ready, 1)

            @staticmethod
            def shift(dve, i, part):
                js = SLOT_PARTS[part]
                dve.wait_ge(smax_ready, 3 * i + part + 1)
                wait_past(dve, TdT_ready, 2 * i)
                dve.tensor_tensor(Td[:, js, :], LT[:, js, :],
                                  slot_max[:, js].unsqueeze(2).broadcast_to([128, js.stop - js.start, TOK]),
                                  ALU.subtract).then_inc(Td_ready, 1)

            @staticmethod
            def tokpart(dve, i):
                wait_past(dve, tpartT_ready, i)
                dve.tensor_reduce(tok_part[:, :], LT[:, :, :].rearrange("p j t -> p t j"), AX.X,
                                  ALU.max).then_inc(tpart_ready, 1)

            @staticmethod
            def tokmax(dve, i):
                dve.wait_ge(tpartT_ready, i + 1)
                dve.tensor_reduce(tok_max[:, :], ps[0:TT, 5, 0:256].rearrange("p (t n) -> p t n", t=2), AX.X,
                                  ALU.max).then_inc(tmax_ready, 1)
                dve.wait_ge(tmax_ready, i + 1)
                for t in range(2):
                    d = dve.tensor_scalar(tok_diag[:, t, :], ident[0:TT, 0:TT], tok_max[:, t:t + 1], None,
                                          ALU.mult)
                d.then_inc(tdiag_ready, 1)

            @staticmethod
            def dispatch(dve, i, k):
                n = i * 4 + k + 1
                o = seg(6 + k % 2, EMB + 1)
                dve.wait_ge(Xs_ready, n)
                dve.reciprocal(rz[:, 2 * k:2 * k + 2], o[:, :, EMB]).then_inc(rz_ready, 1)
                dve.wait_ge(rz_ready, n)
                if k == 0:
                    wait_past(dve, xs_stored, i * 16)
                dve.tensor_tensor(xs[:, 2 * k:2 * k + 2, :], o[:, :, 0:EMB],
                                  rz[:, 2 * k:2 * k + 2].unsqueeze(2).broadcast_to([128, 2, EMB]),
                                  ALU.mult).then_inc(xs_ready, 1)

        def load_x(sp, i):
            for r in range(SIDE):
                src = x[i, r * PATCH:(r + 1) * PATCH, :, :].rearrange(
                    "a (j b) c -> j a (b c)", j=SIDE)
                p0 = (r % HI) * SIDE
                dst = xin[p0:p0 + SIDE, r // HI, :].rearrange("p (a f) -> p a f", a=PATCH)
                sp.dma_start(dst, src).then_inc(x_loaded, 16)

        PE_ORDER = ["a.s0", "m.dturn", "a.s1", "e.patches", "m.x0", "a.s2", "m.x1", "a.p0", "e.embed", "a.p1", "a.p2",
                    "a.w0", "e.turn1", "m.tokmax", "a.w1", "m.spread", "e.q0", "a.turno", "e.q1", "a.proj", "m.x2",
                    "m.x3", "e.q2", "a.turn2", "e.v", "l.0", "l.1", "l.2", "l.3"]
        ACT_ORDER = ["m.dturn", "a.s0", "a.s1", "a.p0", "a.s2", "a.p1", "a.p2", "e.turn1", "m.spread", "a.turno",
                     "m.combine", "a.turn2", "e.qk", "e.v", "l.0", "l.1", "l.2", "l.3"]
        DVE_ORDER = ["m.slot0", "m.slot1", "m.shift1", "m.slot2", "m.shift2", "a.s0", "a.s1", "e.patches", "a.s2",
                     "m.x0", "e.embed", "m.x1", "e.norm1", "m.tokpart", "m.tokmax", "a.weigh", "a.proj", "m.x2",
                     "a.turn2", "m.x3", "e.k"]

        def run_pe(pe, i, parts):
            for s in PE_ORDER:
                if s[0] not in parts:
                    continue
                if s == "e.patches":
                    pe_att.patches(pe, i + 1)
                elif s == "e.embed":
                    pe_att.embed(pe, i + 1)
                elif s == "e.turn1":
                    wait_past(pe, xs_ready, 4 * i - 2)
                    pe_att.turn(pe, i + 1, xn1, 7, xn1_ready, xn1T_ready)
                elif s in ("e.q0", "e.q1", "e.q2"):
                    pe_att.qk(pe, i + 1, int(s[3]))
                elif s == "e.v":
                    pe_att.v(pe, i + 1)
                elif s in ("a.s0", "a.s1", "a.s2"):
                    pe_att.scores(pe, i, int(s[3]))
                elif s in ("a.p0", "a.p1", "a.p2"):
                    pe_att.probs_turn(pe, i, int(s[3]), i + 2 if "e" in parts else B)
                elif s in ("a.w0", "a.w1"):
                    pe_att.weigh(pe, i, int(s[3]))
                elif s == "a.turno":
                    pe_att.turn(pe, i, on, 3, on_ready, onT_ready)
                elif s == "a.proj":
                    pe_att.proj(pe, i)
                elif s == "a.turn2":
                    pe_att.turn(pe, i, xn2, 3, xn2_ready, xn2T_ready)
                elif s[0] == "l":
                    pe_moe.logits(pe, i, int(s[2]), i + 2 if "e" in parts else B)
                elif s == "m.tokmax":
                    pe_moe.tokmax_turn(pe, i - 1)
                elif s == "m.spread":
                    pe_moe.tokmax_spread(pe, i - 1)
                elif s == "m.dturn":
                    pe_moe.shifted_turn(pe, i - 1)
                elif s[:3] == "m.x":
                    pe_moe.dispatch(pe, i - 1, int(s[3]))

        def run_act(act, i, parts):
            for s in ACT_ORDER:
                if s[0] not in parts:
                    continue
                if s == "e.turn1":
                    wait_past(act, v_ready, i + 1)
                    act_att.turn(act, i + 1, xn1T, 7, xn1T_ready, xn1T_copied)
                elif s == "e.qk":
                    act_att.qk(act, i + 1)
                elif s == "e.v":
                    act_att.v(act, i + 1)
                elif s in ("a.s0", "a.s1", "a.s2"):
                    act_att.probs(act, i, int(s[3]))
                elif s in ("a.p0", "a.p1", "a.p2"):
                    act_att.probs_turn(act, i, int(s[3]))
                elif s == "a.turno":
                    wait_past(act, proj_ready, i)
                    act_att.turn(act, i, onT, 3, onT_ready, onT_copied)
                elif s == "a.turn2":
                    wait_past(act, LT_ready, i * 4)
                    act_att.turn(act, i, xn2T, 3, xn2T_ready, xn2T_copied)
                elif s[0] == "l":
                    act_moe.logits(act, i, int(s[2]))
                elif s == "m.spread":
                    act_moe.spread(act, i - 1)
                elif s == "m.combine":
                    act_moe.combine(act, i - 1)
                elif s == "m.dturn":
                    act_moe.dispatch(act, i - 1)

        def run_dve(dve, i, parts):
            for s in DVE_ORDER:
                if s[0] not in parts:
                    continue
                if s == "e.patches":
                    dve_att.patches(dve, i + 1)
                elif s == "e.embed":
                    dve_att.embed(dve, i + 1)
                elif s == "e.norm1":
                    dve_att.norm1(dve, i + 1)
                elif s == "e.k":
                    dve_att.k(dve, i + 1)
                elif s in ("a.s0", "a.s1", "a.s2"):
                    dve_att.softmax(dve, i, int(s[3]))
                elif s == "a.weigh":
                    dve_att.weigh(dve, i)
                elif s == "a.proj":
                    dve_att.resid(dve, i)
                elif s == "a.turn2":
                    dve_att.norm2(dve, i)
                elif s in ("m.slot0", "m.slot1", "m.slot2"):
                    dve_moe.slotmax(dve, i - 1, int(s[6]))
                elif s == "m.tokpart":
                    dve_moe.tokpart(dve, i - 1)
                elif s == "m.tokmax":
                    dve_moe.tokmax(dve, i - 1)
                elif s in ("m.shift1", "m.shift2"):
                    dve_moe.shift(dve, i - 1, int(s[7]))
                elif s[:3] == "m.x":
                    dve_moe.dispatch(dve, i - 1, int(s[3]))

        def pool_combine(pool, i):
            pool.wait_ge(tbc_copied, i + 1)
            pool.wait_ge(LT_copied, (i + 1) * 4)
            wait_past(pool, CT_stored, i * 16)
            pool.tensor_tensor(CT[:, :, :], LT[:, :, :],
                               tok_bc[:, :].unsqueeze(1).broadcast_to([128, SJ, TOK]),
                               ALU.subtract).then_inc(U_ready, 1)

        def pool_shift(pool, i):
            js = SLOT_PARTS[0]
            pool.wait_ge(smax_ready, 3 * i + 1)
            wait_past(pool, TdT_ready, 2 * i)
            pool.tensor_tensor(Td[:, js, :], LT[:, js, :],
                               slot_max[:, js].unsqueeze(2).broadcast_to([128, js.stop - js.start, TOK]),
                               ALU.subtract).then_inc(Td_first_ready, 1)

        def run_pool(pool, i, parts):
            if "m" in parts:
                pool_shift(pool, i - 1)
            if "e" in parts:
                pool_rstd(pool, i + 1, mv1, ve1, rs1, mv1_ready, ve1_ready, rs1_ready, xn1_ready)
            if "m" in parts:
                pool_combine(pool, i - 1)
            if "a" in parts:
                pool_rstd(pool, i, mv2, ve2, rs2, mv2_ready, ve2_ready, rs2_ready, xn2_ready)
            if "e" in parts:
                wait_past(pool, h2_ready, i + 1)
                pool.tensor_tensor(hb[:, :, :], h[:, :, :],
                                   bproj[:, :].unsqueeze(1).broadcast_to([TT, 2, EMB]),
                                   ALU.add).then_inc(hb_ready, 1)

        def run_sp(sp, i, parts, load=True):
            if load:
                sp.wait_ge(xT_ready, i + 2)
                load_x(sp, i + 2)
            if "m" in parts:
                wait_past(sp, CT_ready, i)
                sp.dma_start(ct_d[i - 1], CT[:, :, :].rearrange("p j t -> p (j t)")).then_inc(CT_stored, 16)
                wait_past(sp, xs_ready, i * 4)
                sp.dma_start(xs_d[:, i - 1, :, :].rearrange("n (a j) d -> n a (j d)", a=2),
                             xs[:, :, :].rearrange("q j d -> q (j d)")).then_inc(xs_stored, 16)
            if "a" in parts:
                sp.wait_ge(h2_ready, i + 1)
                sp.dma_start(h2_d[i], h2[:, :, :].rearrange("p t e -> p (t e)")).then_inc(h2_stored, 16)

        def all_turns(eng, run):
            run(eng, -1, "e")
            run(eng, 0, "ael")
            run(eng, 1, "amel")
            with eng.Fori(2, B - 1) as i:
                run(eng, i, "amel")
            run(eng, B - 1, "aml")
            run(eng, B, "m")

        with nc.Block() as blk:
            @blk.sync
            def _(sp):
                load_x(sp, 0)
                run_sp(sp, -1, "e")
                run_sp(sp, 0, "ael")
                run_sp(sp, 1, "amel")
                with sp.Fori(2, B - 2) as i:
                    run_sp(sp, i, "amel")
                run_sp(sp, B - 2, "amel", load=False)
                run_sp(sp, B - 1, "aml", load=False)
                run_sp(sp, B, "m", load=False)
                sp.wait_ge(xs_stored, B * 16)
                sp.wait_ge(CT_stored, B * 16)
                sp.wait_ge(h2_stored, B * 16)

            @blk.tensor
            def _(pe):
                all_turns(pe, run_pe)

            @blk.scalar
            def _(act):
                all_turns(act, run_act)

            @blk.vector
            def _(dve):
                all_turns(dve, run_dve)

            @blk.gpsimd
            def _(pool):
                all_turns(pool, run_pool)

        phase_a.close()
        phase_b = ExitStack()
        ctx.enter_context(phase_b)
        ein = [sbp(phase_b, f"ein{u}", [128, RJ, EMB]) for u in range(2)]
        ew1 = [sbp(phase_b, f"ew1_{u}", [FC, 2, HID]) for u in range(2)]
        ew2 = [sbp(phase_b, f"ew2_{u}", [128, HC, EMB]) for u in range(2)]
        eb2 = [sbp(phase_b, f"eb2_{u}", [128, EMB]) for u in range(2)]
        col = [sbp(phase_b, f"ecol{u}", [128, 2 * 2 + HC]) for u in range(2)]
        est = sbp(phase_b, "est", [128, RJ, 6])
        emv = sbp(phase_b, "emv", [128, RJ, 2])
        eve = sbp(phase_b, "eve", [128, RJ])
        ers = sbp(phase_b, "ers", [128, RJ])
        ehn = sbp(phase_b, "ehn", [128, RJ, EMB])
        ehT = sbp(phase_b, "ehT", [FC, 2, ROWS])
        eh_high = sbp(phase_b, "eh_high", [FC, 2, ROWS], F32R)
        eh_rest = sbp(phase_b, "eh_rest", [FC, 2, ROWS], F32R)
        w_high = [sbp(phase_b, f"w_high{u}", [FC, 2, HID], F32R) for u in range(2)]
        w_rest = [sbp(phase_b, f"w_rest{u}", [FC, 2, HID], F32R) for u in range(2)]
        ys = sbp(phase_b, "ys", [128, RJ, EMB])
        hid = sbp(phase_b, "hid", [128, HC, ROWS])

        e_loaded = [sem(f"e_loaded{u}") for u in range(2)]
        w_loaded = [sem(f"w_loaded{u}") for u in range(2)]
        est_ready = sem("est_ready")
        emv_ready = sem("emv_ready")
        eve_ready = sem("eve_ready")
        ers_ready = sem("ers_ready")
        ehn_ready = sem("ehn_ready")
        ehT_ready = sem("ehT_ready")
        col_ready = sem("col_ready")
        ehT_copied = sem("ehT_copied")
        eh_high_ready = sem("eh_high_ready")
        eh_rest_ready = sem("eh_rest_ready")
        w_high_ready = sem("w_high_ready")
        w_rest_ready = sem("w_rest_ready")
        H_ready = sem("H_ready")
        H_copied = sem("H_copied")
        Y_ready = sem("Y_ready")
        Y_copied = sem("Y_copied")
        ys_stored = sem("ys_stored")
        NH = 2 * HC

        def load_rows(sp, n, u):
            wait_past(sp, ehn_ready, n - 1)
            sp.dma_start(ein[u][:, :, :].rearrange("r j d -> r (j d)"),
                         xs_d[n].rearrange("b p d -> (b p) d").rearrange("(r j) d -> r (j d)", j=RJ)
                         ).then_inc(e_loaded[u], 16)

        def load_weights(sp, n, u):
            wait_past(sp, Y_copied, (n - 1) * 4)
            sp.dma_start(ew1[u][:, :, :], w1[n].rearrange("(c p) f -> p c f", p=FC)).then_inc(w_loaded[u], 16)
            sp.dma_start(ew2[u][:, :, :], w2[n].rearrange("(c p) f -> p c f", p=128)).then_inc(w_loaded[u], 16)
            sp.dma_start(eb2[u][:, :], b2[n].partition_broadcast(128)).then_inc(w_loaded[u], 16)

        def store_expert(sp, n):
            sp.wait_ge(Y_copied, (n + 1) * 4)
            sp.dma_start(ys_d[n].rearrange("b p d -> (b p) d").rearrange("(r j) d -> r (j d)", j=RJ),
                         ys[:, :, :].rearrange("r j d -> r (j d)")).then_inc(ys_stored, 16)

        def run_sp_experts(sp, n, u, rows=True, weights=True):
            if weights:
                load_weights(sp, n + 1, 1 - u)
            if rows:
                load_rows(sp, n + 2, u)
            store_expert(sp, n)

        def expert_stats_dve(dve, n, u, k):
            dve.wait_ge(e_loaded[u], k * 16)
            for t in range(RJ):
                s_ = dve.bn_stats(est[:, t, :], ein[u][:, t, :])
            s_.then_inc(est_ready, 1)
            dve.wait_ge(est_ready, n + 1)
            dve.memset(spare[:, :], 0.0)
            for t in range(RJ):
                s_ = dve.bn_aggr(emv[:, t, :], est[:, t, :])
            s_.then_inc(emv_ready, 1)
            wait_past(dve, H_copied, (n - 1) * NH)
            dve.tensor_copy(col[u][0:FC, 0:2], gT[:, :, n])
            dve.tensor_copy(col[u][0:FC, 2:4], bT[:, :, n])
            dve.tensor_copy(col[u][:, 4:4 + HC], b1T[:, :, n]).then_inc(col_ready, 1)

        def expert_norm_dve(dve, n, u):
            wait_past(dve, ehT_ready, n * 4)
            dve.wait_ge(ers_ready, n + 1)
            for t in range(RJ):
                s_ = dve.tensor_scalar(ehn[:, t, :], ein[u][:, t, :], emv[:, t, 0:1], ers[:, t:t + 1],
                                       ALU.subtract, ALU.mult)
            s_.then_inc(ehn_ready, 1)

        def expert_pre_pe(pe, n):
            pe.wait_ge(ehn_ready, n + 1)
            wait_past(pe, eh_high_ready, n * 4)
            for c in range(2):
                for hh in range(2):
                    for t in range(4):
                        mm = pe.transpose(ps[0:FC, 2 * c + hh, t * 128:(t + 1) * 128],
                                          ehn[:, 4 * hh + t, c * FC:(c + 1) * FC], ident[:, :])
                    mm.then_inc(ehT_ready, 1)

        def expert_pre_act(act, n, u):
            act.wait_ge(col_ready, n + 1)
            wait_past(act, eh_rest_ready, n * 4)
            wait_past(act, H_ready, n * NH)
            for c in range(2):
                for hh in range(2):
                    act.wait_ge(ehT_ready, n * 4 + 2 * c + hh + 1)
                    for dst, done in ((ehT, ehT_copied), (eh_high, eh_high_ready)):
                        act.activation(dst[:, c, hh * 512:(hh + 1) * 512], ps[0:FC, 2 * c + hh, :], ACT.Identity,
                                       bias=col[u][0:FC, 2 + c:3 + c], scale=col[u][0:FC, c:c + 1]
                                       ).then_inc(done, 1)

        def expert_pool(pool, n, u):
            pool.wait_ge(emv_ready, n + 1)
            pool.tensor_tensor(eve[:, :], emv[:, :, 1], eps_ln[:, :], ALU.add).then_inc(eve_ready, 1)
            pool.wait_ge(eve_ready, n + 1)
            pool.tensor_tensor(ers[:, :], eve[:, :], minus_half[:, :], ALU.pow).then_inc(ers_ready, 1)
            pool.wait_ge(w_high_ready, n + 1)
            wait_past(pool, H_ready, (n - 1) * NH)
            pool.tensor_tensor(w_rest[u][:, :, :], ew1[u][:, :, :], w_high[u][:, :, :],
                               ALU.subtract).then_inc(w_rest_ready, 1)
            wait_past(pool, H_ready, n * NH)
            for q in range(4):
                part = (slice(None), q // 2, slice(q % 2 * 512, (q % 2 + 1) * 512))
                pool.wait_ge(eh_high_ready, n * 4 + q + 1)
                pool.tensor_tensor(eh_rest[part], ehT[part], eh_high[part], ALU.subtract).then_inc(eh_rest_ready, 1)

        def expert_pe(pe, n, u, k):
            pe.wait_ge(w_loaded[u], k * 48)
            pe.wait_ge(w_rest_ready, n + 1)
            pe.wait_ge(eh_rest_ready, (n + 1) * 4)
            for m in range(HC):
                if m == 0:
                    wait_past(pe, H_copied, n * NH)
                elif m == 1:
                    wait_past(pe, Y_copied, n * 4)
                else:
                    pe.wait_ge(H_copied, n * NH + 2)
                for hh in range(2):
                    for c in range(2):
                        for p, (w, e) in enumerate(((w_high, eh_high), (w_high, eh_rest), (w_rest, eh_high))):
                            mm = pe.matmul(ps[:, 4 + 2 * (m % 2) + hh, :], w[u][:, c, m * 128:(m + 1) * 128],
                                           e[:, c, hh * 512:(hh + 1) * 512], start=(c == 0 and p == 0),
                                           stop=(c == 1 and p == 2))
                    mm.then_inc(H_ready, 1)

        def high_weights(act, n, u, k):
            act.wait_ge(w_loaded[u], k * 48)
            wait_past(act, H_ready, (n - 1) * NH)
            act.activation(w_high[u][:, :, :], ew1[u][:, :, :], ACT.Copy).then_inc(w_high_ready, 1)

        def expert_act(act, n, u, next_k=None):
            wait_past(act, Y_ready, n * 4)
            for m in range(NH):
                act.wait_ge(H_ready, n * NH + m + 1)
                third, half = m // 2, m % 2
                act.activation(hid[:, third, half * 512:(half + 1) * 512], ps[:, 4 + 2 * (third % 2) + half, :],
                               ACT.Gelu, bias=col[u][:, 4 + third:5 + third]).then_inc(H_copied, 1)
                if m == NH - 3 and next_k is not None:
                    high_weights(act, n + 1, 1 - u, next_k)

        def expert_pe2(pe, n, u):
            pe.wait_ge(H_copied, (n + 1) * NH)
            for m in range(4):
                if m >= 2:
                    pe.wait_ge(Y_copied, n * 4 + m - 1)
                else:
                    wait_past(pe, Y_copied, n * 4)
                for t in (2 * m, 2 * m + 1):
                    for c in range(HC):
                        mm = pe.matmul(ps[:, 6 + m % 2, (t % 2) * EMB:(t % 2 + 1) * EMB],
                                       hid[:, c, t * 128:(t + 1) * 128], ew2[u][:, c, :],
                                       start=(c == 0), stop=(c == HC - 1))
                mm.then_inc(Y_ready, 1)

        def expert_dve(dve, n, u):
            wait_past(dve, ys_stored, n * 16)
            for m in range(4):
                dve.wait_ge(Y_ready, n * 4 + m + 1)
                dve.tensor_tensor(ys[:, 2 * m:2 * m + 2, :],
                                  ps[:, 6 + m % 2, 0:2 * EMB].rearrange("p (t e) -> p t e", t=2),
                                  eb2[u][:, :].unsqueeze(1).broadcast_to([128, 2, EMB]),
                                  ALU.add).then_inc(Y_copied, 1)

        with nc.Block() as blk:
            @blk.sync
            def _(sp):
                load_rows(sp, 0, 0)
                load_weights(sp, 0, 0)
                load_rows(sp, 1, 1)
                for u in range(2):
                    run_sp_experts(sp, u, u)
                with sp.Fori(1, NX // 2 - 1) as i:
                    for u in range(2):
                        run_sp_experts(sp, 2 * i + u, u)
                run_sp_experts(sp, NX - 2, 0, rows=False)
                run_sp_experts(sp, NX - 1, 1, rows=False, weights=False)
                sp.wait_ge(ys_stored, NX * 16)

            @blk.tensor
            def _(pe):
                expert_pre_pe(pe, 0)
                for u in range(2):
                    expert_pe(pe, u, u, 1)
                    expert_pre_pe(pe, u + 1)
                    expert_pe2(pe, u, u)
                with pe.Fori(1, NX // 2 - 1) as i:
                    for u in range(2):
                        expert_pe(pe, 2 * i + u, u, i + 1)
                        expert_pre_pe(pe, 2 * i + u + 1)
                        expert_pe2(pe, 2 * i + u, u)
                expert_pe(pe, NX - 2, 0, NX // 2)
                expert_pre_pe(pe, NX - 1)
                expert_pe2(pe, NX - 2, 0)
                expert_pe(pe, NX - 1, 1, NX // 2)
                expert_pe2(pe, NX - 1, 1)

            @blk.scalar
            def _(act):
                expert_pre_act(act, 0, 0)
                high_weights(act, 0, 0, 1)
                for u in range(2):
                    expert_act(act, u, u, 1 + u)
                    expert_pre_act(act, u + 1, 1 - u)
                with act.Fori(1, NX // 2 - 1) as i:
                    for u in range(2):
                        expert_act(act, 2 * i + u, u, i + 1 + u)
                        expert_pre_act(act, 2 * i + u + 1, 1 - u)
                expert_act(act, NX - 2, 0, NX // 2)
                expert_pre_act(act, NX - 1, 1)
                expert_act(act, NX - 1, 1)

            @blk.vector
            def _(dve):
                for n in range(2):
                    expert_stats_dve(dve, n, n, 1)
                    expert_norm_dve(dve, n, n)
                expert_stats_dve(dve, 2, 0, 2)
                for u in range(2):
                    expert_dve(dve, u, u)
                    expert_norm_dve(dve, u + 2, u)
                    expert_stats_dve(dve, u + 3, 1 - u, u + 2)
                with dve.Fori(1, NX // 2 - 2) as i:
                    for u in range(2):
                        expert_dve(dve, 2 * i + u, u)
                        expert_norm_dve(dve, 2 * i + u + 2, u)
                        expert_stats_dve(dve, 2 * i + u + 3, 1 - u, i + u + 2)
                expert_dve(dve, NX - 4, 0)
                expert_norm_dve(dve, NX - 2, 0)
                expert_stats_dve(dve, NX - 1, 1, NX // 2)
                expert_dve(dve, NX - 3, 1)
                expert_norm_dve(dve, NX - 1, 1)
                expert_dve(dve, NX - 2, 0)
                expert_dve(dve, NX - 1, 1)

            @blk.gpsimd
            def _(pool):
                for u in range(2):
                    expert_pool(pool, u, u)
                with pool.Fori(1, NX // 2) as i:
                    for u in range(2):
                        expert_pool(pool, 2 * i + u, u)

        phase_b.close()
        YW = EMB + 1
        NB = 4
        cct = [sb(f"cct{u}", [128, SJ, TOK]) for u in range(NB)]
        cys = [sb(f"cys{u}", [128, SJ, YW]) for u in range(NB)]
        ch2 = [sb(f"ch2_{u}", [TT, 2, EMB]) for u in range(NB)]
        cout = [sb(f"cout{u}", [TT, 2, EMB]) for u in range(NB)]
        crd = [sb(f"crd{u}", [TT, 2]) for u in range(NB)]

        c_loaded = [sem(f"c_loaded{u}") for u in range(NB)]
        ones_set = sem("ones_set")
        comb_ready = sem("comb_ready")
        crd_ready = sem("crd_ready")
        cout_ready = sem("cout_ready")
        out_stored = [sem(f"out_stored{u}") for u in range(NB)]

        def load_comb(sp, i, u):
            sp.dma_start(cct[u].rearrange("p j t -> p (j t)"), ct_d[i]).then_inc(c_loaded[u], 16)
            sp.dma_start(cys[u][:, :, 0:EMB], ys_d[:, i, :, :].rearrange("n (a j) d -> n a (j d)", a=2)
                         ).then_inc(c_loaded[u], 16)
            sp.dma_start(ch2[u][:, :, :].rearrange("p t e -> p (t e)"), h2_d[i]).then_inc(c_loaded[u], 16)

        def store_out(act, i, u):
            act.wait_ge(cout_ready, i + 1)
            for t in range(2):
                act.dma_start(out[i, t * TT:(t + 1) * TT, :], cout[u][:, t, :]).then_inc(out_stored[u], 16)

        def comb_pe(pe, i, u, k):
            pe.wait_ge(c_loaded[u], k * 48)
            wait_past(pe, cout_ready, i - NB + 1)
            for t in range(2):
                for j in range(SJ):
                    mm = pe.matmul(ps[0:TT, u, t * YW:(t + 1) * YW], cct[u][:, j, t * TT:(t + 1) * TT],
                                   cys[u][:, j, :], start=(j == 0), stop=(j == SJ - 1))
            mm.then_inc(comb_ready, 1)

        def comb_dve(dve, i, u, k):
            dve.wait_ge(c_loaded[u], k * 48)
            dve.wait_ge(comb_ready, i + 1)
            dve.reciprocal(crd[u][:, :], ps[0:TT, u, 0:2 * YW].rearrange("p (t e) -> p t e", t=2)[:, :, EMB]
                           ).then_inc(crd_ready, 1)
            dve.wait_ge(crd_ready, i + 1)
            wait_past(dve, out_stored[u], (k - 1) * 32)
            for t in range(2):
                o = dve.scalar_tensor_tensor(out=cout[u][:, t, :], in0=ps[0:TT, u, t * YW:t * YW + EMB],
                                             scalar=crd[u][:, t:t + 1], in1=ch2[u][:, t, :],
                                             op0=ALU.mult, op1=ALU.add)
            o.then_inc(cout_ready, 1)

        with nc.Block() as blk:
            @blk.sync
            def _(sp):
                sp.wait_ge(ones_set, NB)
                for u in range(NB):
                    load_comb(sp, u, u)
                with sp.Fori(0, B // NB - 1) as i:
                    for u in range(NB):
                        sp.wait_ge(cout_ready, NB * i + u + 1)
                        load_comb(sp, NB * i + NB + u, u)

            @blk.scalar
            def _(act):
                with act.Fori(0, B // NB) as i:
                    for u in range(NB):
                        store_out(act, NB * i + u, u)
                for u in range(NB):
                    act.wait_ge(out_stored[u], B // NB * 32)

            @blk.tensor
            def _(pe):
                pe.wait_ge(ones_set, NB)
                for u in range(NB):
                    comb_pe(pe, u, u, 1)
                with pe.Fori(1, B // NB) as i:
                    for u in range(NB):
                        comb_pe(pe, NB * i + u, u, i + 1)

            @blk.vector
            def _(dve):
                for u in range(NB):
                    dve.memset(cys[u][:, :, :], 1.0).then_inc(ones_set, 1)
                for u in range(NB):
                    comb_dve(dve, u, u, 1)
                with dve.Fori(1, B // NB) as i:
                    for u in range(NB):
                        comb_dve(dve, NB * i + u, u, i + 1)


_INS = ['x', 'cls_tok', 'L0_tok_W', 'L0_tok_b', 'L0_tok_cls_token', 'L0_tok_pos_embed', 'L0_attn_W_attn',
        'L0_attn_b_attn', 'L0_attn_W_proj', 'L0_attn_b_proj', 'L0_ffn_phi', 'L0_ffn_ln_g', 'L0_ffn_ln_b',
        'L0_ffn_w1', 'L0_ffn_b1', 'L0_ffn_w2', 'L0_ffn_b2']
_OUTS = [((64, 198, 192), 'float32')]


def kernel(**inputs):
    import numpy as _np
    import concourse.bacc as _bacc
    from concourse import mybir as _mybir
    from concourse.bass_utils import run_bass_kernel_spmd as _run

    nc = _bacc.Bacc("TRN2", target_bir_lowering=False, num_devices=1)
    arrays, args = {}, []
    for name in _INS:
        a = _np.ascontiguousarray(inputs[name])
        arrays[f"in_{name}_dram"] = a
        args.append(nc.dram_tensor(f"in_{name}_dram", a.shape, _mybir.dt.from_np(a.dtype), kind="ExternalInput").ap())
    for i, (shape, dtype) in enumerate(_OUTS):
        dt = _mybir.dt.from_np(_np.dtype(dtype))
        args.append(nc.dram_tensor(f"out_{i}_dram", shape, dt, kind="ExternalOutput").ap())
    vit_tower(nc, *args)
    r = _run(nc, [arrays], core_ids=[0])
    got = tuple(r.results[0][f"out_{i}_dram"] for i in range(len(_OUTS)))
    return got[0]
```
